# Optimizing a Trainium2 kernel written in Bass

```python
import numpy as np
import jax
import jax.numpy as jnp

def _softmax(x, axis=-1):
    return jax.nn.softmax(x, axis=axis)

def _gelu(x):
    return jax.nn.gelu(x, approximate=True)

def _silu(x):
    return jax.nn.silu(x)

def _sigmoid(x):
    return jax.nn.sigmoid(x)

def _layernorm(x, axis=-1, eps=1e-05):
    m = jnp.mean(x, axis=axis, keepdims=True)
    v = jnp.var(x, axis=axis, keepdims=True)
    return (x - m) / jnp.sqrt(v + eps)

def _scatter_add(tgt, idx, src, axis=0):
    return tgt.at[idx].add(src)

def _segment_sum(src, seg, n):
    return jax.ops.segment_sum(src, seg, n)
kernel_name = 'mk_flamingo_gated_d2_seqx_r4_fc03ac'

def setup_inputs(seed: int=0):
    np.random.seed(seed)
    _w = jnp.asarray

    def _rec_inputs():
        import jax
        import jax.numpy as jnp
        _rk = jax.random.key(seed)
        x = 0.0003765 + 1 * jax.random.normal(jax.random.fold_in(_rk, 1), (16, 256, 512), jnp.float32)
        _lenS = 256 - jax.random.randint(jax.random.fold_in(_rk, 7), (16,), 0, max(1, 256 // 4) + 1, jnp.int32)
        _lenS2 = 256 - jax.random.randint(jax.random.fold_in(_rk, 8), (16,), 0, max(1, 256 // 4) + 1, jnp.int32)
        _ctx_2048P = jax.random.normal(jax.random.fold_in(_rk, 11), (16, 16, 512), jnp.float32)
        _ctx_2048c = jax.random.dirichlet(jax.random.fold_in(_rk, 511), 0.3 * jnp.ones((16,), jnp.float32), (16, 256))
        _ctx_2048t = jnp.einsum('bsk,bkd->bsd', _ctx_2048c, _ctx_2048P)
        _ctx_2048t = _ctx_2048t * jax.lax.rsqrt(jnp.mean(jnp.square(_ctx_2048t)) + 1e-12) * 0.953939
        ctx_2048 = -0.000292821 + 1.00034 * (_ctx_2048t + 0.3 * jax.random.normal(jax.random.fold_in(_rk, 611), (16, 256, 512), jnp.float32))
        _g = jax.random.normal(jax.random.fold_in(_rk, 9001), (2, 2), jnp.float32)
        _g = jnp.sign(_g) * jnp.maximum(jnp.abs(_g), 1.0) + (_g == 0) * 1.0
        g_xattn = _g[0]
        g_ffn = _g[1]
        return (x, ctx_2048, g_xattn, g_ffn)
    x, ctx_2048, g_xattn, g_ffn = _rec_inputs()

    def _L0_xattn_setup():
        import jax, jax.numpy as jnp
        import numpy as np
        key = jax.random.key(seed)
        k1, k2, k3, k4, k5 = jax.random.split(key, 5)
        B, D_MODEL, L = (2, 256, 512)
        HEAD_DIM = 8
        H = D_MODEL // HEAD_DIM
        return {'k': jax.random.normal(k1, (B, D_MODEL, L), dtype=jnp.float32), 'v': jax.random.normal(k2, (B, D_MODEL, L), dtype=jnp.float32), 'q': jax.random.normal(k3, (B, D_MODEL, L), dtype=jnp.float32), 'ssm_kernel': jax.random.normal(k4, (H, L), dtype=jnp.float32), 'D': jax.random.normal(k5, (H,), dtype=jnp.float32), 'head_dim': HEAD_DIM}
    _L0_xattn_all = _L0_xattn_setup()
    _L0_xattn_in = {k: v for k, v in _L0_xattn_all.items() if k in ('ssm_kernel', 'D')}
    del _L0_xattn_all

    def _L0_ffn_setup():
        import jax, jax.numpy as jnp
        import numpy as np
        B, T, C = (8, 512, 512)
        E, H = (32, 64)

        def _gating(hidden_states, sim_matrix, gates):
            seq_rep = jnp.mean(hidden_states, axis=1)
            sr_n = seq_rep / jnp.linalg.norm(seq_rep, axis=-1, keepdims=True)
            sm_n = sim_matrix / jnp.linalg.norm(sim_matrix, axis=0, keepdims=True)
            affinity = sr_n @ sm_n
            logits = affinity - jax.nn.sigmoid(gates)
            gated = jax.nn.relu(logits)
            mask = (gated > 0).astype(hidden_states.dtype)
            inactive = jnp.sum(mask, axis=1) == 0
            k_fb = E // 2
            _, fb_idx = jax.lax.top_k(logits, k_fb)
            fb_mask = jnp.sum(jax.nn.one_hot(fb_idx, E, dtype=mask.dtype), axis=1)
            mask = jnp.where(inactive[:, None], jnp.maximum(mask, fb_mask), mask)
            fallback_count = jnp.sum(inactive).astype(jnp.float32)
            neg = -jnp.finfo(hidden_states.dtype).max
            routing = jax.nn.softmax(jnp.where(mask > 0, gated, neg), axis=-1)
            return (routing, mask, fallback_count)
        key = jax.random.key(seed)
        ks = jax.random.split(key, 7)
        scale = 1.0 / np.sqrt(C)
        return {'hidden_states': jax.random.normal(ks[0], (B, T, C), dtype=jnp.float32), 'sim_matrix': jax.random.normal(ks[1], (C, E), dtype=jnp.float32), 'gates': jnp.zeros((E,), dtype=jnp.float32), 'w_q': jax.random.normal(ks[2], (E, H, C), dtype=jnp.float32) * scale, 'w_k': jax.random.normal(ks[3], (E, H, C), dtype=jnp.float32) * scale, 'w_v': jax.random.normal(ks[4], (E, H, C), dtype=jnp.float32) * scale, 'o_weights': jax.random.normal(ks[5], (E, H, C), dtype=jnp.float32)}
    _L0_ffn_all = _L0_ffn_setup()
    _L0_ffn_in = {k: v for k, v in _L0_ffn_all.items() if k in ('sim_matrix', 'gates', 'w_q', 'w_k', 'w_v', 'o_weights')}
    del _L0_ffn_all

    def _L1_xattn_setup():
        import jax, jax.numpy as jnp
        import numpy as np
        N_HEAD = 8
        key = jax.random.key(seed)
        k1, k2, k3 = jax.random.split(key, 3)
        b, d, m = (4, 256, 512)
        c, n = (256, 512)
        q = jax.random.normal(k1, (b, d, m), dtype=jnp.float32)
        k = jax.random.normal(k2, (d // d * b, d, n), dtype=jnp.float32).reshape(b, d, n)
        v = jax.random.normal(k3, (b, c, n), dtype=jnp.float32)
        return {'q': q, 'k': k, 'v': v}
    _L1_xattn_all = _L1_xattn_setup()
    _L1_xattn_in = {k: v for k, v in _L1_xattn_all.items() if k in ()}
    del _L1_xattn_all

    def _L1_ffn_setup():
        import jax, jax.numpy as jnp
        import numpy as np
        NUM_EXPERTS = 8
        TOP_K = 2
        key = jax.random.key(seed)
        k1, k2, k3, k4 = jax.random.split(key, 4)
        B, T, C, E, D = (4, 512, 512, NUM_EXPERTS, 512)
        scale = 0.02
        return {'x': jax.random.normal(k1, (B, T, C), dtype=jnp.float32), 'w_router': jax.random.normal(k2, (C, E), dtype=jnp.float32) * scale, 'w_fc': jax.random.normal(k3, (E, C, D), dtype=jnp.float32) * scale, 'w_proj': jax.random.normal(k4, (E, D, C), dtype=jnp.float32) * scale}
    _L1_ffn_all = _L1_ffn_setup()
    _L1_ffn_in = {k: v for k, v in _L1_ffn_all.items() if k in ('w_router', 'w_fc', 'w_proj')}
    del _L1_ffn_all
    return {'x': x, 'ctx_2048': ctx_2048, 'g_xattn': g_xattn, 'g_ffn': g_ffn, 'L0_xattn_ssm_kernel': _L0_xattn_in['ssm_kernel'], 'L0_xattn_D': _L0_xattn_in['D'], 'L0_ffn_sim_matrix': _L0_ffn_in['sim_matrix'], 'L0_ffn_gates': _L0_ffn_in['gates'], 'L0_ffn_w_q': _L0_ffn_in['w_q'], 'L0_ffn_w_k': _L0_ffn_in['w_k'], 'L0_ffn_w_v': _L0_ffn_in['w_v'], 'L0_ffn_o_weights': _L0_ffn_in['o_weights'], 'L1_ffn_w_router': _L1_ffn_in['w_router'], 'L1_ffn_w_fc': _L1_ffn_in['w_fc'], 'L1_ffn_w_proj': _L1_ffn_in['w_proj']}

def reference(x, ctx_2048, g_xattn, g_ffn, L0_xattn_ssm_kernel, L0_xattn_D, L0_ffn_sim_matrix, L0_ffn_gates, L0_ffn_w_q, L0_ffn_w_k, L0_ffn_w_v, L0_ffn_o_weights, L1_ffn_w_router, L1_ffn_w_fc, L1_ffn_w_proj):
    import jax
    import jax.numpy as jnp

    def _L0_xattn_ref(k, v, q, ssm_kernel, D, head_dim):
        import jax, jax.numpy as jnp
        import numpy as np
        B, HD, L = k.shape
        H = HD // head_dim
        fft_size = 2 * L
        k_ = k.reshape(B, H, head_dim, L)
        v_ = v.reshape(B, H, head_dim, L)
        q_ = q.reshape(B, H, head_dim, L)
        kv = jnp.einsum('bhil,bhjl->bijhl', k_, v_)
        kv_f = jnp.fft.rfft(kv, n=fft_size)
        kernel_f = jnp.fft.rfft(ssm_kernel, n=fft_size)
        y = jnp.fft.irfft(kv_f * kernel_f, n=fft_size)[..., :L]
        out = y + kv * D[None, None, None, :, None]
        out = jnp.einsum('bijhl,bhil->bjhl', out, q_)
        out = jnp.transpose(out, (0, 2, 1, 3)).reshape(B, H * head_dim, L)
        return out.astype(k.dtype)

    def _L0_ffn_ref(hidden_states, sim_matrix, gates, w_q, w_k, w_v, o_weights):
        import jax, jax.numpy as jnp
        import numpy as np
        B, T, C = (8, 512, 512)
        E, H = (32, 64)

        def _gating(hidden_states, sim_matrix, gates):
            seq_rep = jnp.mean(hidden_states, axis=1)
            sr_n = seq_rep / jnp.linalg.norm(seq_rep, axis=-1, keepdims=True)
            sm_n = sim_matrix / jnp.linalg.norm(sim_matrix, axis=0, keepdims=True)
            affinity = sr_n @ sm_n
            logits = affinity - jax.nn.sigmoid(gates)
            gated = jax.nn.relu(logits)
            mask = (gated > 0).astype(hidden_states.dtype)
            inactive = jnp.sum(mask, axis=1) == 0
            k_fb = E // 2
            _, fb_idx = jax.lax.top_k(logits, k_fb)
            fb_mask = jnp.sum(jax.nn.one_hot(fb_idx, E, dtype=mask.dtype), axis=1)
            mask = jnp.where(inactive[:, None], jnp.maximum(mask, fb_mask), mask)
            fallback_count = jnp.sum(inactive).astype(jnp.float32)
            neg = -jnp.finfo(hidden_states.dtype).max
            routing = jax.nn.softmax(jnp.where(mask > 0, gated, neg), axis=-1)
            return (routing, mask, fallback_count)
        routing, mask, fallback_count = _gating(hidden_states, sim_matrix, gates)
        v_all = jnp.einsum('btc,ehc->bteh', hidden_states, w_v)
        full_expert_outputs = v_all * mask[:, None, :, None]
        combined = jnp.einsum('be,bteh->bth', routing, full_expert_outputs)
        w_o_dyn = jnp.einsum('be,ehd->bhd', routing, o_weights)
        final_output = jnp.einsum('bth,bhd->btd', combined, w_o_dyn)
        return final_output

    def _L1_xattn_ref(q, k, v):
        import jax, jax.numpy as jnp
        import numpy as np
        N_HEAD = 8
        b, d, m = q.shape
        c = v.shape[1]
        h = N_HEAD
        qh = q.reshape(b * h, d // h, m)
        kh = k.reshape(b * h, d // h, -1)
        vh = v.reshape(b * h, c // h, -1)
        scale = 1.0 / jnp.sqrt(jnp.asarray(d // h, dtype=q.dtype))
        qk = jnp.einsum('bdm,bdn->bmn', qh, kh) * scale
        sm = jax.nn.softmax(qk, axis=-1)
        ret = jnp.einsum('bmn,bcn->bcm', sm, vh)
        return ret.reshape(b, c, m)

    def _L1_ffn_ref(x, w_router, w_fc, w_proj):
        import jax, jax.numpy as jnp
        import numpy as np
        NUM_EXPERTS = 8
        TOP_K = 2
        B, T, C = x.shape
        E = w_fc.shape[0]
        x_flat = x.reshape(-1, C)
        N = x_flat.shape[0]
        router_logits = x_flat @ w_router
        top_vals, top_idx = jax.lax.top_k(router_logits, TOP_K)
        probs = jax.nn.softmax(top_vals, axis=-1)
        rows = jnp.arange(N)[:, None]
        w_tok = jnp.zeros((N, E), dtype=x.dtype).at[rows, top_idx].add(probs)
        h = jnp.einsum('nc,ecd->ned', x_flat, w_fc)
        h = jnp.square(jax.nn.relu(h))
        y = jnp.einsum('ned,edc->nec', h, w_proj)
        out = jnp.einsum('nec,ne->nc', y, w_tok)
        return out.reshape(B, T, C)
    x = x + jnp.tanh(g_xattn[0]) * _L0_xattn_ref(ctx_2048, ctx_2048, _layernorm(x, axis=-1), L0_xattn_ssm_kernel, L0_xattn_D, 8)
    x = x + jnp.tanh(g_ffn[0]) * _L0_ffn_ref(_layernorm(x, axis=-1), L0_ffn_sim_matrix, L0_ffn_gates, L0_ffn_w_q, L0_ffn_w_k, L0_ffn_w_v, L0_ffn_o_weights)
    x = x + jnp.tanh(g_xattn[1]) * _L1_xattn_ref(_layernorm(x, axis=-1), ctx_2048, ctx_2048)
    x = x + jnp.tanh(g_ffn[1]) * _L1_ffn_ref(_layernorm(x, axis=-1), L1_ffn_w_router, L1_ffn_w_fc, L1_ffn_w_proj)
    return x

_drawn_inputs = setup_inputs


def setup_inputs(seed=0):
    import zlib

    import numpy as np

    out = dict(_drawn_inputs(seed))
    spreads = {'g_ffn': (-1.0, 0.6), 'L0_ffn_gates': (0.0, 0.8)}
    factors = {'L0_ffn_sim_matrix': 7.991,
     'L0_ffn_w_v': 6.287,
     'L0_ffn_o_weights': 6.324,
     'L1_ffn_w_router': 8.0,
     'L1_ffn_w_fc': 8.0,
     'L1_ffn_w_proj': 8.0}
    for name, (base, spread) in spreads.items():
        noise = np.random.default_rng([zlib.crc32(name.encode()), seed]).standard_normal(out[name].shape)
        drawn = base * np.exp(spread * noise) if base else spread * noise
        out[name] = jnp.asarray(drawn.astype(out[name].dtype))
    for name, factor in factors.items():
        out[name] = (out[name] * factor).astype(out[name].dtype)
    return out
```

```python
import numpy as np
from contextlib import ExitStack
import concourse.bass as bass
from concourse import mybir

F32 = mybir.dt.float32
F32R = mybir.dt.float32r
I32 = mybir.dt.int32
U32 = mybir.dt.uint32
ALU = mybir.AluOpType
ACT = mybir.ActivationFunctionType
AX = mybir.AxisListType

P = 128
B, T, C = 16, 256, 512
TH = T // P
CB = C // P
H0, HD0 = 32, 8
HALF, B8 = 2, B // 2
CYC = 12
NDG = 5
PAIRS = NDG * HD0
SLOT = NDG + 2 * (NDG - 2)
E0, EH = 32, 64
HQ, HR = 4, EH // 4
NH, HD1 = 4, 32
SCALE1 = float(HD1) ** -0.5
E1 = 8
UNITS = B * TH
TILES9 = 2 * ((2 * UNITS + E1 - 1 + 1) // 2)
ROW = C + 4
FALLBACK = E0 // 2
EPS = 1e-5
FMAX = float(np.finfo(np.float32).max)


def ap(view, offset, dims):
    return bass.AP(view.tensor, view.offset + offset, [list(view.ap[0])] + [list(d) for d in dims])


class Chain:

    def __init__(self, sem, eng):
        self.sem, self.eng, self.n = sem, eng, 0

    def inc(self, instruction):
        instruction.then_inc(self.sem, 1)
        self.n += 1

    def link(self, instruction):
        self.inc(instruction)
        self.wait()

    def wait(self):
        self.eng.wait_ge(self.sem, self.n)

    def restart(self):
        self.wait()
        self.eng.sem_clear(self.sem)
        self.n = 0


def layer_stats(dve, chain, x, stats, mv):
    n = x.shape[1]
    for i in range(n):
        chain.inc(dve.bn_stats(stats[:, i, :], x[:, i, :]))
    chain.wait()
    for i in range(n):
        chain.inc(dve.bn_aggr(mv[:, i, :], stats[:, i, :]))
    chain.wait()


def layer_scale(dve, chain, var, std, work, rstd, eps=EPS):
    chain.link(dve.reciprocal(rstd, std))
    chain.link(dve.scalar_tensor_tensor(work, var, eps, rstd, ALU.add, ALU.mult))
    chain.link(dve.tensor_tensor(work, work, rstd, ALU.mult))
    chain.link(dve.tensor_scalar(work, work, -0.5, 1.5, ALU.mult, ALU.add))
    chain.link(dve.tensor_tensor(rstd, rstd, work, ALU.mult))


def build(nc, a, out):
    with ExitStack() as whole:
        _build(nc, a, out, whole)


def _build(nc, a, out, whole):
    def sem(name, ctx=whole):
        return ctx.enter_context(nc.semaphore(name))

    def sb(ctx, name, shape, dt=F32):
        return ctx.enter_context(nc.sbuf_tensor(name, shape, dt))[:]

    def pb(ctx, name, shape, dt=F32):
        return ctx.enter_context(nc.psum_tensor(name, shape, dt))[:]

    KP = nc.dram_tensor("kernel_and_skip", [H0, P - 1 + C], F32).ap()
    X1 = nc.dram_tensor("x_after_convolution", [B, T, C], F32).ap()
    X2 = nc.dram_tensor("x_after_experts", [B, T, C], F32).ap()
    WO = nc.dram_tensor("mixed_out_weights", [B, EH, C], F32).ap()
    QH = nc.dram_tensor("q_high", [B, T, C], F32).ap()
    QL = nc.dram_tensor("q_low", [B, T, C], F32).ap()
    XS = nc.dram_tensor("experts_rows", [TILES9 * P, ROW], F32).ap()
    KH = nc.dram_tensor("ctx_high", [B, T, C], F32).ap()
    KL = nc.dram_tensor("ctx_low", [B, T, C], F32).ap()

    ident = sb(whole, "ident", [P, P])
    gates = sb(whole, "gates", [P, 4])
    gates_raw = sb(whole, "gates_raw", [P, 4])
    eps = sb(whole, "eps", [P, 1])
    s_ident = sem("s_ident")
    s_eps = sem("s_eps")
    s_gates = sem("s_gates")
    with ExitStack() as era1:
        QT = sb(era1, "QT", [P, H0 * HALF * CB * B8 * HD0])
        HSTEP, HALFSTEP, BLKSTEP = HALF * CB * B8 * HD0, CB * B8 * HD0, B8 * HD0

        with ExitStack() as st:
            xt = [sb(st, f"xt{i}", [P, TH, C]) for i in range(2)]
            ct = [sb(st, f"ct{i}", [P, TH, C]) for i in range(2)]
            qt = [sb(st, f"qt{i}", [P, TH, C]) for i in range(2)]
            kh = [sb(st, f"kh{i}", [P, TH, C]) for i in range(2)]
            kl = [sb(st, f"kl{i}", [P, TH, C]) for i in range(2)]
            stats = sb(st, "stats", [P, TH, 6])
            mv = sb(st, "mv", [P, TH, 2])
            std = sb(st, "std", [P, TH])
            work = sb(st, "work", [P, TH])
            rstd = sb(st, "rstd", [P, TH])
            kp = sb(st, "kp", [H0, P - 1 + C])
            skip = sb(st, "skip", [H0, 1])
            pq = [pb(st, f"pq{i}", [P, CB, T]) for i in range(2)]
            s_x = [sem(f"s_x{i}", st) for i in range(2)]
            s_c = [sem(f"s_c{i}", st) for i in range(2)]
            s_q = sem("s_q", st)
            s_tr = sem("s_tr", st)
            s_ev = sem("s_ev", st)
            s_kh = sem("s_kh", st)
            s_kl = sem("s_kl", st)
            s_kst = [sem(f"s_kst{i}", st) for i in range(2)]
            s_dve = sem("s_dve", st)
            s_mv = sem("s_mv", st)
            s_std = sem("s_std", st)
            s_kp = sem("s_kp", st)
            s_g = sem("s_g", st)
            s_pool = sem("s_pool", st)
            block = st.enter_context(nc.Block())

            @block.sync
            def _(sp):
                sp.dma_start(kp, a["kern_pad"]).then_inc(s_kp, 16)
                sp.dma_start(skip, a["skip"].rearrange("(h o) -> h o", o=1)).then_inc(s_kp, 16)
                sp.dma_start(gates_raw, a["g"].partition_broadcast(P)).then_inc(s_g, 16)
                with sp.Fori(0, B // 2) as i:
                    for u in range(2):
                        b = 2 * i + u
                        sp.wait_ge(s_q, b + 1)
                        sp.dma_start(xt[u], a["x"][b].rearrange("(th p) c -> p th c", p=P)).then_inc(s_x[u], 16)
                        sp.wait_ge(s_kl, b + 1)
                        sp.dma_start(ct[u], a["ctx"][b].rearrange("(th p) c -> p th c", p=P)).then_inc(s_c[u], 16)
                sp.wait_ge(s_kp, 33)
                sp.dma_start(KP, kp).then_inc(s_kp, 16)
                sp.wait_ge(s_kp, 49)

            @block.vector
            def _(dve):
                chain = Chain(s_dve, dve)
                dve.sem_inc(s_q, 2)
                dve.wait_ge(s_kp, 32)
                dve.tensor_tensor(kp[:, P - 1:P], kp[:, P - 1:P], skip, ALU.add).then_inc(s_kp, 1)
                with dve.Fori(0, B // 2) as i:
                    for u in range(2):
                        b = 2 * i + u
                        dve.wait_ge(s_x[u], i * 16 + 16)
                        layer_stats(dve, chain, xt[u], stats, mv)
                        dve.sem_inc(s_mv, 1)
                        dve.wait_ge(s_std, b + 1)
                        layer_scale(dve, chain, mv[:, :, 1], std, work, rstd)
                        chain.restart()
                        dve.wait_ge(s_tr, b + 1)
                        for th in range(TH):
                            q = dve.tensor_scalar(qt[u][:, th, :], xt[u][:, th, :], mv[:, th, 0:1], rstd[:, th:th + 1],
                                                  ALU.subtract, ALU.mult)
                        q.then_inc(s_q, 1)

            @block.gpsimd
            def _(pool):
                pool.memset(eps, EPS).then_inc(s_eps, 1)
                pool.memset(ident, 0.0).then_inc(s_ident, 1)
                pool.wait_ge(s_ident, 1)
                pool.affine_select(out=ident, in_=ident, compare_op=ALU.not_equal, fill=1.0, base=0,
                                   pattern=[[-1, P]], channel_multiplier=1).then_inc(s_ident, 1)
                pool.sem_inc(s_kl, 2)
                with pool.Fori(0, B // 2) as i:
                    for u in range(2):
                        b = 2 * i + u
                        pool.wait_ge(s_kh, b + 1)
                        pool.wait_ge(s_kst[u], i * 32 + 32)
                        pool.tensor_tensor(kl[u].bitcast(F32R), ct[u], kh[u], ALU.subtract).then_inc(s_kl, 1)

            @block.scalar
            def _(act):
                act.wait_ge(s_eps, 1)
                act.wait_ge(s_g, 16)
                act.activation(gates, gates_raw, ACT.Tanh).then_inc(s_gates, 1)
                act.sem_inc(s_kst[0], 32)
                act.sem_inc(s_kst[1], 32)
                with act.Fori(0, B // 2) as i:
                    for u in range(2):
                        b = 2 * i + u
                        act.wait_ge(s_mv, b + 1)
                        act.activation(std, mv[:, :, 1], ACT.Sqrt, bias=eps).then_inc(s_std, 1)
                        act.wait_ge(s_c[u], i * 16 + 16)
                        act.wait_ge(s_kst[u], i * 32 + 32)
                        act.activation(kh[u].bitcast(F32R), ct[u], ACT.Copy).then_inc(s_kh, 1)
                        act.wait_ge(s_kh, b + 1)
                        act.dma_start(KH[b].rearrange("(th p) c -> p th c", p=P), kh[u]).then_inc(s_kst[u], 16)
                        act.wait_ge(s_tr, b + 3)
                        off = (b // B8) * HALFSTEP + (b % B8) * HD0
                        for k in range(CB // 2):
                            e = act.activation(
                                ap(QT, off + 2 * k * BLKSTEP, [[BLKSTEP, 2], [HSTEP, H0], [1, HD0]]),
                                pq[u][:, 2 * k:2 * k + 2, :].rearrange("p k (h j) -> p k h j", j=HD0), ACT.Copy)
                        e.then_inc(s_ev, 1)
                        act.wait_ge(s_kl, b + 3)
                        act.dma_start(KL[b].rearrange("(th p) c -> p th c", p=P), kl[u]).then_inc(s_kst[u], 16)
                for u in range(2):
                    act.wait_ge(s_kst[u], 32 + 32 * B // 2)

            @block.tensor
            def _(pe):
                pe.wait_ge(s_ident, 2)
                pe.sem_inc(s_tr, 2)
                pe.sem_inc(s_ev, 2)
                with pe.Fori(0, B // 2) as i:
                    for u in range(2):
                        b = 2 * i + u
                        pe.wait_ge(s_q, b + 3)
                        pe.wait_ge(s_ev, b + 1)
                        for th in range(TH):
                            for k in range(CB):
                                t = pe.transpose(pq[u][:, k, th * P:(th + 1) * P], qt[u][:, th, k * P:(k + 1) * P], ident)
                        t.then_inc(s_tr, 1)


        with ExitStack() as st:
            toep = [sb(st, f"toep{i}", [P, C]) for i in range(2)]
            kc = [sb(st, f"kc{i}", [P, HALF * CB * B8, CYC]) for i in range(2)]
            kv = [sb(st, f"kv{i}", [P, HALF, CB, B8 * PAIRS]) for i in range(2)]
            qc = [sb(st, f"qc{i}", [P, HALF * CB * B8, 2 * HD0]) for i in range(2)]
            z = [sb(st, f"z{i}", [P, CB * B8, SLOT * HD0]) for i in range(2)]
            y = [pb(st, f"y{i}", [P, CB * B8, 64]) for i in range(2)]
            s_in = [sem(f"s_in{i}", st) for i in range(2)]
            s_kv = sem("s_kv", st)
            s_qc = sem("s_qc", st)
            s_y = sem("s_y", st)
            s_zb = sem("s_zb", st)
            s_pad = sem("s_pad", st)
            s_fill = sem("s_fill", st)
            pad = sb(st, "pad", [P, ROW])
            padi = sb(st, "padi", [P, 1], I32)
            s_o = sem("s_o", st)
            s_z0 = sem("s_z0", st)
            s_dve = sem("s_dve2", st)
            block = st.enter_context(nc.Block())

            @block.sync
            def _(sp):
                with sp.Fori(0, H0 // 2) as i:
                    for u in range(2):
                        h = 2 * i + u
                        sp.wait_ge(s_kv, h + 1)
                        sp.dma_start(kc[u].rearrange("p n c -> p (n c)"), a["ctx_conv"][h]).then_inc(s_in[u], 16)
                        sp.wait_ge(s_y, 2 * h + 2)
                        sp.dma_start(toep[u], bass.AP(KP.tensor, h * (P - 1 + C), [[1, P], [1, C]])).then_inc(s_in[u], 16)

            @block.gpsimd
            def _(pool):
                for i in range(2):
                    pool.memset(z[i], 0.0).then_inc(s_z0, 1)
                pool.memset(pad, 0.0).then_inc(s_pad, 1)
                pool.iota(padi, [[1, 1]], base=B * T, channel_multiplier=1).then_inc(s_pad, 1)
                pool.sem_inc(s_kv, 2)
                with pool.Fori(0, H0 // 2) as i:
                    for u in range(2):
                        h = 2 * i + u
                        pool.wait_ge(s_in[u], i * 32 + 32)
                        pool.wait_ge(s_y, 2 * h + 2)
                        n = HALF * CB * B8
                        pool.tensor_tensor(kv[u].rearrange("p a b (n d i) -> p (a b n) d i", d=NDG, i=HD0),
                                           ap(kc[u], 0, [[CYC, n], [0, NDG], [1, HD0]]),
                                           ap(kc[u], 0, [[CYC, n], [1, NDG], [1, HD0]]), ALU.mult).then_inc(s_kv, 1)

            @block.scalar
            def _(act):
                act.wait_ge(s_pad, 2)
                act.activation(pad[:, C:C + 1], padi, ACT.Copy).then_inc(s_pad, 1)
                act.wait_ge(s_pad, 3)
                lists = XS.rearrange("(t p) w -> p t w", p=P)
                for n in range(TILES9 - 4 * (H0 // 2)):
                    act.dma_start(lists[:, n, :], pad).then_inc(s_fill, 16)
                with act.Fori(0, H0 // 2) as i:
                    for n in range(4):
                        act.dma_start(XS.rearrange("(t p) w -> t p w", p=P)[TILES9 - 4 * (H0 // 2) + 4 * i + n], pad).then_inc(s_fill, 16)
                    for u in range(2):
                        h = 2 * i + u
                        act.wait_ge(s_zb, 2 * h + 2)
                        n = HALF * CB * B8
                        act.activation(qc[u].rearrange("p n (r j) -> p n r j", r=2),
                                       ap(QT, h * HSTEP, [[HD0, n], [0, 2], [1, HD0]]), ACT.Copy).then_inc(s_qc, 1)
                act.wait_ge(s_fill, 16 * TILES9)

            @block.tensor
            def _(pe):
                pe.sem_inc(s_y, 4)
                pe.sem_inc(s_zb, 4)
                with pe.Fori(0, H0 // 2) as i:
                    for u in range(2):
                        h = 2 * i + u
                        pe.wait_ge(s_in[u], i * 32 + 32)
                        pe.wait_ge(s_kv, h + 3)
                        for half in range(HALF):
                            pe.wait_ge(s_zb, 2 * h + half + 3)
                            for l in range(CB):
                                for s in range(l + 1):
                                    m = pe.matmul(y[half].rearrange("p (l n) c -> p l n c", l=CB)[:, l, :, 0:PAIRS],
                                                  toep[u][:, (l - s) * P:(l - s + 1) * P],
                                                  kv[u][:, half, s, :].rearrange("p (n c) -> p n c", c=PAIRS),
                                                  start=(s == 0), stop=(s == l))
                            m.then_inc(s_y, 1)

            @block.vector
            def _(dve):
                chain = Chain(s_dve, dve)
                n = CB * B8
                W = SLOT * HD0
                dve.wait_ge(s_z0, 2)
                with dve.Fori(0, H0 // 2) as i:
                    for u in range(2):
                        h = 2 * i + u
                        dve.wait_ge(s_qc, h + 1)
                        for half in range(HALF):
                            q0 = half * n * 2 * HD0
                            dve.wait_ge(s_y, 2 * h + half + 5)
                            chain.inc(dve.tensor_tensor(
                                ap(z[half], 0, [[W, n], [HD0, NDG], [1, HD0]]),
                                ap(y[half], 0, [[64, n], [HD0, NDG], [1, HD0]]),
                                ap(qc[u], q0, [[2 * HD0, n], [1, NDG], [1, HD0]]), ALU.mult))
                            dve.tensor_tensor(
                                ap(z[half], NDG * HD0 + 1, [[W, n], [2 * HD0 + 1, NDG - 2], [1, HD0]]),
                                ap(y[half], HD0, [[64, n], [HD0, NDG - 2], [1, HD0]]),
                                ap(qc[u], q0, [[2 * HD0, n], [0, NDG - 2], [1, HD0]]), ALU.mult).then_inc(s_zb, 1)
                            dve.wait_ge(s_zb, 2 * h + half + 5)
                            chain.wait()
                            chain.inc(dve.tensor_reduce(
                                ap(QT, h * HSTEP + half * HALFSTEP, [[HD0, n], [1, HD0]]),
                                ap(z[half], 0, [[W, n], [1, HD0], [HD0, SLOT]]), op=ALU.add, axis=AX.X))
                        chain.restart()

        HT = sb(era1, "HT", [P, B, CB, T])
        SR = sb(era1, "SR", [P, CB, B])
        WV = sb(era1, "WV", [P, HR, C])
        s_wv = sem("s_wv", era1)
        with ExitStack() as st:
            ot = [sb(st, f"ot{i}", [P, CB, T]) for i in range(2)]
            xt = [sb(st, f"xu{i}", [P, TH, C]) for i in range(2)]
            x1 = [sb(st, f"x1_{i}", [P, TH, C]) for i in range(2)]
            hs = [sb(st, f"hs{i}", [P, TH, C]) for i in range(2)]
            stats = sb(st, "stats3", [P, TH, 6])
            mv = sb(st, "mv3", [P, TH, 2])
            std = sb(st, "std3", [P, TH])
            work = sb(st, "work3", [P, TH])
            rstd = sb(st, "rstd3", [P, TH])
            px = [pb(st, f"px{i}", [P, TH, C]) for i in range(2)]
            ph = [pb(st, f"ph{i}", [P, CB, T]) for i in range(2)]
            s_x = [sem(f"s_xx{i}", st) for i in range(2)]
            s_st = [sem(f"s_st{i}", st) for i in range(2)]
            s_ot, s_t1, s_t2, s_x1, s_mv, s_std, s_hs, s_ev, s_dve, s_go = [sem(n + "_3", st) for n in (
                "s_ot", "s_t1", "s_t2", "s_x1", "s_mv", "s_std", "s_hs", "s_ev", "s_dve", "s_go")]
            block = st.enter_context(nc.Block())

            @block.sync
            def _(sp):
                with sp.Fori(0, B // 2) as i:
                    for u in range(2):
                        b = 2 * i + u
                        sp.wait_ge(s_x1, b + 1)
                        sp.dma_start(xt[u], a["x"][b].rearrange("(th p) c -> p th c", p=P)).then_inc(s_x[u], 16)
                for hq in range(HQ):
                    sp.dma_start(WV[hq * E0:(hq + 1) * E0], a["w_v"][:, hq * HR:(hq + 1) * HR, :]).then_inc(s_wv, 16)

            @block.gpsimd
            def _(pool):
                with pool.Fori(0, B // 2) as i:
                    for u in range(2):
                        b = 2 * i + u
                        off = (b // B8) * HALFSTEP + (b % B8) * HD0
                        pool.wait_ge(s_t1, b + 1)
                        pool.sem_inc(s_go, 1)
                        for k in range(CB):
                            pool.tensor_copy(ot[u][:, k, :].rearrange("p (h j) -> p h j", j=HD0),
                                             ap(QT, off + k * BLKSTEP, [[HSTEP, H0], [1, HD0]])).then_inc(s_ot, 1)

            @block.tensor
            def _(pe):
                pe.sem_inc(s_t1, 2)
                pe.sem_inc(s_t2, 2)

                def back(b, u):
                    pe.wait_ge(s_ot, 4 * b + 4)
                    pe.wait_ge(s_x1, b + 1)
                    for th in range(TH):
                        for k in range(CB):
                            t = pe.transpose(px[u][:, th, k * P:(k + 1) * P], ot[u][:, k, th * P:(th + 1) * P], ident)
                    t.then_inc(s_t1, 1)

                def forth(b, u):
                    pe.wait_ge(s_hs, b + 1)
                    pe.wait_ge(s_ev, b + 1)
                    for k in range(CB):
                        for th in range(TH):
                            t = pe.transpose(ph[u][:, k, th * P:(th + 1) * P], hs[u][:, th, k * P:(k + 1) * P], ident)
                    t.then_inc(s_t2, 1)

                back(0, 0)
                with pe.Fori(0, B // 2 - 1) as i:
                    for u in range(2):
                        back(2 * i + u + 1, 1 - u)
                        forth(2 * i + u, u)
                back(B - 1, 1)
                forth(B - 2, 0)
                forth(B - 1, 1)

            @block.vector
            def _(dve):
                chain = Chain(s_dve, dve)
                dve.sem_inc(s_x1, 2)
                with dve.Fori(0, B // 2) as i:
                    for u in range(2):
                        b = 2 * i + u
                        dve.wait_ge(s_x[u], i * 16 + 16)
                        dve.wait_ge(s_t1, b + 3)
                        dve.wait_ge(s_st[u], i * 16 + 16)
                        for th in range(TH):
                            chain.inc(dve.scalar_tensor_tensor(x1[u][:, th, :], px[u][:, th, :], gates[:, 0:1],
                                                               xt[u][:, th, :], ALU.mult, ALU.add))
                        chain.wait()
                        dve.sem_inc(s_x1, 1)
                        layer_stats(dve, chain, x1[u], stats, mv)
                        dve.sem_inc(s_mv, 1)
                        dve.wait_ge(s_std, b + 1)
                        layer_scale(dve, chain, mv[:, :, 1], std, work, rstd)
                        chain.restart()
                        dve.wait_ge(s_t2, b + 1)
                        for th in range(TH):
                            q = dve.tensor_scalar(hs[u][:, th, :], x1[u][:, th, :], mv[:, th, 0:1], rstd[:, th:th + 1],
                                                  ALU.subtract, ALU.mult)
                        q.then_inc(s_hs, 1)

            @block.scalar
            def _(act):
                act.sem_inc(s_ev, 2)
                act.sem_inc(s_st[0], 16)
                act.sem_inc(s_st[1], 16)
                with act.Fori(0, B // 2) as i:
                    for u in range(2):
                        b = 2 * i + u
                        act.wait_ge(s_x1, b + 3)
                        act.dma_start(X1[b].rearrange("(th p) c -> p th c", p=P), x1[u]).then_inc(s_st[u], 16)
                        act.wait_ge(s_mv, b + 1)
                        act.activation(std, mv[:, :, 1], ACT.Sqrt, bias=eps).then_inc(s_std, 1)
                        act.wait_ge(s_t2, b + 3)
                        for k in range(CB):
                            e = act.activation(ap(HT, b * (CB * T) + k * T, [[1, T]]), ph[u][:, k, :], ACT.Copy,
                                               accum_out=ap(SR, b + k * B, [[1, 1]]))
                        e.then_inc(s_ev, 1)
                for u in range(2):
                    act.wait_ge(s_st[u], 16 + 16 * B // 2)

        WM = sb(era1, "WM", [P, B, CB, EH])
        with ExitStack() as st:
            WOT = QT[:, 0:HR * C].rearrange("p (r c) -> p r c", c=C)
            WOS = QT[0:HQ * B, HR * C:2 * HR * C].rearrange("p (r c) -> p r c", c=C)
            sim = sb(st, "sim", [P, CB, E0])
            sim2 = sb(st, "sim2", [P, CB, E0])
            sr2 = sb(st, "sr2", [P, CB, B])
            ones = sb(st, "ones4", [P, B])
            later = sb(st, "later", [B, E0, E0])
            over = sb(st, "over", [B, E0, E0])
            same = sb(st, "same", [B, E0, E0])
            eg = sb(st, "eg", [B, E0])
            t = {n: sb(st, n + "_4", [B, E0]) for n in ("sig", "logits", "gated", "mask", "rank", "z", "e", "rm")}
            nn = sb(st, "nn", [B, E0 + 1])
            rn = sb(st, "rn", [B, E0 + 1])
            sq = sb(st, "sq", [B, E0 + 1])
            wk = sb(st, "wk", [B, E0 + 1])
            cnt = sb(st, "cnt", [B, 1])
            zmax = sb(st, "zmax", [B, 1])
            zsum = sb(st, "zsum", [B, 1])
            RB = sb(st, "RB", [P, HQ * B])
            p_aff = pb(st, "p_aff", [B, C])
            p_n = pb(st, "p_n", [B, C])
            p_e = pb(st, "p_e", [B, C])
            p_rm = pb(st, "p_rm", [P, C])
            p_w = [pb(st, f"p_w{i}", [P, 8, 64]) for i in range(4)]
            (s_in4, s_con, s_pe, s_act, s_dve, s_sr, s_rm, s_rb, s_wp, s_wd, s_wa, s_wp2, s_wst) = [
                sem(n + "_4", st) for n in ("s_in", "s_con", "s_pe", "s_act", "s_dve", "s_sr", "s_rm", "s_rb",
                                            "s_wp", "s_wd", "s_wa", "s_wp2", "s_wst")]
            s_wo = [sem(f"s_wo4{i}", st) for i in range(2)]
            block = st.enter_context(nc.Block())

            @block.sync
            def _(sp):
                sp.dma_start(sim, a["sim"].rearrange("(k p) e -> p k e", p=P)).then_inc(s_in4, 16)
                sp.dma_start(eg, a["eg"].partition_broadcast(B)).then_inc(s_in4, 16)
                for n in range(2):
                    for hq in range(HQ):
                        sp.dma_start(WOT[hq * E0:(hq + 1) * E0, 8 * n:8 * n + 8, :],
                                     a["w_o"][:, hq * HR + 8 * n:hq * HR + 8 * n + 8, :]).then_inc(s_wo[n], 16)
                sp.wait_ge(s_wa, HR)
                for hq in range(HQ):
                    sp.dma_start(WO[:, hq * HR:(hq + 1) * HR, :], WOS[hq * B:(hq + 1) * B]).then_inc(s_wst, 16)
                sp.wait_ge(s_wst, 16 * HQ)

            @block.gpsimd
            def _(pool):
                pool.memset(ones, 1.0).then_inc(s_con, 1)
                pool.memset(RB, 0.0).then_inc(s_con, 1)
                pool.memset(later, 1.0).then_inc(s_con, 1)
                pool.wait_ge(s_con, 3)
                pool.affine_select(out=later, in_=later, compare_op=ALU.is_gt, fill=0.0, base=0,
                                   pattern=[[1, E0], [-1, E0]], channel_multiplier=0).then_inc(s_con, 1)

            @block.vector
            def _(dve):
                chain = Chain(s_dve, dve)
                dve.wait_ge(s_in4, 32)
                chain.inc(dve.tensor_scalar(SR, SR, 1.0 / T, None, ALU.mult))
                chain.link(dve.tensor_tensor(sim2, sim, sim, ALU.mult))
                dve.tensor_tensor(sr2, SR, SR, ALU.mult).then_inc(s_sr, 1)
                dve.wait_ge(s_pe, 1)
                chain.inc(dve.tensor_copy(nn[:, 0:E0], p_e[:, 0:E0]))
                chain.link(dve.tensor_copy(nn[:, E0:], p_n[:, 0:1]))
                dve.sem_inc(s_sr, 1)
                dve.wait_ge(s_act, 2)
                layer_scale(dve, chain, nn, sq, wk, rn, 0.0)
                chain.link(dve.tensor_scalar(t["sig"], t["e"], 1.0, None, ALU.add))
                chain.link(dve.reciprocal(t["sig"], t["sig"]))
                chain.link(dve.scalar_tensor_tensor(t["logits"], p_aff[:, 0:E0], rn[:, E0:], rn[:, 0:E0], ALU.mult, ALU.mult))
                chain.link(dve.tensor_tensor(t["logits"], t["logits"], t["sig"], ALU.subtract))
                chain.inc(dve.tensor_scalar(t["gated"], t["logits"], 0.0, None, ALU.max))
                chain.link(dve.tensor_scalar(t["mask"], t["logits"], 0.0, None, ALU.is_gt))
                chain.link(dve.tensor_reduce(cnt, t["mask"], op=ALU.add, axis=AX.X))
                chain.link(dve.tensor_scalar(cnt, cnt, 0.0, None, ALU.is_equal))
                dve.wait_ge(s_con, 4)
                mine = ap(t["logits"], 0, [[1, E0], [0, E0]])
                other = ap(t["logits"], 0, [[0, E0], [1, E0]])
                chain.inc(dve.tensor_tensor(over, other, mine, ALU.is_gt))
                chain.link(dve.tensor_tensor(same, other, mine, ALU.is_equal))
                chain.link(dve.tensor_tensor(same, same, later, ALU.mult))
                chain.link(dve.tensor_tensor(over, over, same, ALU.add))
                chain.link(dve.tensor_reduce(t["rank"], over, op=ALU.add, axis=AX.X))
                chain.link(dve.tensor_scalar(t["rank"], t["rank"], float(FALLBACK), cnt, ALU.is_lt, ALU.mult))
                chain.link(dve.tensor_tensor(t["mask"], t["mask"], t["rank"], ALU.max))
                chain.inc(dve.tensor_tensor(t["gated"], t["gated"], t["mask"], ALU.mult))
                chain.link(dve.tensor_scalar(t["z"], t["mask"], FMAX, -FMAX, ALU.mult, ALU.add))
                chain.link(dve.tensor_tensor(t["z"], t["z"], t["gated"], ALU.add))
                chain.link(dve.tensor_reduce(zmax, t["z"], op=ALU.max, axis=AX.X, negate=True))
                dve.sem_inc(s_sr, 1)
                dve.wait_ge(s_act, 3)
                chain.link(dve.reciprocal(zsum, zsum))
                dve.scalar_tensor_tensor(t["rm"], t["e"], zsum, t["mask"], ALU.mult, ALU.mult).then_inc(s_rm, 1)
                dve.wait_ge(s_pe, 2)
                for g in range(HQ):
                    c = dve.tensor_copy(RB[g * E0:(g + 1) * E0, g * B:(g + 1) * B], p_rm[g * E0:(g + 1) * E0, 0:B])
                    chain.inc(c)
                chain.wait()
                dve.sem_inc(s_rb, 1)
                for r in range(HR):
                    dve.wait_ge(s_wp, r // 2 + 1)
                    dve.tensor_copy(ap(WM, r, [[EH, CB], [HR, HQ], [CB * EH, B]]),
                                    p_w[r // 2 % 2][:, 4 * (r % 2):4 * (r % 2) + 4, :].rearrange("p k (q b) -> p k q b", q=HQ)
                                    ).then_inc(s_wd, 1)

            @block.scalar
            def _(act):
                act.wait_ge(s_in4, 32)
                act.activation(t["e"], eg, ACT.Exp, scale=-1.0).then_inc(s_act, 1)
                act.wait_ge(s_sr, 2)
                act.activation(sq, nn, ACT.Sqrt).then_inc(s_act, 1)
                act.wait_ge(s_sr, 3)
                act.activation(t["e"], t["z"], ACT.Exp, bias=zmax, accum_out=zsum).then_inc(s_act, 1)
                for r in range(HR):
                    act.wait_ge(s_wp2, r + 1)
                    act.activation(WOS[:, r, :], p_w[2 + r % 2][0:HQ * B].rearrange("p a b -> p (a b)"), ACT.Copy).then_inc(s_wa, 1)

            @block.tensor
            def _(pe):
                pe.wait_ge(s_sr, 1)
                pe.wait_ge(s_con, 2)
                pe.wait_ge(s_in4, 32)
                for k in range(CB):
                    pe.matmul(p_aff[:, 0:E0], SR[:, k, :], sim[:, k, :], start=(k == 0), stop=(k == CB - 1))
                for k in range(CB):
                    pe.matmul(p_n[:, 0:1], sr2[:, k, :], ones[:, 0:1], start=(k == 0), stop=(k == CB - 1))
                for k in range(CB):
                    m = pe.matmul(p_e[:, 0:E0], ones, sim2[:, k, :], start=(k == 0), stop=(k == CB - 1))
                m.then_inc(s_pe, 1)
                pe.wait_ge(s_rm, 1)
                for g in range(HQ):
                    m = pe.matmul(p_rm[g * E0:(g + 1) * E0, 0:B], t["rm"], ident[0:B, 0:B], start=True, stop=True)
                m.then_inc(s_pe, 1)
                pe.wait_ge(s_rb, 1)
                pe.wait_ge(s_wv, 16 * HQ)
                for r in range(HR):
                    if r >= 4 and r % 2 == 0:
                        pe.wait_ge(s_wd, r - 2)
                    for k in range(CB):
                        m = pe.matmul(p_w[r // 2 % 2][:, 4 * (r % 2) + k, :], WV[:, r, k * P:(k + 1) * P], RB, start=True, stop=True)
                    if r % 2:
                        m.then_inc(s_wp, 1)
                for r in range(HR):
                    pe.wait_ge(s_wo[r // 8], 16 * HQ)
                    if r >= 2:
                        pe.wait_ge(s_wa, r - 1)
                    pe.matmul(p_w[2 + r % 2][0:HQ * B].rearrange("p a b -> p (a b)"), RB, WOT[:, r, :],
                              start=True, stop=True).then_inc(s_wp2, 1)

        with ExitStack() as st:
            hc = [sb(st, f"hc{i}", [P, CB, T]) for i in range(2)]
            wc = [sb(st, f"wc{i}", [P, CB, EH]) for i in range(2)]
            wo = [sb(st, f"wo{i}", [EH, C]) for i in range(2)]
            cb = [sb(st, f"cb{i}", [EH, T]) for i in range(2)]
            xt = [sb(st, f"xv{i}", [P, TH, C]) for i in range(2)]
            big = QT.rearrange("p (n th c) -> p n th c", th=TH, c=C)
            x2, q, qh, ql = ([big[:, 2 * n + i] for i in range(2)] for n in range(4))
            stats = sb(st, "stats5", [P, TH, 6])
            mv = sb(st, "mv5", [P, TH, 2])
            std = sb(st, "std5", [P, TH])
            work = sb(st, "work5", [P, TH])
            rstd = sb(st, "rstd5", [P, TH])
            pc = [pb(st, f"pc{i}", [EH, C]) for i in range(2)]
            py = [pb(st, f"py{i}", [P, TH, C]) for i in range(2)]
            s_x = [sem(f"s_x5{i}", st) for i in range(2)]
            s_st = [sem(f"s_st5{i}", st) for i in range(2)]
            s_hc, s_pc, s_cb, s_py, s_x2, s_mv, s_std, s_q, s_qh, s_dve, s_ql, s_go = [sem(n + "_5", st) for n in (
                "s_hc", "s_pc", "s_cb", "s_py", "s_x2", "s_mv", "s_std", "s_q", "s_qh", "s_dve", "s_ql", "s_go")]
            block = st.enter_context(nc.Block())

            def rows(d):
                return d.rearrange("(th p) c -> p th c", p=P)

            @block.sync
            def _(sp):
                with sp.Fori(0, B // 2) as i:
                    for u in range(2):
                        b = 2 * i + u
                        sp.wait_ge(s_x2, b + 1)
                        sp.dma_start(xt[u], rows(X1[b])).then_inc(s_x[u], 16)
                        sp.dma_start(wo[u], WO[b]).then_inc(s_x[u], 16)

            @block.gpsimd
            def _(pool):
                with pool.Fori(0, B // 2) as i:
                    for u in range(2):
                        b = 2 * i + u
                        pool.wait_ge(s_pc, b + 1)
                        pool.sem_inc(s_go, 1)
                        pool.tensor_copy(hc[u].rearrange("p k t -> p (k t)"), ap(HT, b * (CB * T), [[1, CB * T]])).then_inc(s_hc, 1)
                        pool.tensor_copy(wc[u].rearrange("p k h -> p (k h)"), ap(WM, b * (CB * EH), [[1, CB * EH]])).then_inc(s_hc, 1)

            @block.tensor
            def _(pe):
                pe.sem_inc(s_pc, 2)

                def inner(b, u):
                    pe.wait_ge(s_hc, 2 * b + 2)
                    pe.wait_ge(s_cb, b + 1)
                    for k in range(CB):
                        m = pe.matmul(pc[u][:, 0:T], wc[u][:, k, :], hc[u][:, k, :], start=(k == 0), stop=(k == CB - 1))
                    m.then_inc(s_pc, 1)

                def outer(b, u, wo_here):
                    pe.wait_ge(s_cb, b + 3)
                    pe.wait_ge(s_x[u], wo_here)
                    pe.wait_ge(s_x2, b + 1)
                    for th in range(TH):
                        m = pe.matmul(py[u][:, th, :], cb[u][:, th * P:(th + 1) * P], wo[u], start=True, stop=True)
                    m.then_inc(s_py, 1)

                inner(0, 0)
                with pe.Fori(0, B // 2 - 1) as i:
                    for u in range(2):
                        inner(2 * i + u + 1, 1 - u)
                        outer(2 * i + u, u, i * 32 + 32)
                inner(B - 1, 1)
                outer(B - 2, 0, 16 * B)
                outer(B - 1, 1, 16 * B)

            @block.vector
            def _(dve):
                chain = Chain(s_dve, dve)
                dve.sem_inc(s_x2, 2)
                with dve.Fori(0, B // 2) as i:
                    for u in range(2):
                        b = 2 * i + u
                        dve.wait_ge(s_x[u], i * 32 + 32)
                        dve.wait_ge(s_py, b + 1)
                        dve.wait_ge(s_st[u], i * 48 + 48)
                        for th in range(TH):
                            chain.inc(dve.scalar_tensor_tensor(x2[u][:, th, :], py[u][:, th, :], gates[:, 2:3],
                                                               xt[u][:, th, :], ALU.mult, ALU.add))
                        chain.wait()
                        dve.sem_inc(s_x2, 1)
                        layer_stats(dve, chain, x2[u], stats, mv)
                        dve.sem_inc(s_mv, 1)
                        dve.wait_ge(s_std, b + 1)
                        layer_scale(dve, chain, mv[:, :, 1], std, work, rstd)
                        chain.restart()
                        for th in range(TH):
                            n = dve.tensor_scalar(q[u][:, th, :], x2[u][:, th, :], mv[:, th, 0:1], rstd[:, th:th + 1],
                                                  ALU.subtract, ALU.mult)
                        n.then_inc(s_q, 1)
                        dve.wait_ge(s_qh, b + 1)
                        dve.tensor_tensor(ql[u].bitcast(F32R), q[u], qh[u], ALU.subtract).then_inc(s_ql, 1)

            @block.scalar
            def _(act):
                act.sem_inc(s_cb, 2)
                act.sem_inc(s_st[0], 48)
                act.sem_inc(s_st[1], 48)
                with act.Fori(0, B // 2) as i:
                    for u in range(2):
                        b = 2 * i + u
                        act.wait_ge(s_pc, b + 3)
                        act.activation(cb[u], pc[u][:, 0:T], ACT.Copy).then_inc(s_cb, 1)
                        act.wait_ge(s_mv, b + 1)
                        act.activation(std, mv[:, :, 1], ACT.Sqrt, bias=eps).then_inc(s_std, 1)
                        act.wait_ge(s_q, b + 1)
                        act.activation(qh[u].bitcast(F32R), q[u], ACT.Copy).then_inc(s_qh, 1)
                        act.dma_start(rows(X2[b]), x2[u]).then_inc(s_st[u], 16)
                        act.wait_ge(s_ql, b + 1)
                        act.dma_start(rows(QH[b]), qh[u]).then_inc(s_st[u], 16)
                        act.dma_start(rows(QL[b]), ql[u]).then_inc(s_st[u], 16)
                for u in range(2):
                    act.wait_ge(s_st[u], 48 + 48 * B // 2)

    X3 = out["out"][0:B * T].rearrange("(u p) c -> u p c", p=P)
    with ExitStack() as st:
        qs = [sb(st, f"qs{i}", [P, NH, C]) for i in range(4)]
        ks = [sb(st, f"ks{i}", [P, NH, C]) for i in range(4)]
        vt = [sb(st, f"vt{i}", [P, CB, P]) for i in range(4)]
        xt = [sb(st, f"xw{i}", [P, C]) for i in range(4)]
        pt = [sb(st, f"pt{i}", [P, NH, C]) for i in range(2)]
        x3 = [sb(st, f"x3_{i}", [P, C]) for i in range(2)]
        lns = sb(st, "lns", [P, C])
        inv = sb(st, "inv", [P, C])
        att = sb(st, "att", [P, C])
        corr = sb(st, "corr", [P, C])
        minus_gate = sb(st, "minus_gate", [P, 1])
        mx = sb(st, "mx", [P, CB, NH])
        mh = sb(st, "mh", [NH, C])
        ml = sb(st, "ml", [NH, C])
        ones = sb(st, "ones6", [P, HD1])
        pA = [pb(st, f"pA{i}", [P, 2, C]) for i in range(2)]
        pB = [pb(st, f"pB{i}", [P, C]) for i in range(2)]
        pV = pb(st, "pV", [P, C])
        pS = pb(st, "pS", [P, C])
        s_ld = [sem(f"s_ld{i}", st) for i in range(4)]
        s_v = [sem(f"s_v{i}", st) for i in range(4)]
        s_st = [sem(f"s_st6{i}", st) for i in range(2)]
        (s_rep, s_a, s_red, s_mt, s_mh, s_ml, s_md, s_b, s_exp, s_av, s_inv, s_x3, s_c, s_dve, s_act, s_dn, s_pool, s_go) = [
            sem(n + "_6", st) for n in ("s_rep", "s_a", "s_red", "s_mt", "s_mh", "s_ml", "s_md", "s_b", "s_exp",
                                        "s_av", "s_inv", "s_x3", "s_c", "s_dve", "s_act", "s_dn", "s_pool", "s_go")]
        block = st.enter_context(nc.Block())
        TRIP = 4
        NS = 3 * HD1
        TILES = NH * CB // 2
        RING = TILES + 1
        units = lambda d: d.rearrange("b (g h d) c -> (b g) d h c", g=TH, h=NH)
        KHu, KLu, QHu, QLu = units(KH), units(KL), units(QH), units(QL)
        X2u = X2.rearrange("b (g p) c -> (b g) p c", g=TH)

        def unit_loop(eng, body):
            trips = UNITS // TRIP
            for u in range(TRIP):
                body(u, 0, u)
            with eng.Fori(1, trips - 1) as i:
                for u in range(TRIP):
                    body(i * TRIP + u, i, u)
            for u in range(TRIP):
                body(UNITS - TRIP + u, trips - 1, u)

        def is_last(j):
            return isinstance(j, int) and j == UNITS - 1

        @block.sync
        def _(sp):
            def load(j, u):
                for dst, src in ((ks[u][0:HD1], KHu[j]), (ks[u][HD1:2 * HD1], KLu[j]),
                                 (qs[u][0:HD1], QHu[j]), (qs[u][HD1:2 * HD1], QHu[j]), (qs[u][2 * HD1:NS], QLu[j])):
                    sp.dma_start(dst, src).then_inc(s_ld[u], 16)
                sp.dma_start(vt[u], a["v_t"][j]).then_inc(s_v[u], 16)
                sp.dma_start(xt[u], X2u[j]).then_inc(s_v[u], 16)

            def store(j, u):
                sp.wait_ge(s_x3, j + 1)
                sp.dma_start(X3[j], x3[u % 2]).then_inc(s_st[u % 2], 16)

            def shift(j, u):
                sp.wait_ge(s_mh, j + 1)
                for row, part in enumerate((mh, ml)):
                    sp.dma_start(qs[u][NS + row:NS + row + 1], bass.AP(part.tensor, part.offset, [list(part.ap[0]), [C, 1], [1, C]])).then_inc(s_md, 16)

            def body(j, i, u):
                if not (isinstance(j, int) and j == 0):
                    sp.wait_ge(s_b, 16 * j)
                    store(j - 1, (u + TRIP - 1) % TRIP)
                if not isinstance(j, int) or j + 3 < UNITS:
                    load(j + 3, (u + 3) % TRIP)
                if not is_last(j):
                    shift(j + 1, (u + 1) % TRIP)

            for u in range(3):
                load(u, u)
            shift(0, 0)
            unit_loop(sp, body)
            store(UNITS - 1, TRIP - 1)
            for u in range(2):
                sp.wait_ge(s_st[u], 16 * UNITS // 2)

        @block.gpsimd
        def _(pool):
            chain = Chain(s_pool, pool)
            chain.link(pool.memset(ones, 1.0))
            for u in range(4):
                chain.link(pool.memset(ks[u][NS:P], 1.0))
            chain.restart()
            pool.sem_inc(s_c, 1)
            with pool.Fori(0, UNITS // TRIP) as i:
                for u in range(TRIP):
                    pool.wait_ge(s_ld[u], i * 80 + 80)
                    pool.sem_inc(s_go, 1)
                    chain.link(pool.tensor_copy(ks[u][2 * HD1:NS].bitcast(F32R), ks[u][0:HD1]))
                    chain.restart()
                    pool.sem_inc(s_rep, 1)

        @block.tensor
        def _(pe):
            pe.sem_inc(s_red, 2)
            pe.sem_inc(s_exp, 2)
            pe.sem_inc(s_dn, 1)
            pe.wait_ge(s_c, 1)

            def first(j, u, lo, hi):
                if lo == 0:
                    pe.wait_ge(s_rep, j + 1)
                for t in range(lo, hi):
                    slot = (u * RING + t) % 2
                    pe.wait_ge(s_red, RING * j + t + 1)
                    h, half = t // 2, t % 2
                    for w in range(2):
                        m0 = (2 * half + w) * P
                        m = pe.matmul(pA[slot][:, w, :], qs[u][0:NS, h, m0:m0 + P].bitcast(F32R), ks[u][0:NS, h, :].bitcast(F32R),
                                      start=True, stop=True)
                    m.then_inc(s_a, 1)

            def maxima(j, u):
                slot = (u * RING + TILES) % 2
                pe.wait_ge(s_red, RING * j + TILES + 2)
                for k in range(CB):
                    t = pe.transpose(pA[slot][0:NH, 0, k * P:(k + 1) * P], mx[:, k, :], ident)
                t.then_inc(s_mt, 1)

            def second(j, u, s):
                if s == 0:
                    pe.wait_ge(s_md, 32 * j + 32)
                for h in range(NH):
                    pe.wait_ge(s_exp, 16 * j + NH * s + h + 1)
                    pe.matmul(pB[h % 2], ks[u][0:NS + 2, h, s * P:(s + 1) * P].bitcast(F32R), qs[u][0:NS + 2, h, :].bitcast(F32R),
                              start=True, stop=True).then_inc(s_b, 1)

            def values(j, i, u, s):
                if s == 0:
                    pe.wait_ge(s_v[u], i * 32 + 32)
                    pe.wait_ge(s_dn, j + 1)
                pe.wait_ge(s_exp, 16 * j + NH * s + NH + 2)
                for h in range(NH):
                    pe.matmul(pV[h * HD1:(h + 1) * HD1, :], vt[u][:, s, h * HD1:(h + 1) * HD1], pt[s % 2][:, h, :],
                              start=(s == 0), stop=(s == CB - 1))
                for h in range(NH):
                    m = pe.matmul(pS[h * HD1:(h + 1) * HD1, :], ones, pt[s % 2][:, h, :], start=(s == 0), stop=(s == CB - 1))
                m.then_inc(s_av, 1)

            def body(j, i, u):
                n = (u + 1) % TRIP
                more = not is_last(j)
                second(j, u, 0)
                if more:
                    first(j + 1, n, 0, TILES // 2)
                second(j, u, 1)
                values(j, i, u, 0)
                if more:
                    first(j + 1, n, TILES // 2, TILES)
                second(j, u, 2)
                values(j, i, u, 1)
                if more:
                    maxima(j + 1, n)
                second(j, u, 3)
                values(j, i, u, 2)
                values(j, i, u, 3)

            first(0, 0, 0, TILES)
            maxima(0, 0)
            unit_loop(pe, body)

        @block.scalar
        def _(act):
            act.sem_inc(s_av, 2)
            act.preload_act_table_set("natural_log_exp_and_others")

            def body(j, i, u):
                for s in range(CB):
                    act.wait_ge(s_av, 4 * j + s + 1)
                    for h in range(NH):
                        act.wait_ge(s_b, 16 * j + NH * s + h + 1)
                        act.activation(pt[s % 2][:, h, :], pB[h % 2], ACT.Exp, scale=SCALE1).then_inc(s_exp, 1)
                act.wait_ge(s_av, 4 * j + 6)
                act.activation(lns, pS, ACT.Ln).then_inc(s_act, 1)
                act.wait_ge(s_act, 2 * j + 1)
                act.wait_ge(s_dn, j + 1)
                act.activation(inv, lns, ACT.Exp, scale=-1.0).then_inc(s_act, 1)

            unit_loop(act, body)

        @block.vector
        def _(dve):
            chain = Chain(s_dve, dve)

            def reduce(j, u):
                for t in range(TILES):
                    slot = (u * RING + t) % 2
                    h, half = t // 2, t % 2
                    dve.wait_ge(s_a, TILES * j + t + 1)
                    dve.tensor_reduce(ap(mx, 2 * half * NH + h, [[NH, 2]]), pA[slot], op=ALU.max, axis=AX.X).then_inc(s_red, 1)
                slot = (u * RING + TILES) % 2
                dve.wait_ge(s_mt, j + 1)
                if not (isinstance(j, int) and j == 0):
                    dve.wait_ge(s_md, 32 * j)
                rows = pA[slot][0:NH, 0, :]
                chain.link(dve.tensor_scalar(mh.bitcast(F32R), rows, -1.0, None, ALU.mult))
                chain.link(dve.scalar_tensor_tensor(ml.bitcast(F32R), rows, -1.0, mh, ALU.mult, ALU.subtract))
                chain.restart()
                dve.sem_inc(s_red, 1)
                dve.sem_inc(s_mh, 1)

            def body(j, i, u):
                if not is_last(j):
                    reduce(j + 1, (u + 1) % TRIP)
                dve.wait_ge(s_act, 2 * j + 2)
                chain.inc(dve.tensor_tensor(att, pV, inv, ALU.mult))
                chain.link(dve.tensor_tensor(corr, pS, inv, ALU.mult))
                dve.sem_inc(s_dn, 1)
                chain.link(dve.scalar_tensor_tensor(att, corr, 2.0, att, ALU.subtract, ALU.mult))
                dve.wait_ge(s_v[u], i * 32 + 32)
                if not isinstance(j, int) or j > 1:
                    dve.wait_ge(s_st[u % 2], 32 * i + 16 * (u // 2))
                chain.link(dve.scalar_tensor_tensor(x3[u % 2], att, minus_gate, xt[u], ALU.mult, ALU.add))
                chain.restart()
                dve.sem_inc(s_x3, 1)

            chain.link(dve.tensor_scalar(minus_gate, gates[:, 1:2], -1.0, None, ALU.mult))
            reduce(0, 0)
            unit_loop(dve, body)

    with ExitStack() as era3:
        WF = sb(era3, "WF", [P, E1, CB, C])
        TE = sb(era3, "TE", [P, TILES9])
        TEi = sb(era3, "TEi", [1, TILES9], I32)
        s_wf = sem("s_wf", era3)
        with ExitStack() as era4:
            XN = sb(era4, "XN", [P, UNITS, ROW])
            LG = sb(era4, "LG", [P, UNITS, E1])
            with ExitStack() as st:
                xt = [sb(st, f"xr{i}", [P, C]) for i in range(2)]
                xT = [sb(st, f"xT{i}", [P, CB, P]) for i in range(2)]
                wr = sb(st, "wr", [P, CB, E1])
                xs = [sb(st, f"xn{i}", [P, C]) for i in range(2)]
                stats = sb(st, "stats7", [P, 1, 6])
                mv = sb(st, "mv7", [P, 1, 2])
                std = sb(st, "std7", [P, 1])
                work = sb(st, "work7", [P, 1])
                rstd = sb(st, "rstd7", [P, 1])
                zero = sb(st, "zero7", [P, C])
                pT = [pb(st, f"pT{i}", [P, CB, P]) for i in range(2)]
                pL = [pb(st, f"pL{i}", [P, C]) for i in range(2)]
                s_x = [sem(f"s_x7{i}", st) for i in range(2)]
                s_wr, s_mv, s_std, s_xn, s_t, s_ev, s_l, s_lg, s_dve, s_z = [sem(n + "_7", st) for n in (
                    "s_wr", "s_mv", "s_std", "s_xn", "s_t", "s_ev", "s_l", "s_lg", "s_dve", "s_z")]
                block = st.enter_context(nc.Block())

                @block.sync
                def _(sp):
                    sp.dma_start(wr, a["w_router"].rearrange("(k p) e -> p k e", p=P)).then_inc(s_wr, 16)
                    with sp.Fori(0, UNITS // 2) as i:
                        for u in range(2):
                            j = 2 * i + u
                            sp.wait_ge(s_xn, j + 1)
                            sp.dma_start(xt[u], X3[j]).then_inc(s_x[u], 16)
                    for e in range(E1):
                        sp.dma_start(WF[:, e], a["w_fc"][e].rearrange("(k p) d -> p k d", p=P)).then_inc(s_wf, 16)
                    sp.wait_ge(s_z, 1)
                    sp.dma_start(out["out"][B * T:], zero).then_inc(s_wr, 16)
                    sp.wait_ge(s_wr, 32)

                @block.gpsimd
                def _(pool):
                    pool.memset(zero, 0.0).then_inc(s_z, 1)

                @block.vector
                def _(dve):
                    chain = Chain(s_dve, dve)
                    dve.sem_inc(s_xn, 2)
                    with dve.Fori(0, UNITS // 2) as i:
                        for u in range(2):
                            j = 2 * i + u
                            dve.wait_ge(s_x[u], i * 16 + 16)
                            layer_stats(dve, chain, xt[u].unsqueeze(1), stats, mv)
                            dve.sem_inc(s_mv, 1)
                            dve.wait_ge(s_std, j + 1)
                            layer_scale(dve, chain, mv[:, :, 1], std, work, rstd)
                            chain.restart()
                            dve.wait_ge(s_t, j + 1)
                            dve.tensor_scalar(xs[u], xt[u], mv[:, 0, 0:1], rstd, ALU.subtract, ALU.mult).then_inc(s_xn, 1)
                            dve.wait_ge(s_l, j + 1)
                            dve.tensor_copy(ap(LG, j * E1, [[1, E1]]), pL[u][:, 0:E1]).then_inc(s_lg, 1)

                @block.scalar
                def _(act):
                    act.sem_inc(s_ev, 2)
                    with act.Fori(0, UNITS // 2) as i:
                        for u in range(2):
                            j = 2 * i + u
                            act.wait_ge(s_mv, j + 1)
                            act.activation(std, mv[:, :, 1], ACT.Sqrt, bias=eps).then_inc(s_std, 1)
                            act.wait_ge(s_xn, j + 3)
                            act.activation(ap(XN, j * ROW, [[1, C]]), xs[u], ACT.Copy)
                            act.wait_ge(s_t, j + 3)
                            act.activation(xT[u], pT[u], ACT.Copy).then_inc(s_ev, 1)

                @block.tensor
                def _(pe):
                    pe.sem_inc(s_t, 2)
                    pe.wait_ge(s_wr, 16)
                    with pe.Fori(0, UNITS // 2) as i:
                        for u in range(2):
                            j = 2 * i + u
                            pe.wait_ge(s_xn, j + 3)
                            pe.wait_ge(s_ev, j + 1)
                            for k in range(CB):
                                t = pe.transpose(pT[u][:, k, :], xs[u][:, k * P:(k + 1) * P], ident)
                            t.then_inc(s_t, 1)
                            pe.wait_ge(s_ev, j + 3)
                            for k in range(CB):
                                m = pe.matmul(pL[u][:, 0:E1], xT[u][:, k, :], wr[:, k, :], start=(k == 0), stop=(k == CB - 1))
                            m.then_inc(s_l, 1)

            with ExitStack() as st:
                A = [sb(st, f"A8{i}", [P, UNITS, E1]) for i in range(5)]
                over = sb(st, "over8", [P, UNITS, E1, E1])
                V = {n: sb(st, n + "_8", [P, UNITS]) for n in ("v1", "v2", "s1", "s2", "e2")}
                later = sb(st, "later8", [P, E1, E1])
                before = sb(st, "before8", [P, P])
                ones = sb(st, "ones8", [P, P])
                number = sb(st, "number8", [P, TILES9 + UNITS])
                numi = sb(st, "numi8", [P, TILES9 + UNITS], I32)
                N8 = {n: sb(st, n + "_8", [P, E1]) for n in ("n", "nt", "end", "x")}
                Ni = sb(st, "Ni8", [P, E1], I32)
                slot = [sb(st, f"slot8{i}", [P, UNITS], U32) for i in range(2)]
                pP = pb(st, "pP", [P, UNITS, E1])
                pN = pb(st, "pN", [P, UNITS, E1])
                s_c, s_mask, s_pre, s_d, s_e, s_dve, s_slot, s_sc, s_v = [sem(n + "_8", st) for n in (
                    "s_c", "s_mask", "s_pre", "s_d", "s_e", "s_dve", "s_slot", "s_sc", "s_v")]
                block = st.enter_context(nc.Block())

                @block.gpsimd
                def _(pool):
                    chain = Chain(s_c, pool)
                    chain.link(pool.memset(later, 1.0))
                    chain.link(pool.memset(before, 1.0))
                    chain.link(pool.memset(ones, 1.0))
                    chain.link(pool.affine_select(out=later, in_=later, compare_op=ALU.is_gt, fill=0.0, base=0,
                                                  pattern=[[1, E1], [-1, E1]], channel_multiplier=0))
                    chain.link(pool.affine_select(out=before, in_=before, compare_op=ALU.is_gt, fill=0.0, base=0,
                                                  pattern=[[1, P]], channel_multiplier=-1))
                    chain.link(pool.iota(numi[:, 0:TILES9], [[1, TILES9]], base=0, channel_multiplier=0))
                    chain.link(pool.iota(numi[:, TILES9:], [[P, UNITS]], base=0, channel_multiplier=1))
                    pool.wait_ge(s_slot, 1)
                    for j in range(UNITS):
                        for w in range(2):
                            pool.indirect_dma_start(
                                out=XS, out_offset=bass.IndirectOffsetOnAxis(ap=slot[w][:, j:j + 1], axis=0),
                                in_=XN[:, j, :], in_offset=None).then_inc(s_sc, 16)
                    pool.wait_ge(s_sc, 16 * 2 * UNITS)

                @block.scalar
                def _(act):
                    act.wait_ge(s_d, 1)
                    act.activation(V["e2"], V["s1"], ACT.Exp).then_inc(s_e, 1)

                @block.tensor
                def _(pe):
                    pe.wait_ge(s_mask, 1)
                    pe.matmul(pP.rearrange("p u e -> p (u e)"), before, A[2].rearrange("p u e -> p (u e)"), start=True, stop=True)
                    pe.matmul(pN.rearrange("p u e -> p (u e)"), ones, A[2].rearrange("p u e -> p (u e)"), start=True, stop=True
                              ).then_inc(s_pre, 1)

                @block.vector
                def _(dve):
                    chain = Chain(s_dve, dve)
                    link, inc = chain.link, chain.inc
                    best, second, both, t0, t1 = A
                    mine = ap(LG, 0, [[E1, UNITS], [1, E1], [0, E1]])
                    other = ap(LG, 0, [[E1, UNITS], [0, E1], [1, E1]])
                    link(dve.tensor_tensor(over, other, mine, ALU.is_gt))
                    link(dve.tensor_reduce(t0, over, op=ALU.add, axis=AX.X))
                    link(dve.tensor_tensor(over, other, mine, ALU.is_equal))
                    dve.wait_ge(s_c, 7)
                    link(dve.tensor_tensor(over, over, ap(later, 0, [[0, UNITS], [E1, E1], [1, E1]]), ALU.mult))
                    link(dve.tensor_reduce(t1, over, op=ALU.add, axis=AX.X))
                    link(dve.tensor_tensor(t0, t0, t1, ALU.add))
                    inc(dve.tensor_scalar(best, t0, 0.0, None, ALU.is_equal))
                    inc(dve.tensor_scalar(second, t0, 1.0, None, ALU.is_equal))
                    link(dve.tensor_scalar(both, t0, 1.0, None, ALU.is_le))
                    dve.sem_inc(s_mask, 1)

                    def pick(out_, which, of):
                        link(dve.tensor_tensor(t1, which, of, ALU.mult))
                        link(dve.tensor_reduce(out_, t1, op=ALU.add, axis=AX.X))

                    pick(V["v1"], best, LG)
                    pick(V["v2"], second, LG)
                    link(dve.tensor_tensor(V["s1"], V["v2"], V["v1"], ALU.subtract))
                    dve.sem_inc(s_d, 1)
                    inc(dve.tensor_copy(number, numi))
                    dve.wait_ge(s_e, 1)
                    link(dve.tensor_scalar(V["v1"], V["e2"], 1.0, None, ALU.add))
                    link(dve.reciprocal(V["v1"], V["v1"]))
                    link(dve.tensor_scalar(V["v1"], V["v1"], gates[:, 3:4], None, ALU.mult))
                    inc(dve.tensor_copy(XN[:, :, C + 1], V["v1"]))
                    inc(dve.tensor_tensor(XN[:, :, C + 2], V["v1"], V["e2"], ALU.mult))
                    inc(dve.tensor_copy(XN[:, :, C], number[:, TILES9:]))
                    pick(XN[:, :, C + 3], best, ap(number, 0, [[0, UNITS], [1, E1]]))
                    dve.wait_ge(s_pre, 1)
                    link(dve.tensor_copy(t0, pN))
                    cur, nxt, step = t0, t1, 1
                    while step < UNITS:
                        inc(dve.tensor_copy(nxt[:, 0:step], cur[:, 0:step]))
                        link(dve.tensor_tensor(nxt[:, step:], cur[:, step:], cur[:, 0:UNITS - step], ALU.add))
                        cur, nxt, step = nxt, cur, 2 * step
                    link(dve.tensor_copy(N8["n"], cur[:, UNITS - 1, :]))
                    link(dve.tensor_scalar(Ni, N8["n"], float(P - 1), None, ALU.add))
                    link(dve.tensor_scalar(Ni, Ni, 7, None, ALU.arith_shift_right))
                    link(dve.tensor_copy(N8["nt"], Ni))
                    a0, a1, step = N8["nt"], N8["end"], 1
                    link(dve.tensor_copy(N8["x"], N8["nt"]))
                    a0 = N8["x"]
                    while step < E1:
                        inc(dve.tensor_copy(a1[:, 0:step], a0[:, 0:step]))
                        link(dve.tensor_tensor(a1[:, step:], a0[:, step:], a0[:, 0:E1 - step], ALU.add))
                        a0, a1, step = a1, a0, 2 * step
                    cmp9 = over.rearrange("p u e f -> p (u e f)")[:, 0:TILES9 * E1].rearrange("p (t e) -> p t e", e=E1)
                    link(dve.tensor_tensor(cmp9, ap(number, 0, [[1, TILES9], [0, E1]]), ap(a0, 0, [[0, TILES9], [1, E1]]), ALU.is_ge))
                    link(dve.tensor_reduce(TE, cmp9, op=ALU.add, axis=AX.X))
                    link(dve.tensor_scalar(TE, TE, float(E1 - 1), None, ALU.min))
                    inc(dve.tensor_scalar(TEi, TE[0:1, :], float(CB * C), None, ALU.mult))
                    link(dve.tensor_tensor(a1, a0, N8["nt"], ALU.subtract))
                    link(dve.tensor_scalar(a1, a1, float(P), None, ALU.mult))
                    link(dve.tensor_tensor(nxt, cur, pN, ALU.subtract))
                    link(dve.tensor_tensor(nxt, nxt, pP, ALU.add))
                    link(dve.tensor_tensor(cur, nxt, ap(a1, 0, [[0, UNITS], [1, E1]]), ALU.add))
                    for w, which in enumerate((best, second)):
                        link(dve.tensor_tensor(nxt, which, cur, ALU.mult))
                        link(dve.tensor_reduce(V["s2"], nxt, op=ALU.add, axis=AX.X))
                        link(dve.tensor_copy(slot[w], V["s2"]))
                    dve.sem_inc(s_slot, 1)

        with ExitStack() as st:
            WP = sb(st, "WP", [P, E1, CB, C])
            xs = [sb(st, f"xs{i}", [P, ROW]) for i in range(2)]
            xT = [sb(st, f"x9T{i}", [P, CB, P]) for i in range(2)]
            hr = [sb(st, f"hr{i}", [P, C]) for i in range(2)]
            hT = [sb(st, f"hT{i}", [P, CB, P]) for i in range(2)]
            ys = [sb(st, f"ys{i}", [P, C]) for i in range(2)]
            idx = [sb(st, f"idx{i}", [P, 1], U32) for i in range(2)]
            wt = [sb(st, f"wt{i}", [P, 4]) for i in range(2)]
            pT = [pb(st, f"p9T{i}", [P, CB, P]) for i in range(2)]
            pH = [pb(st, f"pH{i}", [P, C]) for i in range(2)]
            pG = [pb(st, f"pG{i}", [P, CB, P]) for i in range(2)]
            pY = [pb(st, f"pY{i}", [P, C]) for i in range(2)]
            s_x = [sem(f"s_x9{i}", st) for i in range(2)]
            s_wp = [sem(f"s_wp9{i}", st) for i in range(2)]
            s_t, s_xT, s_h, s_hr, s_g, s_hT, s_y, s_w, s_ys, s_add, s_dve, s_go = [sem(n + "_9", st) for n in (
                "s_t", "s_xT", "s_h", "s_hr", "s_g", "s_hT", "s_y", "s_w", "s_ys", "s_add", "s_dve", "s_go")]
            block = st.enter_context(nc.Block())

            @block.sync
            def _(sp):
                for u in range(2):
                    sp.dma_start(xs[u], XS[u * P:(u + 1) * P]).then_inc(s_x[u], 16)
                for e in range(E1):
                    sp.dma_start(WP[:, e], a["w_proj"][e].rearrange("(k p) c -> p k c", p=P)).then_inc(s_wp[e >= 2], 16)
                with sp.Fori(0, TILES9 // 2 - 1) as i:
                    for u in range(2):
                        j = 2 * i + u
                        sp.wait_ge(s_t, j + 1)
                        sp.wait_ge(s_w, j + 1)
                        sp.dma_start(xs[u], XS.rearrange("(t p) w -> t p w", p=P)[j + 2]).then_inc(s_x[u], 16)

            @block.tensor
            def _(pe):
                def columns(j, i, u):
                    pe.wait_ge(s_x[u], i * 16 + 16)
                    pe.wait_ge(s_xT, j + 1)
                    for k in range(CB):
                        t = pe.transpose(pT[u][:, k, :], xs[u][:, k * P:(k + 1) * P], ident)
                    t.then_inc(s_t, 1)

                def up(j, u):
                    e = pe.value_load(TEi[0:1, j:j + 1] if isinstance(j, int) else ap(TEi, j, [[1, 1]]), min_val=0, max_val=(E1 - 1) * CB * C)
                    pe.wait_ge(s_xT, j + 3)
                    pe.wait_ge(s_hr, j + 1)
                    for k in range(CB):
                        m = pe.matmul(pH[u], xT[u][:, k, :], ap(WF, e + k * C, [[1, C]]), start=(k == 0), stop=(k == CB - 1))
                    m.then_inc(s_h, 1)

                def turn(j, u):
                    pe.wait_ge(s_hr, j + 3)
                    pe.wait_ge(s_hT, j + 1)
                    for k in range(CB):
                        t = pe.transpose(pG[u][:, k, :], hr[u][:, k * P:(k + 1) * P], ident)
                    t.then_inc(s_g, 1)

                def down(j, u):
                    e = pe.value_load(TEi[0:1, j:j + 1] if isinstance(j, int) else ap(TEi, j, [[1, 1]]), min_val=0, max_val=(E1 - 1) * CB * C)
                    pe.wait_ge(s_hT, j + 3)
                    pe.wait_ge(s_ys, j + 1)
                    for k in range(CB):
                        m = pe.matmul(pY[u], hT[u][:, k, :], ap(WP, e + k * C, [[1, C]]), start=(k == 0), stop=(k == CB - 1))
                    m.then_inc(s_y, 1)

                for s in (s_xT, s_hr, s_hT, s_ys, s_g, s_y):
                    pe.sem_inc(s, 2)
                pe.sem_inc(s_h, 1)
                pe.wait_ge(s_wf, 16 * E1)
                columns(0, 0, 0)
                up(0, 0)
                columns(1, 0, 1)
                turn(0, 0)
                for e in range(2):
                    pe.wait_ge(s_wp[e], 16 * (2 if e == 0 else E1 - 2))
                with pe.Fori(0, TILES9 // 2 - 1) as i:
                    for u in range(2):
                        j = 2 * i + u
                        up(j + 1, 1 - u)
                        columns(j + 2, i + 1, u)
                        down(j, u)
                        turn(j + 1, 1 - u)
                up(TILES9 - 1, 1)
                down(TILES9 - 2, 0)
                turn(TILES9 - 1, 1)
                down(TILES9 - 1, 1)

            @block.scalar
            def _(act):
                with act.Fori(0, TILES9 // 2) as i:
                    for u in range(2):
                        j = 2 * i + u
                        act.wait_ge(s_h, j + 2)
                        act.wait_ge(s_g, j + 1)
                        act.activation(hr[u], pH[u], ACT.Relu).then_inc(s_hr, 1)
                        act.wait_ge(s_g, j + 3)
                        act.wait_ge(s_y, j + 1)
                        act.activation(hT[u], pG[u], ACT.Square).then_inc(s_hT, 1)

            @block.vector
            def _(dve):
                chain = Chain(s_dve, dve)

                def columns(j, u):
                    dve.wait_ge(s_t, j + 1)
                    dve.wait_ge(s_h, j)
                    dve.tensor_copy(xT[u], pT[u]).then_inc(s_xT, 1)

                def body(j, u, more):
                    if more:
                        columns(j + 1, 1 - u)
                    x = xs[u]
                    te = ap(TE, j, [[1, 1]])
                    if not isinstance(j, int) or j > 1:
                        dve.wait_ge(s_add, 16 * (j - 1))
                    chain.inc(dve.tensor_scalar(wt[u][:, 0:1], x[:, C + 3:C + 4], te, None, ALU.is_equal))
                    chain.inc(dve.tensor_copy(idx[u], x[:, C:C + 1]))
                    chain.wait()
                    chain.inc(dve.tensor_scalar(wt[u][:, 1:2], wt[u][:, 0:1], -1.0, 1.0, ALU.mult, ALU.add))
                    chain.link(dve.tensor_tensor(wt[u][:, 2:3], wt[u][:, 0:1], x[:, C + 1:C + 2], ALU.mult))
                    chain.link(dve.tensor_tensor(wt[u][:, 1:2], wt[u][:, 1:2], x[:, C + 2:C + 3], ALU.mult))
                    chain.link(dve.tensor_tensor(wt[u][:, 3:4], wt[u][:, 1:2], wt[u][:, 2:3], ALU.add))
                    chain.restart()
                    dve.sem_inc(s_w, 1)
                    dve.wait_ge(s_y, j + 3)
                    dve.tensor_scalar(ys[u], pY[u], wt[u][:, 3:4], None, ALU.mult).then_inc(s_ys, 1)

                dve.wait_ge(s_t, 1)
                dve.tensor_copy(xT[0], pT[0]).then_inc(s_xT, 1)
                for u in range(2):
                    body(u, u, True)
                with dve.Fori(1, TILES9 // 2 - 1) as i:
                    for u in range(2):
                        body(2 * i + u, u, True)
                body(TILES9 - 2, 0, True)
                body(TILES9 - 1, 1, False)

            @block.gpsimd
            def _(pool):
                def add(j, u):
                    pool.wait_ge(s_ys, j + 3)
                    if not isinstance(j, int) or j > 0:
                        pool.wait_ge(s_add, 16 * j)
                    pool.sem_inc(s_go, 1)
                    pool.indirect_dma_start(out=out["out"], out_offset=bass.IndirectOffsetOnAxis(ap=idx[u], axis=0),
                                            in_=ys[u], in_offset=None, compute_op=ALU.add).then_inc(s_add, 16)

                for u in range(2):
                    add(u, u)
                with pool.Fori(1, TILES9 // 2) as i:
                    for u in range(2):
                        add(2 * i + u, u)
                pool.wait_ge(s_add, 16 * TILES9)


def kernel(x, ctx_2048, g_xattn, g_ffn, L0_xattn_ssm_kernel, L0_xattn_D, L0_ffn_sim_matrix, L0_ffn_gates,
           L0_ffn_w_q, L0_ffn_w_k, L0_ffn_w_v, L0_ffn_o_weights, L1_ffn_w_router, L1_ffn_w_fc, L1_ffn_w_proj):
    import numpy as _np
    import concourse.bacc as _bacc
    from concourse.bass_utils import run_bass_kernel_spmd as _run

    ctx = _np.asarray(ctx_2048)
    conv = ctx.reshape(HALF, B8, H0, HD0, CB, P)[..., ::-1].transpose(2, 5, 0, 4, 1, 3)
    conv = _np.concatenate([conv, conv[..., :CYC - HD0]], axis=-1)
    laid = {
        "x": x,
        "ctx": ctx,
        "ctx_conv": conv.reshape(H0, P, HALF * CB * B8 * CYC),
        "v_t": ctx.reshape(UNITS, P, CB, P).transpose(0, 3, 2, 1),
        "g": _np.concatenate([_np.asarray(g_xattn), _np.asarray(g_ffn)]),
        "kern_pad": _np.pad(_np.asarray(L0_xattn_ssm_kernel), ((0, 0), (P - 1, 0))),
        "skip": L0_xattn_D,
        "sim": L0_ffn_sim_matrix,
        "eg": L0_ffn_gates,
        "w_v": L0_ffn_w_v,
        "w_o": L0_ffn_o_weights,
        "w_router": L1_ffn_w_router,
        "w_fc": L1_ffn_w_fc,
        "w_proj": L1_ffn_w_proj,
    }
    laid = {name: _np.ascontiguousarray(array) for name, array in laid.items()}
    nc = _bacc.Bacc("TRN2", target_bir_lowering=False, num_devices=1)
    ins = {name: nc.dram_tensor("in_" + name, array.shape, F32, kind="ExternalInput").ap()
           for name, array in laid.items()}
    out = nc.dram_tensor("out_rows", [B * T + P, C], F32, kind="ExternalOutput").ap()
    build(nc, ins, {"out": out})
    r = _run(nc, [{"in_" + name: array for name, array in laid.items()}], core_ids=[0])
    return r.results[0]["out_rows"][:B * T].reshape(B, T, C)
```

```python
import numpy as np
from contextlib import ExitStack
import concourse.bass as bass
from concourse import mybir

F32 = mybir.dt.float32
F32R = mybir.dt.float32r
I32 = mybir.dt.int32
U32 = mybir.dt.uint32
ALU = mybir.AluOpType
ACT = mybir.ActivationFunctionType
AX = mybir.AxisListType

P = 128
B, T, C = 16, 256, 512
TH = T // P
CB = C // P
H0, HD0 = 32, 8
HALF, B8 = 2, B // 2
CYC = 12
NDG = HD0 // 2 + 1
PAIRS = HD0 * (HD0 + 1) // 2
SLOT = NDG + 2 * (NDG - 2)
E0, EH = 32, 64
HQ, HR = 4, EH // 4
NH, HD1 = 4, 32
SCALE1 = float(HD1) ** -0.5
E1 = 8
UNITS = B * TH
TILES9 = 2 * ((2 * UNITS + E1 - 1 + 1) // 2)
ROW = C + 4
FALLBACK = E0 // 2
EPS = 1e-5
FMAX = float(np.finfo(np.float32).max)


def ap(view, offset, dims):
    return bass.AP(view.tensor, view.offset + offset, [list(view.ap[0])] + [list(d) for d in dims])


class Chain:

    def __init__(self, sem, eng):
        self.sem, self.eng, self.n = sem, eng, 0

    def inc(self, instruction):
        instruction.then_inc(self.sem, 1)
        self.n += 1

    def link(self, instruction):
        self.inc(instruction)
        self.wait()

    def wait(self):
        self.eng.wait_ge(self.sem, self.n)

    def restart(self):
        self.wait()
        self.eng.sem_clear(self.sem)
        self.n = 0


def layer_stats(dve, chain, rows, stats, mv):
    for n, row in enumerate(rows):
        chain.inc(dve.bn_stats(stats[:, n, :], row))
    chain.wait()
    for n in range(len(rows)):
        chain.inc(dve.bn_aggr(mv[:, n, :], stats[:, n, :]))
    chain.restart()


def layer_scale(dve, chain, var, std, work, rstd, eps=EPS):
    chain.link(dve.reciprocal(rstd, std))
    chain.link(dve.scalar_tensor_tensor(work, var, eps, rstd, ALU.add, ALU.mult))
    chain.link(dve.tensor_tensor(work, work, rstd, ALU.mult))
    chain.link(dve.tensor_scalar(work, work, -0.5, 1.5, ALU.mult, ALU.add))
    chain.link(dve.tensor_tensor(rstd, rstd, work, ALU.mult))


def pipelined(eng, count, lag, step):
    def at(i, u):
        def item(d=0):
            n = 2 * i + u + d
            if isinstance(n, int) and not 0 <= n < count:
                return None
            return n, (u + d) % 2, i + (u + d) // 2
        return item

    for n in range(-lag, 0):
        step(at(n // 2, n % 2))
    with eng.Fori(0, (count - lag) // 2) as i:
        for u in range(2):
            step(at(i, u))
    for n in range(count - lag, count):
        step(at(n // 2, n % 2))


def both(item, *works):
    for work in works if item else ():
        work(*item)


def build(nc, a, out):
    with ExitStack() as whole:
        _build(nc, a, out, whole)


def _build(nc, a, out, whole):
    def sem(name, ctx=whole):
        return ctx.enter_context(nc.semaphore(name))

    def sb(ctx, name, shape, dt=F32):
        return ctx.enter_context(nc.sbuf_tensor(name, shape, dt))[:]

    def pb(ctx, name, shape, dt=F32):
        return ctx.enter_context(nc.psum_tensor(name, shape, dt))[:]

    KP = nc.dram_tensor("kernel_and_skip", [H0, P - 1 + C], F32).ap()
    WO = nc.dram_tensor("mixed_out_weights", [B, EH, C], F32).ap()
    QH = nc.dram_tensor("q_high", [B, T, C], F32).ap()
    QL = nc.dram_tensor("q_low", [B, T, C], F32).ap()
    XS = nc.dram_tensor("experts_rows", [TILES9 * P, ROW], F32).ap()
    KH = nc.dram_tensor("ctx_high", [B, T, C], F32).ap()
    KL = nc.dram_tensor("ctx_low", [B, T, C], F32).ap()

    ident = sb(whole, "ident", [P, P])
    gates = sb(whole, "gates", [P, 4])
    gates_raw = sb(whole, "gates_raw", [P, 4])
    eps = sb(whole, "eps", [P, 1])
    s_ident = sem("s_ident")
    s_eps = sem("s_eps")
    s_gates = sem("s_gates")
    XN = sb(whole, "XN", [P, UNITS, ROW])

    def x_rows(b):
        return [ap(XN, (TH * b + th) * ROW, [[1, C]]) for th in range(TH)]

    with ExitStack() as era1:
        QT = sb(era1, "QT", [P, H0 * HALF * CB * B8 * HD0])
        HSTEP, HALFSTEP, BLKSTEP = HALF * CB * B8 * HD0, CB * B8 * HD0, B8 * HD0

        def columns_of(b, k, blocks=1):
            dims = [[HSTEP, H0], [1, HD0]]
            if blocks > 1:
                dims = [[BLKSTEP, blocks]] + dims
            return ap(QT, (b // B8) * HALFSTEP + (b % B8) * HD0 + k * BLKSTEP, dims)

        with ExitStack() as st:
            qt = [sb(st, f"qt{i}", [P, TH, C]) for i in range(2)]
            stats = sb(st, "stats", [P, TH, 6])
            mv = [sb(st, f"mv{i}", [P, TH, 2]) for i in range(2)]
            std = [sb(st, f"std{i}", [P, TH]) for i in range(2)]
            work = [sb(st, f"work_{i}", [P, TH]) for i in range(2)]
            rstd = [sb(st, f"rstd_{i}", [P, TH]) for i in range(2)]
            kp = sb(st, "kp", [H0, P - 1 + C])
            skip = sb(st, "skip", [H0, 1])
            pq = [pb(st, f"pq{i}", [P, CB, T]) for i in range(2)]
            s_x = [sem(f"s_x{i}", st) for i in range(2)]
            s_q, s_tr, s_ev, s_dve, s_mv, s_std, s_kp, s_skip, s_kps, s_g = [sem(n, st) for n in (
                "s_q", "s_tr", "s_ev", "s_dve", "s_mv", "s_std", "s_kp", "s_skip", "s_kps", "s_g")]
            block = st.enter_context(nc.Block())

            @block.sync
            def _(sp):
                def load(b, u):
                    sp.dma_start(ap(XN, TH * b * ROW, [[ROW, TH], [1, C]]), a["x"][b].rearrange("(th p) c -> p th c", p=P)).then_inc(s_x[u], 16)

                load(0, 0)
                load(1, 1)
                sp.dma_start(kp, a["kern_pad"]).then_inc(s_kp, 16)
                sp.dma_start(skip, a["skip"].rearrange("(h o) -> h o", o=1)).then_inc(s_kp, 16)
                sp.dma_start(gates_raw, a["g"].partition_broadcast(P)).then_inc(s_g, 16)
                with sp.Fori(1, B // 2) as i:
                    for u in range(2):
                        sp.wait_ge(s_x[u], 16 * i)
                        load(2 * i + u, u)
                sp.wait_ge(s_skip, 1)
                sp.dma_start(KP, kp).then_inc(s_kps, 16)
                sp.wait_ge(s_kps, 16)

            @block.vector
            def _(dve):
                chain = Chain(s_dve, dve)

                def measure(b, u, i):
                    dve.wait_ge(s_x[u], 16 * i + 16)
                    layer_stats(dve, chain, x_rows(b), stats, mv[u])
                    dve.sem_inc(s_mv, 1)

                def norm(b, u, i):
                    dve.wait_ge(s_std, b + 1)
                    dve.wait_ge(s_tr, b + 1)
                    layer_scale(dve, chain, mv[u][:, :, 1], std[u], work[u], rstd[u])
                    chain.restart()
                    for th, row in enumerate(x_rows(b)):
                        q = dve.tensor_scalar(qt[u][:, th, :], row, mv[u][:, th, 0:1], rstd[u][:, th:th + 1],
                                              ALU.subtract, ALU.mult)
                    q.then_inc(s_q, 1)

                def step(k):
                    both(k(1), measure)
                    both(k(), norm)

                pipelined(dve, B, 2, step)
                dve.wait_ge(s_kp, 32)
                dve.tensor_tensor(kp[:, P - 1:P], kp[:, P - 1:P], skip, ALU.add).then_inc(s_skip, 1)

            @block.gpsimd
            def _(pool):
                pool.memset(eps, EPS).then_inc(s_eps, 1)
                pool.memset(ident, 0.0).then_inc(s_ident, 1)
                pool.wait_ge(s_ident, 1)
                pool.affine_select(out=ident, in_=ident, compare_op=ALU.not_equal, fill=1.0, base=0,
                                   pattern=[[-1, P]], channel_multiplier=1).then_inc(s_ident, 1)

            @block.scalar
            def _(act):
                act.wait_ge(s_eps, 1)
                act.wait_ge(s_g, 16)
                act.activation(gates, gates_raw, ACT.Tanh).then_inc(s_gates, 1)

                def root(b, u, i):
                    act.wait_ge(s_mv, b + 1)
                    act.activation(std[u], mv[u][:, :, 1], ACT.Sqrt, bias=eps).then_inc(s_std, 1)

                def keep(b, u, i):
                    act.wait_ge(s_tr, b + 3)
                    for k in range(CB // 2):
                        e = act.activation(columns_of(b, 2 * k, 2),
                                           pq[u][:, 2 * k:2 * k + 2, :].rearrange("p k (h j) -> p k h j", j=HD0), ACT.Copy)
                    e.then_inc(s_ev, 1)

                def step(k):
                    both(k(1), root)
                    both(k(), keep)

                pipelined(act, B, 2, step)

            @block.tensor
            def _(pe):
                pe.wait_ge(s_ident, 2)
                pe.sem_inc(s_tr, 2)
                pe.sem_inc(s_ev, 2)
                with pe.Fori(0, B // 2) as i:
                    for u in range(2):
                        b = 2 * i + u
                        pe.wait_ge(s_q, b + 1)
                        pe.wait_ge(s_ev, b + 1)
                        for th in range(TH):
                            for k in range(CB):
                                t = pe.transpose(pq[u][:, k, th * P:(th + 1) * P], qt[u][:, th, k * P:(k + 1) * P], ident)
                        t.then_inc(s_tr, 1)

        with ExitStack() as st:
            toep = [sb(st, f"toep{i}", [P, C]) for i in range(2)]
            kc = [sb(st, f"kc{i}", [P, HALF * CB * B8, CYC]) for i in range(2)]
            kv = [sb(st, f"kv{i}", [P, HALF, CB, B8 * PAIRS]) for i in range(2)]
            qc = [sb(st, f"qc{i}", [P, HALF * CB * B8, 2 * HD0]) for i in range(2)]
            z = [sb(st, f"z{i}", [P, CB * B8, SLOT * HD0]) for i in range(2)]
            y = [pb(st, f"y{i}", [P, CB * B8, 64]) for i in range(2)]
            s_kc = [sem(f"s_kc{i}", st) for i in range(2)]
            s_tp = [sem(f"s_tp{i}", st) for i in range(2)]
            s_kv = sem("s_kv", st)
            s_qc = sem("s_qc", st)
            s_y = sem("s_y", st)
            s_tt = sem("s_tt", st)
            s_pad = sem("s_pad", st)
            s_fill = sem("s_fill", st)
            pad = sb(st, "pad", [P, ROW])
            ct = sb(st, "ct", [P, TH, C])
            kh = sb(st, "kh", [P, TH, C])
            kl = sb(st, "kl", [P, TH, C])
            s_c, s_kh, s_kl, s_ks = [sem(n + "_2", st) for n in ("s_c", "s_kh", "s_kl", "s_ks")]
            padi = sb(st, "padi", [P, 1], I32)
            s_o = sem("s_o", st)
            s_z0 = sem("s_z0", st)
            s_dve = sem("s_dve2", st)
            block = st.enter_context(nc.Block())

            @block.sync
            def _(sp):
                with sp.Fori(0, H0 // 2) as i:
                    sp.wait_ge(s_kl, i + 1)
                    sp.dma_start(ct, a["ctx"].rearrange("b (th p) c -> b p th c", p=P)[i]).then_inc(s_c, 16)
                    for u in range(2):
                        h = 2 * i + u
                        sp.wait_ge(s_kv, 2 * h + 2)
                        sp.dma_start(kc[u].rearrange("p n c -> p (n c)"), a["ctx_conv"][h]).then_inc(s_kc[u], 16)
                        sp.wait_ge(s_y, 2 * h + 2)
                        sp.dma_start(toep[u], bass.AP(KP.tensor, h * (P - 1 + C), [[1, P], [1, C]])).then_inc(s_tp[u], 16)

            @block.gpsimd
            def _(pool):
                for i in range(2):
                    pool.memset(z[i], 0.0).then_inc(s_z0, 1)
                pool.memset(pad, 0.0).then_inc(s_pad, 1)
                pool.iota(padi, [[1, 1]], base=B * T, channel_multiplier=1).then_inc(s_pad, 1)
                pool.sem_inc(s_kv, 4)
                pool.sem_inc(s_kl, 1)
                with pool.Fori(0, H0 // 2) as i:
                    for u in range(2):
                        h = 2 * i + u
                        pool.wait_ge(s_kc[u], i * 16 + 16)
                        pool.wait_ge(s_y, 2 * h + 2)
                        n = HALF * CB * B8
                        D4 = NDG - 1
                        pool.tensor_tensor(ap(kv[u], 0, [[PAIRS, n], [HD0, D4], [1, HD0]]),
                                           ap(kc[u], 0, [[CYC, n], [0, D4], [1, HD0]]),
                                           ap(kc[u], 0, [[CYC, n], [1, D4], [1, HD0]]), ALU.mult).then_inc(s_kv, 1)
                        pool.tensor_tensor(ap(kv[u], D4 * HD0, [[PAIRS, n], [1, HD0 // 2]]),
                                           ap(kc[u], 0, [[CYC, n], [1, HD0 // 2]]),
                                           ap(kc[u], HD0 // 2, [[CYC, n], [1, HD0 // 2]]), ALU.mult).then_inc(s_kv, 1)
                    pool.wait_ge(s_kh, i + 1)
                    pool.wait_ge(s_ks, 32 * i + 32)
                    pool.tensor_tensor(kl.bitcast(F32R), ct, kh, ALU.subtract).then_inc(s_kl, 1)

            @block.scalar
            def _(act):
                act.wait_ge(s_pad, 2)
                act.activation(pad[:, C:C + 1], padi, ACT.Copy).then_inc(s_pad, 1)
                act.wait_ge(s_pad, 3)
                lists = XS.rearrange("(t p) w -> p t w", p=P)
                for n in range(TILES9 - 4 * (H0 // 2)):
                    act.dma_start(lists[:, n, :], pad).then_inc(s_fill, 16)
                act.sem_inc(s_ks, 32)
                with act.Fori(0, H0 // 2) as i:
                    for n in range(4):
                        act.dma_start(XS.rearrange("(t p) w -> t p w", p=P)[TILES9 - 4 * (H0 // 2) + 4 * i + n], pad).then_inc(s_fill, 16)
                    for u in range(2):
                        h = 2 * i + u
                        act.wait_ge(s_tt, 6 * h + 6)
                        n = HALF * CB * B8
                        act.activation(qc[u].rearrange("p n (r j) -> p n r j", r=2),
                                       ap(QT, h * HSTEP, [[HD0, n], [0, 2], [1, HD0]]), ACT.Copy).then_inc(s_qc, 1)
                        if u == 0:
                            act.wait_ge(s_c, 16 * i + 16)
                            act.wait_ge(s_ks, 32 * i + 32)
                            act.activation(kh.bitcast(F32R), ct, ACT.Copy).then_inc(s_kh, 1)
                    act.wait_ge(s_kl, i + 2)
                    for part, to in ((kh, KH), (kl, KL)):
                        act.dma_start(to.rearrange("b (th p) c -> b p th c", p=P)[i], part).then_inc(s_ks, 16)
                act.wait_ge(s_ks, 32 * B + 32)
                act.wait_ge(s_fill, 16 * TILES9)

            @block.tensor
            def _(pe):
                pe.sem_inc(s_y, 4)
                pe.sem_inc(s_tt, 12)
                with pe.Fori(0, H0 // 2) as i:
                    for u in range(2):
                        h = 2 * i + u
                        pe.wait_ge(s_tp[u], i * 16 + 16)
                        pe.wait_ge(s_kv, 2 * h + 6)
                        for half in range(HALF):
                            pe.wait_ge(s_tt, 6 * h + 3 * half + 9)
                            for l in range(CB):
                                for s in range(l + 1):
                                    m = pe.matmul(y[half].rearrange("p (l n) c -> p l n c", l=CB)[:, l, :, 0:PAIRS],
                                                  toep[u][:, (l - s) * P:(l - s + 1) * P],
                                                  kv[u][:, half, s, :].rearrange("p (n c) -> p n c", c=PAIRS),
                                                  start=(s == 0), stop=(s == l))
                            m.then_inc(s_y, 1)

            @block.vector
            def _(dve):
                chain = Chain(s_dve, dve)
                n = CB * B8
                W = SLOT * HD0
                H4, D4 = HD0 // 2, NDG - 1

                def weigh(h, u, i, half):
                    if half == 0:
                        dve.wait_ge(s_qc, h + 1)
                    dve.wait_ge(s_y, 2 * h + half + 5)
                    q0 = half * n * 2 * HD0
                    for out_, in0, in1 in (
                            (ap(z[half], 0, [[W, n], [HD0, D4], [1, HD0]]),
                             ap(y[half], 0, [[64, n], [HD0, D4], [1, HD0]]),
                             ap(qc[u], q0, [[2 * HD0, n], [1, D4], [1, HD0]])),
                            (ap(z[half], D4 * HD0, [[W, n], [H4, 2], [1, H4]]),
                             ap(y[half], D4 * HD0, [[64, n], [0, 2], [1, H4]]),
                             ap(qc[u], q0 + H4, [[2 * HD0, n], [H4, 2], [1, H4]])),
                            (ap(z[half], NDG * HD0 + 1, [[W, n], [2 * HD0 + 1, NDG - 2], [1, HD0]]),
                             ap(y[half], HD0, [[64, n], [HD0, NDG - 2], [1, HD0]]),
                             ap(qc[u], q0, [[2 * HD0, n], [0, NDG - 2], [1, HD0]]))):
                        dve.tensor_tensor(out_, in0, in1, ALU.mult).then_inc(s_tt, 1)

                def total(h, u, i, half):
                    dve.wait_ge(s_tt, 6 * h + 3 * half + 15)
                    chain.link(dve.tensor_reduce(
                        ap(QT, h * HSTEP + half * HALFSTEP, [[HD0, n], [1, HD0]]),
                        ap(z[half], 0, [[W, n], [1, HD0], [HD0, SLOT]]), op=ALU.add, axis=AX.X))

                def step(k):
                    if k():
                        weigh(*k(), 0)
                    if k(-1):
                        total(*k(-1), 1)
                    if k():
                        weigh(*k(), 1)
                        total(*k(), 0)
                    chain.restart()

                dve.wait_ge(s_z0, 2)
                step(lambda d=0: ((0, 0, 0) if d == 0 else None))
                step(lambda d=0: (1 + d, 1 + d, 0))
                with dve.Fori(1, H0 // 2) as i:
                    for u in range(2):
                        step(lambda d=0: (2 * i + u + d, (u + d) % 2, i + (u + d) // 2))
                total(H0 - 1, 1, H0 // 2 - 1, 1)
                chain.restart()

        SR = sb(era1, "SR", [P, CB, B])
        WM = sb(era1, "WM", [P, B, CB, EH])
        era2 = whole.enter_context(ExitStack())
        WV = sb(era2, "WV", [P, HR, C])
        s_wv = sem("s_wv", era2)
        with ExitStack() as st:
            ot = [sb(st, f"ot{i}", [P, CB, T]) for i in range(2)]
            hs = [sb(st, f"hs{i}", [P, TH, C]) for i in range(2)]
            stats = sb(st, "stats3", [P, TH, 6])
            mv = [sb(st, f"mv3{i}", [P, TH, 2]) for i in range(2)]
            std = [sb(st, f"std3{i}", [P, TH]) for i in range(2)]
            work = [sb(st, f"work3_{i}", [P, TH]) for i in range(2)]
            rstd = [sb(st, f"rstd3_{i}", [P, TH]) for i in range(2)]
            px = [pb(st, f"px{i}", [P, TH, C]) for i in range(2)]
            ph = [pb(st, f"ph{i}", [P, CB, T]) for i in range(2)]
            s_ot, s_t1, s_t2, s_x1, s_mv, s_std, s_hs, s_ev, s_dve, s_go = [sem(n + "_3", st) for n in (
                "s_ot", "s_t1", "s_t2", "s_x1", "s_mv", "s_std", "s_hs", "s_ev", "s_dve", "s_go")]
            block = st.enter_context(nc.Block())

            @block.sync
            def _(sp):
                for hq in range(HQ):
                    sp.dma_start(WV[hq * E0:(hq + 1) * E0], a["w_v"][:, hq * HR:(hq + 1) * HR, :]).then_inc(s_wv, 16)

            @block.gpsimd
            def _(pool):
                with pool.Fori(0, B // 2) as i:
                    for u in range(2):
                        b = 2 * i + u
                        pool.wait_ge(s_t1, b + 1)
                        pool.sem_inc(s_go, 1)
                        for k in range(CB):
                            pool.tensor_copy(ot[u][:, k, :].rearrange("p (h j) -> p h j", j=HD0), columns_of(b, k)).then_inc(s_ot, 1)

            @block.tensor
            def _(pe):
                pe.sem_inc(s_t1, 2)
                pe.sem_inc(s_t2, 2)

                def back(b, u, i):
                    pe.wait_ge(s_ot, 4 * b + 4)
                    pe.wait_ge(s_x1, b + 1)
                    for th in range(TH):
                        for k in range(CB):
                            t = pe.transpose(px[u][:, th, k * P:(k + 1) * P], ot[u][:, k, th * P:(th + 1) * P], ident)
                    t.then_inc(s_t1, 1)

                def forth(b, u, i):
                    pe.wait_ge(s_hs, b + 1)
                    pe.wait_ge(s_ev, b + 1)
                    for k in range(CB):
                        for th in range(TH):
                            t = pe.transpose(ph[u][:, k, th * P:(th + 1) * P], hs[u][:, th, k * P:(k + 1) * P], ident)
                    t.then_inc(s_t2, 1)

                def step(k):
                    both(k(2), back)
                    both(k(), forth)

                pipelined(pe, B, 2, step)

            @block.vector
            def _(dve):
                chain = Chain(s_dve, dve)
                dve.sem_inc(s_x1, 2)

                def add(b, u, i):
                    dve.wait_ge(s_t1, b + 3)
                    for th, row in enumerate(x_rows(b)):
                        chain.inc(dve.scalar_tensor_tensor(row, px[u][:, th, :], gates[:, 0:1], row, ALU.mult, ALU.add))
                    chain.wait()
                    dve.sem_inc(s_x1, 1)
                    layer_stats(dve, chain, x_rows(b), stats, mv[u])
                    dve.sem_inc(s_mv, 1)

                def norm(b, u, i):
                    dve.wait_ge(s_std, b + 1)
                    dve.wait_ge(s_t2, b + 1)
                    layer_scale(dve, chain, mv[u][:, :, 1], std[u], work[u], rstd[u])
                    chain.restart()
                    for th, row in enumerate(x_rows(b)):
                        q = dve.tensor_scalar(hs[u][:, th, :], row, mv[u][:, th, 0:1], rstd[u][:, th:th + 1],
                                              ALU.subtract, ALU.mult)
                    q.then_inc(s_hs, 1)

                def step(k):
                    both(k(1), add)
                    both(k(), norm)

                pipelined(dve, B, 2, step)

            @block.scalar
            def _(act):
                act.sem_inc(s_ev, 2)

                def root(b, u, i):
                    act.wait_ge(s_mv, b + 1)
                    act.activation(std[u], mv[u][:, :, 1], ACT.Sqrt, bias=eps).then_inc(s_std, 1)

                def keep(b, u, i):
                    act.wait_ge(s_t2, b + 3)
                    for k in range(CB):
                        e = act.activation(columns_of(b, k), ph[u][:, k, :].rearrange("p (h j) -> p h j", j=HD0), ACT.Copy,
                                           accum_out=ap(SR, b + k * B, [[1, 1]]))
                    e.then_inc(s_ev, 1)

                def step(k):
                    both(k(1), root)
                    both(k(), keep)

                pipelined(act, B, 2, step)

        with ExitStack() as st:
            GR = HR // 4
            WOS = sb(st, "WOS", [HQ * B, 2, GR, C])
            sim = sb(st, "sim", [P, CB, E0])
            sim2 = sb(st, "sim2", [P, CB, E0])
            sr2 = sb(st, "sr2", [P, CB, B])
            ones = sb(st, "ones4", [P, B])
            later, over, same = (WM[0:B].rearrange("p b k h -> p (b k h)")[:, n * E0 * E0:(n + 1) * E0 * E0]
                                 .rearrange("p (e f) -> p e f", f=E0) for n in range(3))
            eg = sb(st, "eg", [B, E0])
            t = {n: sb(st, n + "_4", [B, E0]) for n in ("sig", "logits", "gated", "mask", "rank", "z", "e", "rm")}
            nn = sb(st, "nn", [B, E0 + 1])
            rn = sb(st, "rn", [B, E0 + 1])
            sq = sb(st, "sq", [B, E0 + 1])
            wk = sb(st, "wk", [B, E0 + 1])
            cnt = sb(st, "cnt", [B, 1])
            zmax = sb(st, "zmax", [B, 1])
            zsum = sb(st, "zsum", [B, 1])
            RB = sb(st, "RB", [P, HQ * B])
            p_aff = pb(st, "p_aff", [B, C])
            p_n = pb(st, "p_n", [B, C])
            p_e = pb(st, "p_e", [B, C])
            p_rm = pb(st, "p_rm", [P, C])
            p_w = [pb(st, f"p_w{i}", [P, 8, 64]) for i in range(4)]
            (s_in4, s_con, s_pe, s_act, s_dve, s_sr, s_rm, s_rb, s_wp, s_wd, s_wa, s_wp2) = [
                sem(n + "_4", st) for n in ("s_in", "s_con", "s_pe", "s_act", "s_dve", "s_sr", "s_rm", "s_rb",
                                            "s_wp", "s_wd", "s_wa", "s_wp2")]
            s_wst = [sem(f"s_wst4{i}", st) for i in range(2)]
            s_wo = [sem(f"s_wo4{i}", st) for i in range(2)]
            block = st.enter_context(nc.Block())

            @block.sync
            def _(sp):
                sp.dma_start(sim, a["sim"].rearrange("(k p) e -> p k e", p=P)).then_inc(s_in4, 16)
                sp.dma_start(eg, a["eg"].partition_broadcast(B)).then_inc(s_in4, 16)
                for n in range(2):
                    sp.wait_ge(s_wp, HR // 4 * (n + 1))
                    for hq in range(HQ):
                        sp.dma_start(WV[hq * E0:(hq + 1) * E0, 8 * n:8 * n + 8, :],
                                     a["w_o"][:, hq * HR + 8 * n:hq * HR + 8 * n + 8, :]).then_inc(s_wo[n], 16)
                for n in range(HR // GR):
                    sp.wait_ge(s_wa, (n + 1) * GR)
                    for hq in range(HQ):
                        sp.dma_start(WO[:, hq * HR + n * GR:hq * HR + (n + 1) * GR, :],
                                     WOS[hq * B:(hq + 1) * B, n % 2]).then_inc(s_wst[n % 2], 16)
                for n in range(2):
                    sp.wait_ge(s_wst[n], 16 * HQ * HR // GR // 2)

            @block.gpsimd
            def _(pool):
                pool.memset(ones, 1.0).then_inc(s_con, 1)
                pool.memset(RB, 0.0).then_inc(s_con, 1)
                pool.memset(later, 1.0).then_inc(s_con, 1)
                pool.wait_ge(s_con, 3)
                pool.affine_select(out=later, in_=later, compare_op=ALU.is_gt, fill=0.0, base=0,
                                   pattern=[[1, E0], [-1, E0]], channel_multiplier=0).then_inc(s_con, 1)

            @block.vector
            def _(dve):
                chain = Chain(s_dve, dve)
                dve.wait_ge(s_in4, 32)
                chain.inc(dve.tensor_scalar(SR, SR, 1.0 / T, None, ALU.mult))
                chain.link(dve.tensor_tensor(sim2, sim, sim, ALU.mult))
                dve.tensor_tensor(sr2, SR, SR, ALU.mult).then_inc(s_sr, 1)
                dve.wait_ge(s_pe, 1)
                chain.inc(dve.tensor_copy(nn[:, 0:E0], p_e[:, 0:E0]))
                chain.link(dve.tensor_copy(nn[:, E0:], p_n[:, 0:1]))
                dve.sem_inc(s_sr, 1)
                dve.wait_ge(s_act, 2)
                layer_scale(dve, chain, nn, sq, wk, rn, 0.0)
                chain.link(dve.tensor_scalar(t["sig"], t["e"], 1.0, None, ALU.add))
                chain.link(dve.reciprocal(t["sig"], t["sig"]))
                chain.link(dve.scalar_tensor_tensor(t["logits"], p_aff[:, 0:E0], rn[:, E0:], rn[:, 0:E0], ALU.mult, ALU.mult))
                chain.link(dve.tensor_tensor(t["logits"], t["logits"], t["sig"], ALU.subtract))
                chain.inc(dve.tensor_scalar(t["gated"], t["logits"], 0.0, None, ALU.max))
                chain.link(dve.tensor_scalar(t["mask"], t["logits"], 0.0, None, ALU.is_gt))
                chain.link(dve.tensor_reduce(cnt, t["mask"], op=ALU.add, axis=AX.X))
                chain.link(dve.tensor_scalar(cnt, cnt, 0.0, None, ALU.is_equal))
                dve.wait_ge(s_con, 4)
                mine = ap(t["logits"], 0, [[1, E0], [0, E0]])
                other = ap(t["logits"], 0, [[0, E0], [1, E0]])
                chain.inc(dve.tensor_tensor(over, other, mine, ALU.is_gt))
                chain.link(dve.tensor_tensor(same, other, mine, ALU.is_equal))
                chain.link(dve.tensor_tensor(same, same, later, ALU.mult))
                chain.link(dve.tensor_tensor(over, over, same, ALU.add))
                chain.link(dve.tensor_reduce(t["rank"], over, op=ALU.add, axis=AX.X))
                chain.link(dve.tensor_scalar(t["rank"], t["rank"], float(FALLBACK), cnt, ALU.is_lt, ALU.mult))
                chain.link(dve.tensor_tensor(t["mask"], t["mask"], t["rank"], ALU.max))
                chain.inc(dve.tensor_tensor(t["gated"], t["gated"], t["mask"], ALU.mult))
                chain.link(dve.tensor_scalar(t["z"], t["mask"], FMAX, -FMAX, ALU.mult, ALU.add))
                chain.link(dve.tensor_tensor(t["z"], t["z"], t["gated"], ALU.add))
                chain.link(dve.tensor_reduce(zmax, t["z"], op=ALU.max, axis=AX.X, negate=True))
                dve.sem_inc(s_sr, 1)
                dve.wait_ge(s_act, 3)
                chain.link(dve.reciprocal(zsum, zsum))
                dve.scalar_tensor_tensor(t["rm"], t["e"], zsum, t["mask"], ALU.mult, ALU.mult).then_inc(s_rm, 1)
                dve.wait_ge(s_pe, 2)
                for g in range(HQ):
                    c = dve.tensor_copy(RB[g * E0:(g + 1) * E0, g * B:(g + 1) * B], p_rm[g * E0:(g + 1) * E0, 0:B])
                    chain.inc(c)
                chain.wait()
                dve.sem_inc(s_rb, 1)
                for r in range(HR):
                    dve.wait_ge(s_wp, r // 2 + 1)
                    dve.tensor_copy(ap(WM, r, [[EH, CB], [HR, HQ], [CB * EH, B]]),
                                    p_w[r // 2 % 2][:, 4 * (r % 2):4 * (r % 2) + 4, :].rearrange("p k (q b) -> p k q b", q=HQ)
                                    ).then_inc(s_wd, 1)

            @block.scalar
            def _(act):
                act.wait_ge(s_in4, 32)
                act.activation(t["e"], eg, ACT.Exp, scale=-1.0).then_inc(s_act, 1)
                act.wait_ge(s_sr, 2)
                act.activation(sq, nn, ACT.Sqrt).then_inc(s_act, 1)
                act.wait_ge(s_sr, 3)
                act.activation(t["e"], t["z"], ACT.Exp, bias=zmax, accum_out=zsum).then_inc(s_act, 1)
                for r in range(HR):
                    act.wait_ge(s_wp2, r + 1)
                    n = r // GR
                    if r % GR == 0 and n >= 2:
                        act.wait_ge(s_wst[n % 2], 16 * HQ * (n // 2))
                    act.activation(WOS[:, n % 2, r % GR, :], p_w[2 + r % 2][0:HQ * B].rearrange("p a b -> p (a b)"), ACT.Copy).then_inc(s_wa, 1)

            @block.tensor
            def _(pe):
                pe.wait_ge(s_sr, 1)
                pe.wait_ge(s_con, 2)
                pe.wait_ge(s_in4, 32)
                for k in range(CB):
                    pe.matmul(p_aff[:, 0:E0], SR[:, k, :], sim[:, k, :], start=(k == 0), stop=(k == CB - 1))
                for k in range(CB):
                    pe.matmul(p_n[:, 0:1], sr2[:, k, :], ones[:, 0:1], start=(k == 0), stop=(k == CB - 1))
                for k in range(CB):
                    m = pe.matmul(p_e[:, 0:E0], ones, sim2[:, k, :], start=(k == 0), stop=(k == CB - 1))
                m.then_inc(s_pe, 1)
                pe.wait_ge(s_rm, 1)
                for g in range(HQ):
                    m = pe.matmul(p_rm[g * E0:(g + 1) * E0, 0:B], t["rm"], ident[0:B, 0:B], start=True, stop=True)
                m.then_inc(s_pe, 1)
                pe.wait_ge(s_rb, 1)
                pe.wait_ge(s_wv, 16 * HQ)
                for r in range(HR):
                    if r >= 4 and r % 2 == 0:
                        pe.wait_ge(s_wd, r - 2)
                    for k in range(CB):
                        m = pe.matmul(p_w[r // 2 % 2][:, 4 * (r % 2) + k, :], WV[:, r, k * P:(k + 1) * P], RB, start=True, stop=True)
                    if r % 2:
                        m.then_inc(s_wp, 1)
                for r in range(HR):
                    pe.wait_ge(s_wo[r // 8], 16 * HQ)
                    if r >= 2:
                        pe.wait_ge(s_wa, r - 1)
                    pe.matmul(p_w[2 + r % 2][0:HQ * B].rearrange("p a b -> p (a b)"), RB, WV[:, r, :],
                              start=True, stop=True).then_inc(s_wp2, 1)

        era2.close()

        with ExitStack() as st:
            wc = [sb(st, f"wc{i}", [P, CB, EH]) for i in range(2)]
            wo = [sb(st, f"wo{i}", [EH, C]) for i in range(2)]
            cb = [sb(st, f"cb{i}", [EH, T]) for i in range(2)]
            q, qh, ql = ([sb(st, f"{n}{i}", [P, TH, C]) for i in range(2)] for n in ("q5_", "qh5_", "ql5_"))
            stats = sb(st, "stats5", [P, TH, 6])
            mv = [sb(st, f"mv5{i}", [P, TH, 2]) for i in range(2)]
            std = [sb(st, f"std5{i}", [P, TH]) for i in range(2)]
            work = [sb(st, f"work5_{i}", [P, TH]) for i in range(2)]
            rstd = [sb(st, f"rstd5_{i}", [P, TH]) for i in range(2)]
            pc = [pb(st, f"pc{i}", [EH, C]) for i in range(2)]
            py = [pb(st, f"py{i}", [P, TH, C]) for i in range(2)]
            s_w = [sem(f"s_w5{i}", st) for i in range(2)]
            s_st = [sem(f"s_st5{i}", st) for i in range(2)]
            s_wc, s_pc, s_cb, s_py, s_x2, s_mv, s_std, s_q, s_qh, s_dve, s_ql = [sem(n + "_5", st) for n in (
                "s_wc", "s_pc", "s_cb", "s_py", "s_x2", "s_mv", "s_std", "s_q", "s_qh", "s_dve", "s_ql")]
            block = st.enter_context(nc.Block())

            @block.sync
            def _(sp):
                def load(b, u, i):
                    sp.wait_ge(s_py, b + 1)
                    sp.dma_start(wo[u], WO[b]).then_inc(s_w[u], 16)

                def store(b, u, i):
                    sp.wait_ge(s_ql, b + 3)
                    for part, to in ((qh, QH), (ql, QL)):
                        sp.dma_start(to[b].rearrange("(th p) c -> p th c", p=P), part[u]).then_inc(s_st[u], 16)

                def step(k):
                    both(k(2), load)
                    both(k(), store)

                pipelined(sp, B, 2, step)
                for u in range(2):
                    sp.wait_ge(s_st[u], 32 + 32 * B // 2)

            @block.gpsimd
            def _(pool):
                pool.sem_inc(s_st[0], 32)
                pool.sem_inc(s_st[1], 32)
                pool.sem_inc(s_ql, 2)

                def low(b, u, i):
                    pool.wait_ge(s_qh, b + 1)
                    pool.wait_ge(s_st[u], 32 * i + 32)
                    pool.tensor_tensor(ql[u].bitcast(F32R), q[u], qh[u], ALU.subtract).then_inc(s_ql, 1)

                pipelined(pool, B, 0, lambda k: both(k(), low))

            @block.tensor
            def _(pe):
                pe.sem_inc(s_pc, 2)
                pe.sem_inc(s_py, 2)

                def inner(b, u, i):
                    pe.wait_ge(s_wc, b + 1)
                    pe.wait_ge(s_cb, b + 1)
                    for k in range(CB):
                        m = pe.matmul(pc[u][:, 0:T].rearrange("p (h j) -> p h j", j=HD0), wc[u][:, k, :], columns_of(b, k),
                                      start=(k == 0), stop=(k == CB - 1))
                    m.then_inc(s_pc, 1)

                def outer(b, u, i):
                    pe.wait_ge(s_cb, b + 3)
                    pe.wait_ge(s_w[u], 16 * i + 16)
                    pe.wait_ge(s_x2, b + 1)
                    for th in range(TH):
                        m = pe.matmul(py[u][:, th, :], cb[u][:, th * P:(th + 1) * P], wo[u], start=True, stop=True)
                    m.then_inc(s_py, 1)

                def step(k):
                    both(k(1), outer)
                    both(k(2), inner)

                pipelined(pe, B, 2, step)

            @block.vector
            def _(dve):
                chain = Chain(s_dve, dve)
                dve.sem_inc(s_x2, 2)

                def copy(b, u, i):
                    dve.wait_ge(s_pc, b + 1)
                    dve.tensor_copy(wc[u].rearrange("p k h -> p (k h)"), ap(WM, b * (CB * EH), [[1, CB * EH]])).then_inc(s_wc, 1)

                def add(b, u, i):
                    dve.wait_ge(s_py, b + 3)
                    for th, row in enumerate(x_rows(b)):
                        chain.inc(dve.scalar_tensor_tensor(row, py[u][:, th, :], gates[:, 2:3], row, ALU.mult, ALU.add))
                    chain.wait()
                    dve.sem_inc(s_x2, 1)
                    layer_stats(dve, chain, x_rows(b), stats, mv[u])
                    dve.sem_inc(s_mv, 1)

                def norm(b, u, i):
                    dve.wait_ge(s_std, b + 1)
                    dve.wait_ge(s_ql, b + 1)
                    layer_scale(dve, chain, mv[u][:, :, 1], std[u], work[u], rstd[u])
                    chain.restart()
                    for th, row in enumerate(x_rows(b)):
                        n = dve.tensor_scalar(q[u][:, th, :], row, mv[u][:, th, 0:1], rstd[u][:, th:th + 1],
                                              ALU.subtract, ALU.mult)
                    n.then_inc(s_q, 1)

                def step(k):
                    both(k(3), copy)
                    both(k(1), add)
                    both(k(), norm)

                pipelined(dve, B, 4, step)

            @block.scalar
            def _(act):
                act.sem_inc(s_cb, 2)

                def hidden(b, u, i):
                    act.wait_ge(s_pc, b + 3)
                    act.wait_ge(s_py, b + 1)
                    act.activation(cb[u], pc[u][:, 0:T], ACT.Copy).then_inc(s_cb, 1)

                def root(b, u, i):
                    act.wait_ge(s_mv, b + 1)
                    act.activation(std[u], mv[u][:, :, 1], ACT.Sqrt, bias=eps).then_inc(s_std, 1)

                def high(b, u, i):
                    act.wait_ge(s_q, b + 1)
                    act.wait_ge(s_st[u], 32 * i + 32)
                    act.activation(qh[u].bitcast(F32R), q[u], ACT.Copy).then_inc(s_qh, 1)

                def step(k):
                    both(k(2), hidden)
                    both(k(1), root)
                    both(k(), high)

                pipelined(act, B, 2, step)

    X3 = out["out"][0:B * T].rearrange("(u p) c -> u p c", p=P)
    stats6 = sb(whole, "stats6", [P, UNITS, 6])
    with ExitStack() as st:
        qs = [sb(st, f"qs{i}", [P, NH, C]) for i in range(4)]
        ks = [sb(st, f"ks{i}", [P, NH, C]) for i in range(4)]
        vt = [sb(st, f"vt{i}", [P, CB, P]) for i in range(4)]
        pt = [sb(st, f"pt{i}", [P, NH, C]) for i in range(2)]
        lns = sb(st, "lns", [P, C])
        inv = sb(st, "inv", [P, C])
        att = sb(st, "att", [P, C])
        corr = sb(st, "corr", [P, C])
        minus_gate = sb(st, "minus_gate", [P, 1])
        mx = sb(st, "mx", [P, CB, NH])
        mh = sb(st, "mh", [NH, C])
        ml = sb(st, "ml", [NH, C])
        ones = sb(st, "ones6", [P, HD1])
        BANKS = 3
        pA = [pb(st, f"pA{i}", [P, C]) for i in range(BANKS)]
        pB = [pb(st, f"pB{i}", [P, C]) for i in range(2)]
        pV = [pb(st, f"pV{i}", [P, C]) for i in range(2)]
        pS = pb(st, "pS", [P, C])
        s_ld = [sem(f"s_ld{i}", st) for i in range(4)]
        s_v = [sem(f"s_v{i}", st) for i in range(4)]
        (s_rep, s_a, s_red, s_mt, s_mh, s_md, s_b, s_exp, s_av, s_x3, s_c, s_dve, s_act, s_dn, s_pool, s_go, s_st) = [
            sem(n + "_6", st) for n in ("s_rep", "s_a", "s_red", "s_mt", "s_mh", "s_md", "s_b", "s_exp",
                                        "s_av", "s_x3", "s_c", "s_dve", "s_act", "s_dn", "s_pool", "s_go", "s_st")]
        block = st.enter_context(nc.Block())
        TRIP = 4
        NS = 3 * HD1
        TILES = NH * CB
        RING = TILES + 1
        units = lambda d: d.rearrange("b (g h d) c -> (b g) d h c", g=TH, h=NH)
        KHu, KLu, QHu, QLu = units(KH), units(KL), units(QH), units(QL)

        def unit_loop(eng, body):
            trips = UNITS // TRIP
            for u in range(TRIP):
                body(u, 0, u)
            with eng.Fori(1, trips - 1) as i:
                for u in range(TRIP):
                    body(i * TRIP + u, i, u)
            for u in range(TRIP):
                body(UNITS - TRIP + u, trips - 1, u)

        def bank(u, t):
            return pA[(u * RING + t) % BANKS]

        def last_use(j, u, t):
            return RING * j + t + 1 + (BANKS - (2 if u * RING + t < 2 else BANKS))

        def exists(j):
            return not isinstance(j, int) or 0 <= j < UNITS

        SPREAD = ((2, 3), (2, 2), (0, 1), (3, 3))
        EARLY = sum(sum(n) for n in SPREAD[2:])

        def ahead(j, u, s, part):
            n = 1 if s < 2 else 2
            t0 = sum(sum(m) for m in SPREAD[2 if s >= 2 else 0:s]) + sum(SPREAD[s][:part]) + (0 if s >= 2 else EARLY)
            return [(j + n, (u + n) % TRIP, t0 + w) for w in range(SPREAD[s][part])] if exists(j + n) else []

        @block.sync
        def _(sp):
            def load(j, u):
                for dst, src in ((ks[u][0:HD1], KHu[j]), (ks[u][HD1:2 * HD1], KLu[j]),
                                 (qs[u][0:HD1], QHu[j]), (qs[u][HD1:2 * HD1], QHu[j]), (qs[u][2 * HD1:NS], QLu[j])):
                    sp.dma_start(dst, src).then_inc(s_ld[u], 16)

            def load_values(j, u):
                sp.dma_start(vt[u], a["v_t"][j]).then_inc(s_v[u], 16)

            def store(j):
                sp.wait_ge(s_x3, j + 1)
                sp.dma_start(X3[j], ap(XN, j * ROW, [[1, C]])).then_inc(s_st, 16)

            def shift(j, u):
                sp.wait_ge(s_mh, j + 1)
                for row, part in enumerate((mh, ml)):
                    sp.dma_start(qs[u][NS + row:NS + row + 1], bass.AP(part.tensor, part.offset, [list(part.ap[0]), [C, 1], [1, C]])).then_inc(s_md, 16)

            def body(j, i, u):
                before, n = exists(j - 1), (u + TRIP - 1) % TRIP
                if before and exists(j + 3):
                    sp.wait_ge(s_b, TILES * j)
                if exists(j + 3):
                    load(j + 3, n)
                if exists(j + 1):
                    shift(j + 1, (u + 1) % TRIP)
                if before:
                    store(j - 1)
                if exists(j + 3):
                    load_values(j + 3, n)

            for u in range(3):
                load(u, u)
                load_values(u, u)
            shift(0, 0)
            unit_loop(sp, body)
            store(UNITS - 1)
            sp.wait_ge(s_st, 16 * UNITS)

        @block.gpsimd
        def _(pool):
            chain = Chain(s_pool, pool)
            chain.link(pool.memset(ones, 1.0))
            for u in range(4):
                chain.link(pool.memset(ks[u][NS:P], 1.0))
            chain.restart()
            pool.sem_inc(s_c, 1)
            with pool.Fori(0, UNITS // TRIP) as i:
                for u in range(TRIP):
                    pool.wait_ge(s_ld[u], i * 80 + 80)
                    pool.sem_inc(s_go, 1)
                    chain.link(pool.tensor_copy(ks[u][2 * HD1:NS].bitcast(F32R), ks[u][0:HD1]))
                    chain.restart()
                    pool.sem_inc(s_rep, 1)

        @block.tensor
        def _(pe):
            pe.sem_inc(s_red, BANKS)
            pe.sem_inc(s_exp, 2)
            pe.sem_inc(s_dn, 2)
            pe.wait_ge(s_c, 1)

            def first(tiles):
                for j, u, t in tiles:
                    if t == 0:
                        pe.wait_ge(s_rep, j + 1)
                    pe.wait_ge(s_red, last_use(j, u, t))
                    h, m0 = t // CB, t % CB * P
                    pe.matmul(bank(u, t), qs[u][0:NS, h, m0:m0 + P].bitcast(F32R), ks[u][0:NS, h, :].bitcast(F32R),
                              start=True, stop=True).then_inc(s_a, 1)

            def maxima(j, u):
                rows = bank(u, TILES)
                pe.wait_ge(s_red, RING * j + TILES + BANKS)
                for k in range(CB):
                    t = pe.transpose(rows[0:NH, k * P:(k + 1) * P], mx[:, k, :], ident)
                t.then_inc(s_mt, 1)

            def second(j, u, s, part, tiles):
                if s == 0 and part == 0:
                    pe.wait_ge(s_md, 32 * j + 32)
                for h in (2 * part, 2 * part + 1):
                    pe.wait_ge(s_exp, TILES * j + NH * s + h + 1)
                    pe.matmul(pB[h % 2], ks[u][0:NS + 2, h, s * P:(s + 1) * P].bitcast(F32R), qs[u][0:NS + 2, h, :].bitcast(F32R),
                              start=True, stop=True).then_inc(s_b, 1)
                    first(tiles[h % 2:h % 2 + 1])

            def values(j, i, u, s):
                if s == 0:
                    pe.wait_ge(s_v[u], i * 16 + 16)
                    pe.wait_ge(s_dn, j + 1)
                pe.wait_ge(s_exp, TILES * j + NH * s + NH + 2)
                for h in range(NH):
                    pe.matmul(pV[u % 2][h * HD1:(h + 1) * HD1, :], vt[u][:, s, h * HD1:(h + 1) * HD1], pt[s % 2][:, h, :],
                              start=(s == 0), stop=(s == CB - 1))

            def sums(j, u, s):
                if s == 0:
                    pe.wait_ge(s_dn, j + 2)
                for h in range(NH):
                    m = pe.matmul(pS[h * HD1:(h + 1) * HD1, :], ones, pt[s % 2][:, h, :], start=(s == 0), stop=(s == CB - 1))
                m.then_inc(s_av, 1)

            def body(j, i, u):
                for s in range(CB):
                    last = (j, i, u, s - 1) if s else (j - 1, i if u else i - 1, (u + TRIP - 1) % TRIP, CB - 1)
                    for part in range(2):
                        tiles = ahead(j, u, s, part)
                        late = 0 if (s, part) == (2, 1) else 2
                        second(j, u, s, part, tiles[:late])
                        if exists(last[0]):
                            if part == 0:
                                values(*last)
                            else:
                                sums(last[0], *last[2:])
                        if (s, part) == (2, 0) and exists(j + 1):
                            maxima(j + 1, (u + 1) % TRIP)
                        first(tiles[late:])

            first([(0, 0, t) for t in range(TILES)])
            maxima(0, 0)
            first([(1, 1, t) for t in range(EARLY)])
            unit_loop(pe, body)
            values(UNITS - 1, UNITS // TRIP - 1, TRIP - 1, CB - 1)
            sums(UNITS - 1, TRIP - 1, CB - 1)

        @block.scalar
        def _(act):
            act.sem_inc(s_av, 2)
            act.preload_act_table_set("natural_log_exp_and_others")

            def inverse(j, u):
                act.wait_ge(s_av, 4 * j + 6)
                act.activation(lns, pS, ACT.Ln).then_inc(s_act, 1)
                act.wait_ge(s_act, 2 * j + 1)
                act.wait_ge(s_dn, j + 2)
                act.activation(inv, lns, ACT.Exp, scale=-1.0).then_inc(s_act, 1)

            def body(j, i, u):
                for s in range(CB):
                    act.wait_ge(s_av, 4 * j + s + 1)
                    for h in range(NH):
                        act.wait_ge(s_b, TILES * j + NH * s + h + 1)
                        act.activation(pt[s % 2][:, h, :], pB[h % 2], ACT.Exp, scale=SCALE1).then_inc(s_exp, 1)
                    if s == 0 and exists(j - 1):
                        inverse(j - 1, (u + TRIP - 1) % TRIP)

            unit_loop(act, body)
            inverse(UNITS - 1, TRIP - 1)

        @block.vector
        def _(dve):
            chain = Chain(s_dve, dve)

            def reduce(tiles):
                for j, u, t in tiles:
                    dve.wait_ge(s_a, TILES * j + t + 1)
                    dve.tensor_reduce(mx[:, t % CB, t // CB:t // CB + 1], bank(u, t), op=ALU.max, axis=AX.X).then_inc(s_red, 1)

            def shift(j, u):
                dve.wait_ge(s_mt, j + 1)
                if exists(j - 1):
                    dve.wait_ge(s_md, 32 * j)
                rows = bank(u, TILES)[0:NH, :]
                chain.link(dve.tensor_scalar(mh.bitcast(F32R), rows, -1.0, None, ALU.mult))
                chain.link(dve.scalar_tensor_tensor(ml.bitcast(F32R), rows, -1.0, mh, ALU.mult, ALU.subtract))
                chain.restart()
                dve.sem_inc(s_red, 1)
                dve.sem_inc(s_mh, 1)

            def release(j, u):
                dve.wait_ge(s_act, 2 * j + 2)
                chain.inc(dve.tensor_tensor(corr, pS, inv, ALU.mult))
                chain.link(dve.tensor_tensor(att, pV[u % 2], inv, ALU.mult))
                dve.sem_inc(s_dn, 1)

            def norm():
                chain.inc(dve.scalar_tensor_tensor(att, corr, 2.0, att, ALU.subtract, ALU.mult))

            def add(j, i, u):
                chain.wait()
                row = ap(XN, j * ROW, [[1, C]])
                chain.link(dve.scalar_tensor_tensor(row, att, minus_gate, row, ALU.mult, ALU.add))
                dve.sem_inc(s_x3, 1)
                chain.inc(dve.bn_stats(ap(stats6, j * 6, [[1, 6]]), row))
                chain.restart()

            def body(j, i, u):
                before = (j - 1, i if u else i - 1, (u + TRIP - 1) % TRIP)
                for s in range(CB):
                    if s == CB // 2 and exists(j + 1):
                        shift(j + 1, (u + 1) % TRIP)
                    reduce(ahead(j, u, s, 0))
                    if s == 1 and exists(j - 1):
                        release(before[0], before[2])
                    if s == 1 and exists(j - 1):
                        t = ahead(j, u, s, 1)
                        reduce(t[:1])
                        norm()
                        reduce(t[1:])
                        add(*before)
                    else:
                        reduce(ahead(j, u, s, 1))

            chain.link(dve.tensor_scalar(minus_gate, gates[:, 1:2], -1.0, None, ALU.mult))
            reduce([(0, 0, t) for t in range(TILES)])
            shift(0, 0)
            reduce([(1, 1, t) for t in range(EARLY)])
            unit_loop(dve, body)
            release(UNITS - 1, TRIP - 1)
            norm()
            add(UNITS - 1, UNITS // TRIP - 1, TRIP - 1)

    with ExitStack() as era3:
        WF = sb(era3, "WF", [P, E1, CB, C])
        WP = sb(era3, "WP", [P, E1, CB, C])
        TE = sb(era3, "TE", [P, TILES9])
        TEi = sb(era3, "TEi", [1, TILES9], I32)
        s_wf = sem("s_wf", era3)
        s_wp = sem("s_wp9", era3)
        with ExitStack() as era4:
            LG = sb(era4, "LG", [P, UNITS, E1])
            with ExitStack() as st:
                xT = [sb(st, f"xT{i}", [P, CB, P]) for i in range(2)]
                wr = sb(st, "wr", [P, CB, E1])
                xs = [sb(st, f"xn{i}", [P, C]) for i in range(2)]
                mv = sb(st, "mv7", [P, UNITS, 2])
                std = sb(st, "std7", [P, UNITS])
                work = sb(st, "work7", [P, UNITS])
                rstd = sb(st, "rstd7", [P, UNITS])
                zero = sb(st, "zero7", [P, C])
                pT = [pb(st, f"pT{i}", [P, CB, P]) for i in range(2)]
                pL = [pb(st, f"pL{i}", [P, C]) for i in range(2)]
                s_wr, s_mv, s_std, s_xn, s_t, s_ev, s_l, s_lg, s_dve, s_z, s_junk, s_cp = [sem(n + "_7", st) for n in (
                    "s_wr", "s_mv", "s_std", "s_xn", "s_t", "s_ev", "s_l", "s_lg", "s_dve", "s_z", "s_junk", "s_cp")]
                block = st.enter_context(nc.Block())

                @block.sync
                def _(sp):
                    sp.dma_start(wr, a["w_router"].rearrange("(k p) e -> p k e", p=P)).then_inc(s_wr, 16)
                    for e in range(E1):
                        sp.dma_start(WF[:, e], a["w_fc"][e].rearrange("(k p) d -> p k d", p=P)).then_inc(s_wf, 16)
                    for e in range(E1):
                        sp.dma_start(WP[:, e], a["w_proj"][e].rearrange("(k p) c -> p k c", p=P)).then_inc(s_wp, 16)
                    sp.wait_ge(s_z, 1)
                    sp.dma_start(out["out"][B * T:], zero).then_inc(s_junk, 16)
                    sp.wait_ge(s_junk, 16)

                @block.gpsimd
                def _(pool):
                    pool.memset(zero, 0.0).then_inc(s_z, 1)

                @block.vector
                def _(dve):
                    chain = Chain(s_dve, dve)
                    for j in range(UNITS):
                        chain.inc(dve.bn_aggr(mv[:, j, :], stats6[:, j, :]))
                    chain.restart()
                    dve.sem_inc(s_mv, 1)
                    dve.wait_ge(s_std, 1)
                    layer_scale(dve, chain, mv[:, :, 1], std, work, rstd)
                    chain.restart()

                    def scale(j, u):
                        dve.wait_ge(s_t, j + 1)
                        dve.wait_ge(s_cp, j + 1)
                        dve.tensor_scalar(xs[u], ap(XN, j * ROW, [[1, C]]), ap(mv, 2 * j, [[1, 1]]), ap(rstd, j, [[1, 1]]),
                                          ALU.subtract, ALU.mult).then_inc(s_xn, 1)

                    def columns(j, u):
                        dve.wait_ge(s_t, j + 3)
                        dve.wait_ge(s_l, j + 1)
                        dve.tensor_copy(xT[u], pT[u]).then_inc(s_ev, 1)

                    scale(0, 0)
                    scale(1, 1)
                    with dve.Fori(0, UNITS // 2 - 1) as i:
                        for u in range(2):
                            columns(2 * i + u, u)
                            scale(2 * i + u + 2, u)
                    columns(UNITS - 2, 0)
                    columns(UNITS - 1, 1)

                @block.scalar
                def _(act):
                    act.wait_ge(s_mv, 1)
                    act.activation(std, mv[:, :, 1], ACT.Sqrt, bias=eps).then_inc(s_std, 1)

                    def keep(j, u):
                        act.wait_ge(s_xn, j + 1)
                        act.activation(ap(XN, j * ROW, [[1, C]]), xs[u], ACT.Copy).then_inc(s_cp, 1)

                    def logits(j, u):
                        act.wait_ge(s_l, j + 3)
                        act.activation(ap(LG, j * E1, [[1, E1]]), pL[u][:, 0:E1], ACT.Copy).then_inc(s_lg, 1)

                    keep(0, 0)
                    with act.Fori(0, UNITS // 2 - 1) as i:
                        for u in range(2):
                            keep(2 * i + u + 1, 1 - u)
                            logits(2 * i + u, u)
                    keep(UNITS - 1, 1)
                    logits(UNITS - 2, 0)
                    logits(UNITS - 1, 1)

                @block.tensor
                def _(pe):
                    for s in (s_t, s_cp, s_l, s_ev, s_lg):
                        pe.sem_inc(s, 2)
                    pe.wait_ge(s_wr, 16)

                    def turn(j, u):
                        pe.wait_ge(s_xn, j + 1)
                        pe.wait_ge(s_ev, j + 1)
                        for k in range(CB):
                            t = pe.transpose(pT[u][:, k, :], xs[u][:, k * P:(k + 1) * P], ident)
                        t.then_inc(s_t, 1)

                    def route(j, u):
                        pe.wait_ge(s_ev, j + 3)
                        pe.wait_ge(s_lg, j + 1)
                        for k in range(CB):
                            m = pe.matmul(pL[u][:, 0:E1], xT[u][:, k, :], wr[:, k, :], start=(k == 0), stop=(k == CB - 1))
                        m.then_inc(s_l, 1)

                    turn(0, 0)
                    with pe.Fori(0, UNITS // 2 - 1) as i:
                        for u in range(2):
                            turn(2 * i + u + 1, 1 - u)
                            route(2 * i + u, u)
                    turn(UNITS - 1, 1)
                    route(UNITS - 2, 0)
                    route(UNITS - 1, 1)

            with ExitStack() as st:
                A = [sb(st, f"A8{i}", [P, UNITS, E1]) for i in range(5)]
                over = sb(st, "over8", [P, UNITS // 2, E1, E1])
                V = {n: sb(st, n + "_8", [P, UNITS]) for n in ("v1", "v2", "s1", "s2", "e2")}
                later = sb(st, "later8", [P, E1, E1])
                before = sb(st, "before8", [P, P])
                ones = sb(st, "ones8", [P, P])
                number = sb(st, "number8", [P, TILES9 + UNITS])
                numi = sb(st, "numi8", [P, TILES9 + UNITS], I32)
                N8 = {n: sb(st, n + "_8", [P, E1]) for n in ("n", "nt", "end", "x")}
                Ni = sb(st, "Ni8", [P, E1], I32)
                slot = [sb(st, f"slot8{i}", [P, UNITS], U32) for i in range(2)]
                pP = pb(st, "pP", [P, UNITS, E1])
                pN = pb(st, "pN", [P, UNITS, E1])
                s_c, s_mask, s_pre, s_d, s_e, s_dve, s_slot, s_sc, s_v = [sem(n + "_8", st) for n in (
                    "s_c", "s_mask", "s_pre", "s_d", "s_e", "s_dve", "s_slot", "s_sc", "s_v")]
                block = st.enter_context(nc.Block())

                @block.gpsimd
                def _(pool):
                    chain = Chain(s_c, pool)
                    chain.link(pool.memset(later, 1.0))
                    chain.link(pool.memset(before, 1.0))
                    chain.link(pool.memset(ones, 1.0))
                    chain.link(pool.affine_select(out=later, in_=later, compare_op=ALU.is_gt, fill=0.0, base=0,
                                                  pattern=[[1, E1], [-1, E1]], channel_multiplier=0))
                    chain.link(pool.affine_select(out=before, in_=before, compare_op=ALU.is_gt, fill=0.0, base=0,
                                                  pattern=[[1, P]], channel_multiplier=-1))
                    chain.link(pool.iota(numi[:, 0:TILES9], [[1, TILES9]], base=0, channel_multiplier=0))
                    chain.link(pool.iota(numi[:, TILES9:], [[P, UNITS]], base=0, channel_multiplier=1))
                    pool.wait_ge(s_slot, 1)
                    for j in range(UNITS):
                        for w in range(2):
                            pool.indirect_dma_start(
                                out=XS, out_offset=bass.IndirectOffsetOnAxis(ap=slot[w][:, j:j + 1], axis=0),
                                in_=XN[:, j, :], in_offset=None).then_inc(s_sc, 16)
                    pool.wait_ge(s_sc, 16 * 2 * UNITS)

                @block.scalar
                def _(act):
                    act.wait_ge(s_d, 1)
                    act.activation(V["e2"], V["s1"], ACT.Exp).then_inc(s_e, 1)

                @block.tensor
                def _(pe):
                    pe.wait_ge(s_mask, 1)
                    pe.matmul(pP.rearrange("p u e -> p (u e)"), before, A[2].rearrange("p u e -> p (u e)"), start=True, stop=True)
                    pe.matmul(pN.rearrange("p u e -> p (u e)"), ones, A[2].rearrange("p u e -> p (u e)"), start=True, stop=True
                              ).then_inc(s_pre, 1)

                @block.vector
                def _(dve):
                    chain = Chain(s_dve, dve)
                    link, inc = chain.link, chain.inc
                    best, second, both, t0, t1 = A
                    n = UNITS // 2
                    for half in range(2):
                        mine = ap(LG, half * n * E1, [[E1, n], [1, E1], [0, E1]])
                        other = ap(LG, half * n * E1, [[E1, n], [0, E1], [1, E1]])
                        rank, equal = (t[:, half * n:(half + 1) * n] for t in (t0, t1))
                        link(dve.tensor_tensor(over, other, mine, ALU.is_gt))
                        link(dve.tensor_reduce(rank, over, op=ALU.add, axis=AX.X))
                        link(dve.tensor_tensor(over, other, mine, ALU.is_equal))
                        if half == 0:
                            dve.wait_ge(s_c, 7)
                        link(dve.tensor_tensor(over, over, ap(later, 0, [[0, n], [E1, E1], [1, E1]]), ALU.mult))
                        link(dve.tensor_reduce(equal, over, op=ALU.add, axis=AX.X))
                        link(dve.tensor_tensor(rank, rank, equal, ALU.add))
                    inc(dve.tensor_scalar(best, t0, 0.0, None, ALU.is_equal))
                    inc(dve.tensor_scalar(second, t0, 1.0, None, ALU.is_equal))
                    link(dve.tensor_scalar(both, t0, 1.0, None, ALU.is_le))
                    dve.sem_inc(s_mask, 1)

                    def pick(out_, which, of):
                        link(dve.tensor_tensor(t1, which, of, ALU.mult))
                        link(dve.tensor_reduce(out_, t1, op=ALU.add, axis=AX.X))

                    pick(V["v1"], best, LG)
                    pick(V["v2"], second, LG)
                    link(dve.tensor_tensor(V["s1"], V["v2"], V["v1"], ALU.subtract))
                    dve.sem_inc(s_d, 1)
                    inc(dve.tensor_copy(number, numi))
                    dve.wait_ge(s_e, 1)
                    link(dve.tensor_scalar(V["v1"], V["e2"], 1.0, None, ALU.add))
                    link(dve.reciprocal(V["v1"], V["v1"]))
                    link(dve.tensor_scalar(V["v1"], V["v1"], gates[:, 3:4], None, ALU.mult))
                    inc(dve.tensor_copy(XN[:, :, C + 1], V["v1"]))
                    inc(dve.tensor_tensor(XN[:, :, C + 2], V["v1"], V["e2"], ALU.mult))
                    inc(dve.tensor_copy(XN[:, :, C], number[:, TILES9:]))
                    pick(XN[:, :, C + 3], best, ap(number, 0, [[0, UNITS], [1, E1]]))
                    dve.wait_ge(s_pre, 1)
                    link(dve.tensor_copy(t0, pN))
                    cur, nxt, step = t0, t1, 1
                    while step < UNITS:
                        inc(dve.tensor_copy(nxt[:, 0:step], cur[:, 0:step]))
                        link(dve.tensor_tensor(nxt[:, step:], cur[:, step:], cur[:, 0:UNITS - step], ALU.add))
                        cur, nxt, step = nxt, cur, 2 * step
                    link(dve.tensor_copy(N8["n"], cur[:, UNITS - 1, :]))
                    link(dve.tensor_scalar(Ni, N8["n"], float(P - 1), None, ALU.add))
                    link(dve.tensor_scalar(Ni, Ni, 7, None, ALU.arith_shift_right))
                    link(dve.tensor_copy(N8["nt"], Ni))
                    a0, a1, step = N8["nt"], N8["end"], 1
                    link(dve.tensor_copy(N8["x"], N8["nt"]))
                    a0 = N8["x"]
                    while step < E1:
                        inc(dve.tensor_copy(a1[:, 0:step], a0[:, 0:step]))
                        link(dve.tensor_tensor(a1[:, step:], a0[:, step:], a0[:, 0:E1 - step], ALU.add))
                        a0, a1, step = a1, a0, 2 * step
                    cmp9 = over.rearrange("p u e f -> p (u e f)")[:, 0:TILES9 * E1].rearrange("p (t e) -> p t e", e=E1)
                    link(dve.tensor_tensor(cmp9, ap(number, 0, [[1, TILES9], [0, E1]]), ap(a0, 0, [[0, TILES9], [1, E1]]), ALU.is_ge))
                    link(dve.tensor_reduce(TE, cmp9, op=ALU.add, axis=AX.X))
                    link(dve.tensor_scalar(TE, TE, float(E1 - 1), None, ALU.min))
                    inc(dve.tensor_scalar(TEi, TE[0:1, :], float(CB * C), None, ALU.mult))
                    link(dve.tensor_tensor(a1, a0, N8["nt"], ALU.subtract))
                    link(dve.tensor_scalar(a1, a1, float(P), None, ALU.mult))
                    link(dve.tensor_tensor(nxt, cur, pN, ALU.subtract))
                    link(dve.tensor_tensor(nxt, nxt, pP, ALU.add))
                    link(dve.tensor_tensor(cur, nxt, ap(a1, 0, [[0, UNITS], [1, E1]]), ALU.add))
                    for w, which in enumerate((best, second)):
                        link(dve.tensor_tensor(nxt, which, cur, ALU.mult))
                        link(dve.tensor_reduce(V["s2"], nxt, op=ALU.add, axis=AX.X))
                        link(dve.tensor_copy(slot[w], V["s2"]))
                    dve.sem_inc(s_slot, 1)

        with ExitStack() as st:
            xs, xT, hr, hT, ys = ([ap(XN, (2 * n + i) * C, [[1, C]]) for i in range(2)] for n in range(5))
            xT, hT = ([t.rearrange("p (k n) -> p k n", n=P) for t in ring] for ring in (xT, hT))
            meta = sb(st, "meta", [P, TILES9, ROW - C])
            wt = [sb(st, f"wt{i}", [P, TILES9]) for i in range(3)]
            idx = [sb(st, f"idx{i}", [P, 1], U32) for i in range(2)]
            pT = [pb(st, f"p9T{i}", [P, CB, P]) for i in range(2)]
            pH = [pb(st, f"pH{i}", [P, C]) for i in range(2)]
            pG = [pb(st, f"pG{i}", [P, CB, P]) for i in range(2)]
            pY = [pb(st, f"pY{i}", [P, C]) for i in range(2)]
            s_x = [sem(f"s_x9{i}", st) for i in range(2)]
            s_t, s_xT, s_h, s_hr, s_g, s_hT, s_y, s_meta, s_ys, s_add, s_dve, s_go = [sem(n + "_9", st) for n in (
                "s_t", "s_xT", "s_h", "s_hr", "s_g", "s_hT", "s_y", "s_meta", "s_ys", "s_add", "s_dve", "s_go")]
            tiles = XS.rearrange("(t p) w -> t p w", p=P)
            block = st.enter_context(nc.Block())

            @block.sync
            def _(sp):
                for u in range(2):
                    sp.dma_start(xs[u], tiles[u][:, 0:C]).then_inc(s_x[u], 16)
                sp.dma_start(meta, XS.rearrange("(t p) w -> p t w", p=P)[:, :, C:]).then_inc(s_meta, 16)
                with sp.Fori(0, TILES9 // 2 - 1) as i:
                    for u in range(2):
                        j = 2 * i + u
                        sp.wait_ge(s_t, j + 1)
                        sp.dma_start(xs[u], tiles[j + 2][:, 0:C]).then_inc(s_x[u], 16)

            @block.tensor
            def _(pe):
                def columns(j, i, u):
                    pe.wait_ge(s_x[u], i * 16 + 16)
                    pe.wait_ge(s_xT, j + 1)
                    for k in range(CB):
                        t = pe.transpose(pT[u][:, k, :], xs[u][:, k * P:(k + 1) * P], ident)
                    t.then_inc(s_t, 1)

                def up(j, u):
                    e = pe.value_load(TEi[0:1, j:j + 1] if isinstance(j, int) else ap(TEi, j, [[1, 1]]), min_val=0, max_val=(E1 - 1) * CB * C)
                    pe.wait_ge(s_xT, j + 3)
                    pe.wait_ge(s_hr, j + 1)
                    for k in range(CB):
                        m = pe.matmul(pH[u], xT[u][:, k, :], ap(WF, e + k * C, [[1, C]]), start=(k == 0), stop=(k == CB - 1))
                    m.then_inc(s_h, 1)

                def turn(j, u):
                    pe.wait_ge(s_hr, j + 3)
                    pe.wait_ge(s_hT, j + 1)
                    for k in range(CB):
                        t = pe.transpose(pG[u][:, k, :], hr[u][:, k * P:(k + 1) * P], ident)
                    t.then_inc(s_g, 1)

                def down(j, u):
                    e = pe.value_load(TEi[0:1, j:j + 1] if isinstance(j, int) else ap(TEi, j, [[1, 1]]), min_val=0, max_val=(E1 - 1) * CB * C)
                    pe.wait_ge(s_hT, j + 3)
                    pe.wait_ge(s_ys, j + 1)
                    for k in range(CB):
                        m = pe.matmul(pY[u], hT[u][:, k, :], ap(WP, e + k * C, [[1, C]]), start=(k == 0), stop=(k == CB - 1))
                    m.then_inc(s_y, 1)

                for s in (s_xT, s_hr, s_hT, s_ys, s_g, s_y):
                    pe.sem_inc(s, 2)
                pe.sem_inc(s_h, 1)
                pe.wait_ge(s_wf, 16 * E1)
                columns(0, 0, 0)
                up(0, 0)
                columns(1, 0, 1)
                turn(0, 0)
                pe.wait_ge(s_wp, 16 * E1)
                with pe.Fori(0, TILES9 // 2 - 1) as i:
                    for u in range(2):
                        j = 2 * i + u
                        up(j + 1, 1 - u)
                        columns(j + 2, i + 1, u)
                        down(j, u)
                        turn(j + 1, 1 - u)
                up(TILES9 - 1, 1)
                down(TILES9 - 2, 0)
                turn(TILES9 - 1, 1)
                down(TILES9 - 1, 1)

            @block.scalar
            def _(act):
                with act.Fori(0, TILES9 // 2) as i:
                    for u in range(2):
                        j = 2 * i + u
                        act.wait_ge(s_h, j + 2)
                        act.wait_ge(s_g, j + 1)
                        act.activation(hr[u], pH[u], ACT.Relu).then_inc(s_hr, 1)
                        act.wait_ge(s_g, j + 3)
                        act.wait_ge(s_y, j + 1)
                        act.activation(hT[u], pG[u], ACT.Square).then_inc(s_hT, 1)

            @block.vector
            def _(dve):
                chain = Chain(s_dve, dve)

                def columns(j, u):
                    dve.wait_ge(s_t, j + 1)
                    dve.wait_ge(s_h, j)
                    dve.tensor_copy(xT[u], pT[u]).then_inc(s_xT, 1)

                def body(j, u):
                    if not isinstance(j, int) or j + 2 < TILES9:
                        columns(j + 2, u)
                    if not isinstance(j, int) or j > 1:
                        dve.wait_ge(s_add, 16 * (j - 1))
                    chain.inc(dve.tensor_copy(idx[u], ap(meta, j * (ROW - C), [[1, 1]])))
                    dve.wait_ge(s_y, j + 3)
                    chain.link(dve.tensor_scalar(ys[u], pY[u], ap(wt[0], j, [[1, 1]]), None, ALU.mult))
                    chain.restart()
                    dve.sem_inc(s_ys, 1)

                for u in range(2):
                    dve.wait_ge(s_t, u + 1)
                    dve.tensor_copy(xT[u], pT[u]).then_inc(s_xT, 1)
                dve.wait_ge(s_meta, 16)
                first, second, best = (meta[:, :, n] for n in (1, 2, 3))
                chain.link(dve.tensor_tensor(wt[0], best, TE, ALU.is_equal))
                chain.inc(dve.tensor_scalar(wt[1], wt[0], -1.0, 1.0, ALU.mult, ALU.add))
                chain.link(dve.tensor_tensor(wt[0], wt[0], first, ALU.mult))
                chain.link(dve.tensor_tensor(wt[2], wt[1], second, ALU.mult))
                chain.link(dve.tensor_tensor(wt[0], wt[0], wt[2], ALU.add))
                chain.restart()
                for u in range(2):
                    body(u, u)
                with dve.Fori(1, TILES9 // 2 - 1) as i:
                    for u in range(2):
                        body(2 * i + u, u)
                for u in range(2):
                    body(TILES9 - 2 + u, u)

            @block.gpsimd
            def _(pool):
                def add(j, u):
                    pool.wait_ge(s_ys, j + 3)
                    if not isinstance(j, int) or j > 0:
                        pool.wait_ge(s_add, 16 * j)
                    pool.sem_inc(s_go, 1)
                    pool.indirect_dma_start(out=out["out"], out_offset=bass.IndirectOffsetOnAxis(ap=idx[u], axis=0),
                                            in_=ys[u], in_offset=None, compute_op=ALU.add).then_inc(s_add, 16)

                for u in range(2):
                    add(u, u)
                with pool.Fori(1, TILES9 // 2) as i:
                    for u in range(2):
                        add(2 * i + u, u)
                pool.wait_ge(s_add, 16 * TILES9)


def kernel(x, ctx_2048, g_xattn, g_ffn, L0_xattn_ssm_kernel, L0_xattn_D, L0_ffn_sim_matrix, L0_ffn_gates,
           L0_ffn_w_q, L0_ffn_w_k, L0_ffn_w_v, L0_ffn_o_weights, L1_ffn_w_router, L1_ffn_w_fc, L1_ffn_w_proj):
    import numpy as _np
    import concourse.bacc as _bacc
    from concourse.bass_utils import run_bass_kernel_spmd as _run

    ctx = _np.asarray(ctx_2048)
    conv = ctx.reshape(HALF, B8, H0, HD0, CB, P)[..., ::-1].transpose(2, 5, 0, 4, 1, 3)
    conv = _np.concatenate([conv, conv[..., :CYC - HD0]], axis=-1)
    laid = {
        "x": x,
        "ctx": ctx,
        "ctx_conv": conv.reshape(H0, P, HALF * CB * B8 * CYC),
        "v_t": ctx.reshape(UNITS, P, CB, P).transpose(0, 3, 2, 1),
        "g": _np.concatenate([_np.asarray(g_xattn), _np.asarray(g_ffn)]),
        "kern_pad": _np.pad(_np.asarray(L0_xattn_ssm_kernel), ((0, 0), (P - 1, 0))),
        "skip": L0_xattn_D,
        "sim": L0_ffn_sim_matrix,
        "eg": L0_ffn_gates,
        "w_v": L0_ffn_w_v,
        "w_o": L0_ffn_o_weights,
        "w_router": L1_ffn_w_router,
        "w_fc": L1_ffn_w_fc,
        "w_proj": L1_ffn_w_proj,
    }
    laid = {name: _np.ascontiguousarray(array) for name, array in laid.items()}
    nc = _bacc.Bacc("TRN2", target_bir_lowering=False, num_devices=1)
    ins = {name: nc.dram_tensor("in_" + name, array.shape, F32, kind="ExternalInput").ap()
           for name, array in laid.items()}
    out = nc.dram_tensor("out_rows", [B * T + P, C], F32, kind="ExternalOutput").ap()
    build(nc, ins, {"out": out})
    r = _run(nc, [{"in_" + name: array for name, array in laid.items()}], core_ids=[0])
    return r.results[0]["out_rows"][:B * T].reshape(B, T, C)
```

```python
import numpy as np
from contextlib import ExitStack
import concourse.bass as bass
from concourse import mybir

F32 = mybir.dt.float32
F32R = mybir.dt.float32r
I32 = mybir.dt.int32
U32 = mybir.dt.uint32
ALU = mybir.AluOpType
ACT = mybir.ActivationFunctionType
AX = mybir.AxisListType

P = 128
B, T, C = 16, 256, 512
TH = T // P
CB = C // P
H0, HD0 = 32, 8
HALF, B8 = 2, B // 2
CYC = 12
NDG = HD0 // 2 + 1
PAIRS = HD0 * (HD0 + 1) // 2
SLOT = NDG + NDG - 1
E0, EH = 32, 64
HQ, HR = 4, EH // 4
NH, HD1 = 4, 32
SCALE1 = float(HD1) ** -0.5
E1 = 8
UNITS = B * TH
TILES9 = 2 * ((2 * UNITS + E1 - 1 + 1) // 2)
ROW = C + 4
FALLBACK = E0 // 2
EPS = 1e-5
FMAX = float(np.finfo(np.float32).max)


def ap(view, offset, dims):
    return bass.AP(view.tensor, view.offset + offset, [list(view.ap[0])] + [list(d) for d in dims])


class Chain:

    def __init__(self, sem, eng):
        self.sem, self.eng, self.n = sem, eng, 0

    def inc(self, instruction):
        instruction.then_inc(self.sem, 1)
        self.n += 1
        return self.n

    def wait(self, count=None):
        self.eng.wait_ge(self.sem, self.n if count is None else count)

    def link(self, instruction):
        self.inc(instruction)
        self.wait()

    def restart(self):
        self.wait()
        self.eng.sem_clear(self.sem)
        self.n = 0


def weave(*lists):
    for n in range(max(map(len, lists))):
        for works in lists:
            if n < len(works):
                works[n]()


def stats_steps(dve, chain, rows, stats, mv, ready=None):
    seen = {}

    def look(n):
        if ready:
            ready(n)
        seen[n] = chain.inc(dve.bn_stats(stats[:, n, :], rows[n]))

    def close(n):
        chain.wait(seen[n])
        chain.inc(dve.bn_aggr(mv[:, n, :], stats[:, n, :]))

    return [lambda n=n, f=f: f(n) for f in (look, close) for n in range(len(rows))]


def scale_steps(dve, chain, var, std, work, rstd, eps=EPS, mean=None, shift=None):
    last = []

    def then(op):
        if last:
            chain.wait(last[-1])
        last.append(chain.inc(op()))

    ops = [
        lambda: dve.reciprocal(rstd, std),
        lambda: dve.scalar_tensor_tensor(work, var, eps, rstd, ALU.add, ALU.mult),
        lambda: dve.tensor_tensor(work, work, rstd, ALU.mult),
        lambda: dve.tensor_scalar(work, work, -0.5, 1.5, ALU.mult, ALU.add),
        lambda: dve.tensor_tensor(rstd, rstd, work, ALU.mult)]
    if mean is not None:
        ops.append(lambda: dve.scalar_tensor_tensor(shift, mean, -1.0, rstd, ALU.mult, ALU.mult))
    return [lambda op=op: then(op) for op in ops]


def pipelined(eng, count, lag, step, tail=0):
    def at(i, u):
        def item(d=0):
            n = 2 * i + u + d
            if isinstance(n, int) and not 0 <= n < count:
                return None
            return n, (u + d) % 2, i + (u + d) // 2
        return item

    start = 1 if tail else 0
    for n in range(-lag, 2 * start):
        step(at(n // 2, n % 2))
    with eng.Fori(start, (count - lag) // 2) as i:
        for u in range(2):
            step(at(i, u))
    for n in range(count - lag, count + tail):
        step(at(n // 2, n % 2))


def run_on(item, *works):
    for work in works if item else ():
        work(*item)


def build(nc, a, out):
    with ExitStack() as whole:
        _build(nc, a, out, whole)


def _build(nc, a, out, whole):
    def sem(name, ctx=whole):
        return ctx.enter_context(nc.semaphore(name))

    def sb(ctx, name, shape, dt=F32):
        return ctx.enter_context(nc.sbuf_tensor(name, shape, dt))[:]

    def pb(ctx, name, shape, dt=F32):
        return ctx.enter_context(nc.psum_tensor(name, shape, dt))[:]

    KP = nc.dram_tensor("kernel_and_skip", [H0, P - 1 + C], F32).ap()
    WO = nc.dram_tensor("mixed_out_weights", [B, EH, C], F32).ap()
    QH = nc.dram_tensor("q_high", [B, T, C], F32).ap()
    QL = nc.dram_tensor("q_low", [B, T, C], F32).ap()
    XS = nc.dram_tensor("experts_rows", [TILES9 * P, ROW], F32).ap()
    KH = nc.dram_tensor("ctx_high", [B, T, C], F32).ap()
    KL = nc.dram_tensor("ctx_low", [B, T, C], F32).ap()

    ident = sb(whole, "ident", [P, P])
    gates = sb(whole, "gates", [P, 4])
    gates_raw = sb(whole, "gates_raw", [P, 4])
    eps = sb(whole, "eps", [P, 1])
    s_ident = sem("s_ident")
    s_eps = sem("s_eps")
    s_gates = sem("s_gates")
    XN = sb(whole, "XN", [P, UNITS, ROW])

    def x_rows(b):
        return [ap(XN, (TH * b + th) * ROW, [[1, C]]) for th in range(TH)]

    with ExitStack() as era1:
        QT = sb(era1, "QT", [P, H0 * HALF * CB * B8 * HD0])
        HSTEP, HALFSTEP, BLKSTEP = HALF * CB * B8 * HD0, CB * B8 * HD0, B8 * HD0

        def columns_of(b, k, blocks=1):
            dims = [[HSTEP, H0], [1, HD0]]
            if blocks > 1:
                dims = [[BLKSTEP, blocks]] + dims
            return ap(QT, (b // B8) * HALFSTEP + (b % B8) * HD0 + k * BLKSTEP, dims)

        with ExitStack() as st:
            qt = [sb(st, f"qt{i}", [P, TH, C]) for i in range(2)]
            stats = sb(st, "stats", [P, TH, 6])
            mv = [sb(st, f"mv{i}", [P, TH, 2]) for i in range(2)]
            std = [sb(st, f"std{i}", [P, TH]) for i in range(2)]
            work = [sb(st, f"work_{i}", [P, TH]) for i in range(2)]
            rstd = [sb(st, f"rstd_{i}", [P, TH]) for i in range(2)]
            shift = [sb(st, f"shift_{i}", [P, TH]) for i in range(2)]
            kp = sb(st, "kp", [H0, P - 1 + C])
            skip = sb(st, "skip", [H0, 1])
            pq = [pb(st, f"pq{i}", [P, CB, T]) for i in range(2)]
            s_x = [sem(f"s_x{i}", st) for i in range(2)]
            s_q, s_tr, s_ev, s_dve, s_mv, s_rs, s_std, s_kp, s_skip, s_kps, s_g = [sem(n, st) for n in (
                "s_q", "s_tr", "s_ev", "s_dve", "s_mv", "s_rs", "s_std", "s_kp", "s_skip", "s_kps", "s_g")]
            block = st.enter_context(nc.Block())

            @block.sync
            def _(sp):
                def load(b, u):
                    sp.dma_start(ap(XN, TH * b * ROW, [[ROW, TH], [1, C]]), a["x"][b].rearrange("(th p) c -> p th c", p=P)).then_inc(s_x[u], 16)

                load(0, 0)
                load(1, 1)
                sp.dma_start(kp, a["kern_pad"]).then_inc(s_kp, 16)
                sp.dma_start(skip, a["skip"].rearrange("(h o) -> h o", o=1)).then_inc(s_kp, 16)
                sp.dma_start(gates_raw, a["g"].partition_broadcast(P)).then_inc(s_g, 16)
                with sp.Fori(1, B // 2) as i:
                    for u in range(2):
                        sp.wait_ge(s_x[u], 16 * i)
                        load(2 * i + u, u)
                sp.wait_ge(s_skip, 1)
                sp.dma_start(KP, kp).then_inc(s_kps, 16)
                sp.wait_ge(s_kps, 16)

            @block.vector
            def _(dve):
                chain = Chain(s_dve, dve)

                def measure(b, u, i):
                    return stats_steps(dve, chain, x_rows(b), stats, mv[u],
                                       lambda th: dve.wait_ge(s_x[u], 16 * i + 16) if th == 0 else None)

                def root(b, u, i):
                    dve.wait_ge(s_std, b + 1)
                    dve.wait_ge(s_q, b + 1)
                    return scale_steps(dve, chain, mv[u][:, :, 1], std[u], work[u], rstd[u], EPS, mv[u][:, :, 0], shift[u])

                def step(k):
                    weave(root(*k()) if k() else [], measure(*k(1)) if k(1) else [])
                    if k() or k(1):
                        chain.restart()
                    if k(1):
                        dve.sem_inc(s_mv, 1)
                    if k():
                        dve.sem_inc(s_rs, 1)

                pipelined(dve, B, 2, step)
                dve.wait_ge(s_kp, 32)
                dve.tensor_tensor(kp[:, P - 1:P], kp[:, P - 1:P], skip, ALU.add).then_inc(s_skip, 1)

            @block.gpsimd
            def _(pool):
                pool.memset(eps, EPS).then_inc(s_eps, 1)
                pool.memset(ident, 0.0).then_inc(s_ident, 1)
                pool.wait_ge(s_ident, 1)
                pool.affine_select(out=ident, in_=ident, compare_op=ALU.not_equal, fill=1.0, base=0,
                                   pattern=[[-1, P]], channel_multiplier=1).then_inc(s_ident, 1)

            @block.scalar
            def _(act):
                act.wait_ge(s_eps, 1)
                act.wait_ge(s_g, 16)
                act.activation(gates, gates_raw, ACT.Tanh).then_inc(s_gates, 1)

                def norm(b, u, i):
                    act.wait_ge(s_rs, b + 1)
                    act.wait_ge(s_tr, b + 1)
                    for th, row in enumerate(x_rows(b)):
                        n = act.activation(qt[u][:, th, :], row, ACT.Identity, scale=rstd[u][:, th:th + 1], bias=shift[u][:, th:th + 1])
                    n.then_inc(s_q, 1)

                def root(b, u, i):
                    act.wait_ge(s_mv, b + 1)
                    act.activation(std[u], mv[u][:, :, 1], ACT.Sqrt, bias=eps).then_inc(s_std, 1)

                def keep(b, u, i):
                    act.wait_ge(s_tr, b + 3)
                    for k in range(CB // 2):
                        e = act.activation(columns_of(b, 2 * k, 2),
                                           pq[u][:, 2 * k:2 * k + 2, :].rearrange("p k (h j) -> p k h j", j=HD0), ACT.Copy)
                    e.then_inc(s_ev, 1)

                def step(k):
                    run_on(k(1), root)
                    run_on(k(), norm)
                    run_on(k(-1), keep)

                pipelined(act, B, 2, step, 1)

            @block.tensor
            def _(pe):
                pe.wait_ge(s_ident, 2)
                pe.sem_inc(s_tr, 2)
                pe.sem_inc(s_q, 2)
                pe.sem_inc(s_ev, 2)
                with pe.Fori(0, B // 2) as i:
                    for u in range(2):
                        b = 2 * i + u
                        pe.wait_ge(s_q, b + 3)
                        pe.wait_ge(s_ev, b + 1)
                        for th in range(TH):
                            for k in range(CB):
                                t = pe.transpose(pq[u][:, k, th * P:(th + 1) * P], qt[u][:, th, k * P:(k + 1) * P], ident)
                        t.then_inc(s_tr, 1)

        with ExitStack() as st:
            toep = [sb(st, f"toep{i}", [P, C]) for i in range(2)]
            kc = [sb(st, f"kc{i}", [P, HALF * CB * B8, CYC]) for i in range(2)]
            kv = [sb(st, f"kv{i}", [P, HALF, CB, B8 * PAIRS]) for i in range(2)]
            qc = [sb(st, f"qc{i}", [P, HALF * CB * B8, 2 * HD0]) for i in range(2)]
            z = [sb(st, f"z{i}", [P, CB * B8, SLOT * HD0]) for i in range(2)]
            y = [pb(st, f"y{i}", [P, CB * B8, 64]) for i in range(2)]
            s_kc = [sem(f"s_kc{i}", st) for i in range(2)]
            s_tp = [sem(f"s_tp{i}", st) for i in range(2)]
            s_kv = sem("s_kv", st)
            s_qc = sem("s_qc", st)
            s_y = sem("s_y", st)
            s_tt = sem("s_tt", st)
            s_pad = sem("s_pad", st)
            s_fill = sem("s_fill", st)
            pad = sb(st, "pad", [P, ROW])
            ct = sb(st, "ct", [P, TH, C])
            kh = sb(st, "kh", [P, TH, C])
            kl = sb(st, "kl", [P, TH, C])
            s_c, s_kh, s_kl, s_ks = [sem(n + "_2", st) for n in ("s_c", "s_kh", "s_kl", "s_ks")]
            padi = sb(st, "padi", [P, 1], I32)
            s_z0 = sem("s_z0", st)
            s_dve = sem("s_dve2", st)
            block = st.enter_context(nc.Block())

            @block.sync
            def _(sp):
                with sp.Fori(0, H0 // 2) as i:
                    sp.wait_ge(s_kl, i + 1)
                    sp.dma_start(ct, a["ctx"].rearrange("b (th p) c -> b p th c", p=P)[i]).then_inc(s_c, 16)
                    for u in range(2):
                        h = 2 * i + u
                        sp.wait_ge(s_kv, 2 * h + 2)
                        sp.dma_start(kc[u].rearrange("p n c -> p (n c)"), a["ctx_conv"][h]).then_inc(s_kc[u], 16)
                        sp.wait_ge(s_y, 2 * h + 2)
                        sp.dma_start(toep[u], bass.AP(KP.tensor, h * (P - 1 + C), [[1, P], [1, C]])).then_inc(s_tp[u], 16)

            @block.gpsimd
            def _(pool):
                for i in range(2):
                    pool.memset(z[i], 0.0).then_inc(s_z0, 1)
                pool.memset(pad, 0.0).then_inc(s_pad, 1)
                pool.iota(padi, [[1, 1]], base=B * T, channel_multiplier=1).then_inc(s_pad, 1)
                pool.sem_inc(s_kv, 4)
                pool.sem_inc(s_kl, 1)
                with pool.Fori(0, H0 // 2) as i:
                    for u in range(2):
                        h = 2 * i + u
                        pool.wait_ge(s_kc[u], i * 16 + 16)
                        pool.wait_ge(s_y, 2 * h + 2)
                        n = HALF * CB * B8
                        D4 = NDG - 1
                        pool.tensor_tensor(ap(kv[u], 0, [[PAIRS, n], [HD0, D4], [1, HD0]]),
                                           ap(kc[u], 0, [[CYC, n], [0, D4], [1, HD0]]),
                                           ap(kc[u], 0, [[CYC, n], [1, D4], [1, HD0]]), ALU.mult).then_inc(s_kv, 1)
                        pool.tensor_tensor(ap(kv[u], D4 * HD0, [[PAIRS, n], [1, HD0 // 2]]),
                                           ap(kc[u], 0, [[CYC, n], [1, HD0 // 2]]),
                                           ap(kc[u], HD0 // 2, [[CYC, n], [1, HD0 // 2]]), ALU.mult).then_inc(s_kv, 1)
                    pool.wait_ge(s_kh, i + 1)
                    pool.wait_ge(s_ks, 32 * i + 32)
                    pool.tensor_tensor(kl.bitcast(F32R), ct, kh, ALU.subtract).then_inc(s_kl, 1)

            @block.scalar
            def _(act):
                act.wait_ge(s_pad, 2)
                act.activation(pad[:, C:C + 1], padi, ACT.Copy).then_inc(s_pad, 1)
                act.wait_ge(s_pad, 3)
                lists = XS.rearrange("(t p) w -> p t w", p=P)
                for n in range(TILES9 - 2 * H0):
                    act.dma_start(lists[:, n, :], pad).then_inc(s_fill, 16)
                act.sem_inc(s_ks, 32)
                with act.Fori(0, H0 // 2) as i:
                    for n in range(4):
                        act.dma_start(XS.rearrange("(t p) w -> t p w", p=P)[TILES9 - 2 * H0 + 4 * i + n], pad
                                      ).then_inc(s_fill, 16)
                    for u in range(2):
                        h = 2 * i + u
                        act.wait_ge(s_tt, 6 * h + 6)
                        n = HALF * CB * B8
                        act.activation(qc[u].rearrange("p n (r j) -> p n r j", r=2),
                                       ap(QT, h * HSTEP, [[HD0, n], [0, 2], [1, HD0]]), ACT.Copy).then_inc(s_qc, 1)
                        if u == 0:
                            act.wait_ge(s_c, 16 * i + 16)
                            act.wait_ge(s_ks, 32 * i + 32)
                            act.activation(kh.bitcast(F32R), ct, ACT.Copy).then_inc(s_kh, 1)
                    act.wait_ge(s_kl, i + 2)
                    for part, to in ((kh, KH), (kl, KL)):
                        act.dma_start(to.rearrange("b (th p) c -> b p th c", p=P)[i], part).then_inc(s_ks, 16)
                act.wait_ge(s_ks, 32 * B + 32)
                act.wait_ge(s_fill, 16 * TILES9)

            @block.tensor
            def _(pe):
                pe.sem_inc(s_y, 4)
                pe.sem_inc(s_tt, 12)
                with pe.Fori(0, H0 // 2) as i:
                    for u in range(2):
                        h = 2 * i + u
                        pe.wait_ge(s_tp[u], i * 16 + 16)
                        pe.wait_ge(s_kv, 2 * h + 6)
                        for half in range(HALF):
                            pe.wait_ge(s_tt, 6 * h + 3 * half + 9)
                            for l in range(CB):
                                for s in range(l + 1):
                                    m = pe.matmul(y[half].rearrange("p (l n) c -> p l n c", l=CB)[:, l, :, 0:PAIRS],
                                                  toep[u][:, (l - s) * P:(l - s + 1) * P],
                                                  kv[u][:, half, s, :].rearrange("p (n c) -> p n c", c=PAIRS),
                                                  start=(s == 0), stop=(s == l))
                            m.then_inc(s_y, 1)

            @block.vector
            def _(dve):
                chain = Chain(s_dve, dve)
                n = CB * B8
                W = SLOT * HD0
                H4, D4 = HD0 // 2, NDG - 1

                def weigh(h, u, i, half):
                    if half == 0:
                        dve.wait_ge(s_qc, h + 1)
                    dve.wait_ge(s_y, 2 * h + half + 5)
                    q0 = half * n * 2 * HD0
                    for out_, in0, in1 in (
                            (ap(z[half], 0, [[W, n], [HD0, D4], [1, HD0]]),
                             ap(y[half], 0, [[64, n], [HD0, D4], [1, HD0]]),
                             ap(qc[u], q0, [[2 * HD0, n], [1, D4], [1, HD0]])),
                            (ap(z[half], D4 * HD0, [[W, n], [H4, 2], [1, H4]]),
                             ap(y[half], D4 * HD0, [[64, n], [0, 2], [1, H4]]),
                             ap(qc[u], q0 + H4, [[2 * HD0, n], [H4, 2], [1, H4]])),
                            (ap(z[half], NDG * HD0 + 1, [[W, n], [HD0 + 1, NDG - 2], [1, HD0]]),
                             ap(y[half], HD0, [[64, n], [HD0, NDG - 2], [1, HD0]]),
                             ap(qc[u], q0, [[2 * HD0, n], [0, NDG - 2], [1, HD0]]))):
                        dve.tensor_tensor(out_, in0, in1, ALU.mult).then_inc(s_tt, 1)

                def total(h, u, i, half):
                    dve.wait_ge(s_tt, 6 * h + 3 * half + 15)
                    chain.link(dve.tensor_reduce(
                        ap(QT, h * HSTEP + half * HALFSTEP, [[HD0, n], [1, HD0]]),
                        ap(z[half], 0, [[W, n], [1, HD0], [HD0, SLOT]]), op=ALU.add, axis=AX.X))

                def step(k):
                    if k():
                        weigh(*k(), 0)
                    if k(-1):
                        total(*k(-1), 1)
                    if k():
                        weigh(*k(), 1)
                        total(*k(), 0)
                    chain.restart()

                dve.wait_ge(s_z0, 2)
                pipelined(dve, H0, 0, step, 1)

        SR = sb(era1, "SR", [P, CB, B])
        WM = sb(era1, "WM", [P, B, CB, EH])
        era2 = whole.enter_context(ExitStack())
        WV = sb(era2, "WV", [P, HR, C])
        s_wv = sem("s_wv", era2)
        with ExitStack() as st:
            ot = [sb(st, f"ot{i}", [P, CB, T]) for i in range(2)]
            hs = [sb(st, f"hs{i}", [P, TH, C]) for i in range(2)]
            stats = sb(st, "stats3", [P, TH, 6])
            mv = [sb(st, f"mv3{i}", [P, TH, 2]) for i in range(2)]
            std = [sb(st, f"std3{i}", [P, TH]) for i in range(2)]
            work = [sb(st, f"work3_{i}", [P, TH]) for i in range(2)]
            rstd = [sb(st, f"rstd3_{i}", [P, TH]) for i in range(2)]
            shift = [sb(st, f"shift3_{i}", [P, TH]) for i in range(2)]
            px = [pb(st, f"px{i}", [P, TH, C]) for i in range(2)]
            ph = [pb(st, f"ph{i}", [P, CB, T]) for i in range(2)]
            s_ot, s_t1, s_t2, s_x1, s_mv, s_rs, s_std, s_hs, s_ev, s_dve, s_go = [sem(n + "_3", st) for n in (
                "s_ot", "s_t1", "s_t2", "s_x1", "s_mv", "s_rs", "s_std", "s_hs", "s_ev", "s_dve", "s_go")]
            block = st.enter_context(nc.Block())

            @block.sync
            def _(sp):
                for hq in range(HQ):
                    sp.dma_start(WV[hq * E0:(hq + 1) * E0], a["w_v"][:, hq * HR:(hq + 1) * HR, :]).then_inc(s_wv, 16)

            @block.gpsimd
            def _(pool):
                with pool.Fori(0, B // 2) as i:
                    for u in range(2):
                        b = 2 * i + u
                        pool.wait_ge(s_t1, b + 1)
                        pool.sem_inc(s_go, 1)
                        for k in range(CB):
                            pool.tensor_copy(ot[u][:, k, :].rearrange("p (h j) -> p h j", j=HD0), columns_of(b, k)).then_inc(s_ot, 1)

            @block.tensor
            def _(pe):
                pe.sem_inc(s_t1, 2)
                pe.sem_inc(s_hs, 2)
                pe.sem_inc(s_t2, 2)

                def back(b, u, i):
                    pe.wait_ge(s_ot, 4 * b + 4)
                    pe.wait_ge(s_x1, b + 1)
                    for th in range(TH):
                        for k in range(CB):
                            t = pe.transpose(px[u][:, th, k * P:(k + 1) * P], ot[u][:, k, th * P:(th + 1) * P], ident)
                    t.then_inc(s_t1, 1)

                def forth(b, u, i):
                    pe.wait_ge(s_hs, b + 3)
                    pe.wait_ge(s_ev, b + 1)
                    for k in range(CB):
                        for th in range(TH):
                            t = pe.transpose(ph[u][:, k, th * P:(th + 1) * P], hs[u][:, th, k * P:(k + 1) * P], ident)
                    t.then_inc(s_t2, 1)

                def step(k):
                    run_on(k(2), back)
                    run_on(k(), forth)

                pipelined(pe, B, 2, step)

            @block.vector
            def _(dve):
                chain = Chain(s_dve, dve)
                dve.sem_inc(s_x1, 2)

                def add(b, u, i):
                    rows, made = x_rows(b), {}

                    def one(th):
                        if th == 0:
                            dve.wait_ge(s_t1, b + 3)
                        made[th] = chain.inc(dve.scalar_tensor_tensor(rows[th], px[u][:, th, :], gates[:, 0:1],
                                                                      rows[th], ALU.mult, ALU.add))

                    def ready(th):
                        chain.wait(made[th])
                        if th == TH - 1:
                            dve.sem_inc(s_x1, 1)

                    return [lambda th=th: one(th) for th in range(TH)] + stats_steps(dve, chain, rows, stats, mv[u], ready)

                def root(b, u, i):
                    dve.wait_ge(s_std, b + 1)
                    dve.wait_ge(s_hs, b + 1)
                    return scale_steps(dve, chain, mv[u][:, :, 1], std[u], work[u], rstd[u], EPS, mv[u][:, :, 0], shift[u])

                def step(k):
                    weave(root(*k()) if k() else [], add(*k(1)) if k(1) else [])
                    if k() or k(1):
                        chain.restart()
                    if k(1):
                        dve.sem_inc(s_mv, 1)
                    if k():
                        dve.sem_inc(s_rs, 1)

                pipelined(dve, B, 2, step)

            @block.scalar
            def _(act):
                act.sem_inc(s_ev, 2)

                def norm(b, u, i):
                    act.wait_ge(s_rs, b + 1)
                    act.wait_ge(s_t2, b + 1)
                    for th, row in enumerate(x_rows(b)):
                        n = act.activation(hs[u][:, th, :], row, ACT.Identity, scale=rstd[u][:, th:th + 1], bias=shift[u][:, th:th + 1])
                    n.then_inc(s_hs, 1)

                def root(b, u, i):
                    act.wait_ge(s_mv, b + 1)
                    act.activation(std[u], mv[u][:, :, 1], ACT.Sqrt, bias=eps).then_inc(s_std, 1)

                def keep(b, u, i):
                    act.wait_ge(s_t2, b + 3)
                    for k in range(CB):
                        e = act.activation(columns_of(b, k), ph[u][:, k, :].rearrange("p (h j) -> p h j", j=HD0), ACT.Copy,
                                           accum_out=ap(SR, b + k * B, [[1, 1]]))
                    e.then_inc(s_ev, 1)

                def step(k):
                    run_on(k(1), root)
                    run_on(k(), norm)
                    run_on(k(-1), keep)

                pipelined(act, B, 2, step, 1)

        with ExitStack() as st:
            GR = HR // 4
            WOS = sb(st, "WOS", [HQ * B, 2, GR, C])
            sim = sb(st, "sim", [P, CB, E0])
            sim2 = sb(st, "sim2", [P, CB, E0])
            sr2 = sb(st, "sr2", [P, CB, B])
            ones = sb(st, "ones4", [P, B])
            later, over, same = (WM[0:B].rearrange("p b k h -> p (b k h)")[:, n * E0 * E0:(n + 1) * E0 * E0]
                                 .rearrange("p (e f) -> p e f", f=E0) for n in range(3))
            eg = sb(st, "eg", [B, E0])
            t = {n: sb(st, n + "_4", [B, E0]) for n in ("sig", "logits", "gated", "mask", "rank", "z", "e", "rm")}
            nn = sb(st, "nn", [B, E0 + 1])
            rn = sb(st, "rn", [B, E0 + 1])
            sq = sb(st, "sq", [B, E0 + 1])
            wk = sb(st, "wk", [B, E0 + 1])
            cnt = sb(st, "cnt", [B, 1])
            zmax = sb(st, "zmax", [B, 1])
            zsum = sb(st, "zsum", [B, 1])
            RB = sb(st, "RB", [P, HQ * B])
            p_aff = pb(st, "p_aff", [B, C])
            p_n = pb(st, "p_n", [B, C])
            p_e = pb(st, "p_e", [B, C])
            p_rm = pb(st, "p_rm", [P, C])
            p_w = [pb(st, f"p_w{i}", [P, 8, 64]) for i in range(4)]
            (s_in4, s_con, s_pe, s_act, s_dve, s_sr, s_rm, s_rb, s_wp, s_wd, s_wa, s_wp2) = [
                sem(n + "_4", st) for n in ("s_in", "s_con", "s_pe", "s_act", "s_dve", "s_sr", "s_rm", "s_rb",
                                            "s_wp", "s_wd", "s_wa", "s_wp2")]
            s_wst = [sem(f"s_wst4{i}", st) for i in range(2)]
            s_wo = [sem(f"s_wo4{i}", st) for i in range(2)]
            block = st.enter_context(nc.Block())

            @block.sync
            def _(sp):
                sp.dma_start(sim, a["sim"].rearrange("(k p) e -> p k e", p=P)).then_inc(s_in4, 16)
                sp.dma_start(eg, a["eg"].partition_broadcast(B)).then_inc(s_in4, 16)
                for n in range(2):
                    sp.wait_ge(s_wp, HR // 4 * (n + 1))
                    for hq in range(HQ):
                        sp.dma_start(WV[hq * E0:(hq + 1) * E0, 8 * n:8 * n + 8, :],
                                     a["w_o"][:, hq * HR + 8 * n:hq * HR + 8 * n + 8, :]).then_inc(s_wo[n], 16)
                for n in range(HR // GR):
                    sp.wait_ge(s_wa, (n + 1) * GR)
                    for hq in range(HQ):
                        sp.dma_start(WO[:, hq * HR + n * GR:hq * HR + (n + 1) * GR, :],
                                     WOS[hq * B:(hq + 1) * B, n % 2]).then_inc(s_wst[n % 2], 16)
                for n in range(2):
                    sp.wait_ge(s_wst[n], 16 * HQ * HR // GR // 2)

            @block.gpsimd
            def _(pool):
                pool.memset(ones, 1.0).then_inc(s_con, 1)
                pool.memset(RB, 0.0).then_inc(s_con, 1)
                pool.memset(later, 1.0).then_inc(s_con, 1)
                pool.wait_ge(s_con, 3)
                pool.affine_select(out=later, in_=later, compare_op=ALU.is_gt, fill=0.0, base=0,
                                   pattern=[[1, E0], [-1, E0]], channel_multiplier=0).then_inc(s_con, 1)

            @block.vector
            def _(dve):
                chain = Chain(s_dve, dve)
                dve.wait_ge(s_in4, 32)
                chain.inc(dve.tensor_scalar(SR, SR, 1.0 / T, None, ALU.mult))
                chain.link(dve.tensor_tensor(sim2, sim, sim, ALU.mult))
                dve.tensor_tensor(sr2, SR, SR, ALU.mult).then_inc(s_sr, 1)
                dve.wait_ge(s_pe, 1)
                chain.inc(dve.tensor_copy(nn[:, 0:E0], p_e[:, 0:E0]))
                chain.link(dve.tensor_copy(nn[:, E0:], p_n[:, 0:1]))
                dve.sem_inc(s_sr, 1)
                dve.wait_ge(s_act, 2)
                weave(scale_steps(dve, chain, nn, sq, wk, rn, 0.0))
                chain.wait()
                chain.link(dve.tensor_scalar(t["sig"], t["e"], 1.0, None, ALU.add))
                chain.link(dve.reciprocal(t["sig"], t["sig"]))
                chain.link(dve.scalar_tensor_tensor(t["logits"], p_aff[:, 0:E0], rn[:, E0:], rn[:, 0:E0], ALU.mult, ALU.mult))
                chain.link(dve.tensor_tensor(t["logits"], t["logits"], t["sig"], ALU.subtract))
                chain.inc(dve.tensor_scalar(t["gated"], t["logits"], 0.0, None, ALU.max))
                chain.link(dve.tensor_scalar(t["mask"], t["logits"], 0.0, None, ALU.is_gt))
                chain.link(dve.tensor_reduce(cnt, t["mask"], op=ALU.add, axis=AX.X))
                chain.link(dve.tensor_scalar(cnt, cnt, 0.0, None, ALU.is_equal))
                dve.wait_ge(s_con, 4)
                mine = ap(t["logits"], 0, [[1, E0], [0, E0]])
                other = ap(t["logits"], 0, [[0, E0], [1, E0]])
                chain.inc(dve.tensor_tensor(over, other, mine, ALU.is_gt))
                chain.link(dve.tensor_tensor(same, other, mine, ALU.is_equal))
                chain.link(dve.tensor_tensor(same, same, later, ALU.mult))
                chain.link(dve.tensor_tensor(over, over, same, ALU.add))
                chain.link(dve.tensor_reduce(t["rank"], over, op=ALU.add, axis=AX.X))
                chain.link(dve.tensor_scalar(t["rank"], t["rank"], float(FALLBACK), cnt, ALU.is_lt, ALU.mult))
                chain.link(dve.tensor_tensor(t["mask"], t["mask"], t["rank"], ALU.max))
                chain.inc(dve.tensor_tensor(t["gated"], t["gated"], t["mask"], ALU.mult))
                chain.link(dve.tensor_scalar(t["z"], t["mask"], FMAX, -FMAX, ALU.mult, ALU.add))
                chain.link(dve.tensor_tensor(t["z"], t["z"], t["gated"], ALU.add))
                chain.link(dve.tensor_reduce(zmax, t["z"], op=ALU.max, axis=AX.X, negate=True))
                dve.sem_inc(s_sr, 1)
                dve.wait_ge(s_act, 3)
                chain.link(dve.reciprocal(zsum, zsum))
                dve.scalar_tensor_tensor(t["rm"], t["e"], zsum, t["mask"], ALU.mult, ALU.mult).then_inc(s_rm, 1)
                dve.wait_ge(s_pe, 2)
                for g in range(HQ):
                    c = dve.tensor_copy(RB[g * E0:(g + 1) * E0, g * B:(g + 1) * B], p_rm[g * E0:(g + 1) * E0, 0:B])
                    chain.inc(c)
                chain.wait()
                dve.sem_inc(s_rb, 1)
                for r in range(HR):
                    dve.wait_ge(s_wp, r // 2 + 1)
                    dve.tensor_copy(ap(WM, r, [[EH, CB], [HR, HQ], [CB * EH, B]]),
                                    p_w[r // 2 % 2][:, 4 * (r % 2):4 * (r % 2) + 4, :].rearrange("p k (q b) -> p k q b", q=HQ)
                                    ).then_inc(s_wd, 1)

            @block.scalar
            def _(act):
                act.wait_ge(s_in4, 32)
                act.activation(t["e"], eg, ACT.Exp, scale=-1.0).then_inc(s_act, 1)
                act.wait_ge(s_sr, 2)
                act.activation(sq, nn, ACT.Sqrt).then_inc(s_act, 1)
                act.wait_ge(s_sr, 3)
                act.activation(t["e"], t["z"], ACT.Exp, bias=zmax, accum_out=zsum).then_inc(s_act, 1)
                for r in range(HR):
                    act.wait_ge(s_wp2, r + 1)
                    n = r // GR
                    if r % GR == 0 and n >= 2:
                        act.wait_ge(s_wst[n % 2], 16 * HQ * (n // 2))
                    act.activation(WOS[:, n % 2, r % GR, :], p_w[2 + r % 2][0:HQ * B].rearrange("p a b -> p (a b)"), ACT.Copy).then_inc(s_wa, 1)

            @block.tensor
            def _(pe):
                pe.wait_ge(s_sr, 1)
                pe.wait_ge(s_con, 2)
                pe.wait_ge(s_in4, 32)
                for k in range(CB):
                    pe.matmul(p_aff[:, 0:E0], SR[:, k, :], sim[:, k, :], start=(k == 0), stop=(k == CB - 1))
                for k in range(CB):
                    pe.matmul(p_n[:, 0:1], sr2[:, k, :], ones[:, 0:1], start=(k == 0), stop=(k == CB - 1))
                for k in range(CB):
                    m = pe.matmul(p_e[:, 0:E0], ones, sim2[:, k, :], start=(k == 0), stop=(k == CB - 1))
                m.then_inc(s_pe, 1)
                pe.wait_ge(s_rm, 1)
                for g in range(HQ):
                    m = pe.matmul(p_rm[g * E0:(g + 1) * E0, 0:B], t["rm"], ident[0:B, 0:B], start=True, stop=True)
                m.then_inc(s_pe, 1)
                pe.wait_ge(s_rb, 1)
                pe.wait_ge(s_wv, 16 * HQ)
                for r in range(HR):
                    if r >= 4 and r % 2 == 0:
                        pe.wait_ge(s_wd, r - 2)
                    for k in range(CB):
                        m = pe.matmul(p_w[r // 2 % 2][:, 4 * (r % 2) + k, :], WV[:, r, k * P:(k + 1) * P], RB, start=True, stop=True)
                    if r % 2:
                        m.then_inc(s_wp, 1)
                for r in range(HR):
                    pe.wait_ge(s_wo[r // 8], 16 * HQ)
                    if r >= 2:
                        pe.wait_ge(s_wa, r - 1)
                    pe.matmul(p_w[2 + r % 2][0:HQ * B].rearrange("p a b -> p (a b)"), RB, WV[:, r, :],
                              start=True, stop=True).then_inc(s_wp2, 1)

        era2.close()

        with ExitStack() as st:
            wc = [sb(st, f"wc{i}", [P, CB, EH]) for i in range(2)]
            wo = [sb(st, f"wo{i}", [EH, C]) for i in range(2)]
            cb = [sb(st, f"cb{i}", [EH, T]) for i in range(2)]
            q, qh, ql = ([sb(st, f"{n}{i}", [P, TH, C]) for i in range(2)] for n in ("q5_", "qh5_", "ql5_"))
            stats = sb(st, "stats5", [P, TH, 6])
            mv = [sb(st, f"mv5{i}", [P, TH, 2]) for i in range(2)]
            std = [sb(st, f"std5{i}", [P, TH]) for i in range(2)]
            work = [sb(st, f"work5_{i}", [P, TH]) for i in range(2)]
            rstd = [sb(st, f"rstd5_{i}", [P, TH]) for i in range(2)]
            shift = [sb(st, f"shift5_{i}", [P, TH]) for i in range(2)]
            pc = [pb(st, f"pc{i}", [EH, C]) for i in range(2)]
            py = [pb(st, f"py{i}", [P, TH, C]) for i in range(2)]
            s_w = [sem(f"s_w5{i}", st) for i in range(2)]
            s_st = [sem(f"s_st5{i}", st) for i in range(2)]
            s_wc, s_pc, s_cb, s_py, s_x2, s_mv, s_rs, s_std, s_q, s_qh, s_dve, s_ql = [sem(n + "_5", st) for n in (
                "s_wc", "s_pc", "s_cb", "s_py", "s_x2", "s_mv", "s_rs", "s_std", "s_q", "s_qh", "s_dve", "s_ql")]
            block = st.enter_context(nc.Block())

            @block.sync
            def _(sp):
                def store(b, u, i):
                    sp.wait_ge(s_ql, b + 3)
                    for part, to in ((qh, QH), (ql, QL)):
                        sp.dma_start(to[b].rearrange("(th p) c -> p th c", p=P), part[u]).then_inc(s_st[u], 16)

                pipelined(sp, B, 0, lambda k: run_on(k(), store))
                for u in range(2):
                    sp.wait_ge(s_st[u], 32 + 32 * B // 2)

            @block.gpsimd
            def _(pool):
                pool.sem_inc(s_st[0], 32)
                pool.sem_inc(s_st[1], 32)
                pool.sem_inc(s_ql, 2)

                def low(b, u, i):
                    pool.wait_ge(s_qh, b + 1)
                    pool.wait_ge(s_st[u], 32 * i + 32)
                    pool.tensor_tensor(ql[u].bitcast(F32R), q[u], qh[u], ALU.subtract).then_inc(s_ql, 1)

                pipelined(pool, B, 0, lambda k: run_on(k(), low))

            @block.tensor
            def _(pe):
                pe.sem_inc(s_pc, 2)
                pe.sem_inc(s_py, 2)

                def inner(b, u, i):
                    pe.wait_ge(s_wc, b + 1)
                    pe.wait_ge(s_cb, b + 1)
                    for k in range(CB):
                        m = pe.matmul(pc[u][:, 0:T].rearrange("p (h j) -> p h j", j=HD0), wc[u][:, k, :], columns_of(b, k),
                                      start=(k == 0), stop=(k == CB - 1))
                    m.then_inc(s_pc, 1)

                def outer(b, u, i):
                    pe.wait_ge(s_cb, b + 3)
                    pe.wait_ge(s_w[u], 16 * i + 16)
                    pe.wait_ge(s_x2, b + 1)
                    for th in range(TH):
                        m = pe.matmul(py[u][:, th, :], cb[u][:, th * P:(th + 1) * P], wo[u], start=True, stop=True)
                    m.then_inc(s_py, 1)

                def step(k):
                    run_on(k(1), outer)
                    run_on(k(2), inner)

                pipelined(pe, B, 2, step)

            @block.vector
            def _(dve):
                chain = Chain(s_dve, dve)
                dve.sem_inc(s_x2, 2)
                dve.sem_inc(s_q, 2)

                def copy(b, u, i):
                    dve.wait_ge(s_pc, b + 1)
                    dve.tensor_copy(wc[u].rearrange("p k h -> p (k h)"), ap(WM, b * (CB * EH), [[1, CB * EH]])).then_inc(s_wc, 1)

                def add(b, u, i):
                    rows, made = x_rows(b), {}

                    def one(th):
                        if th == 0:
                            dve.wait_ge(s_py, b + 3)
                        made[th] = chain.inc(dve.scalar_tensor_tensor(rows[th], py[u][:, th, :], gates[:, 2:3],
                                                                      rows[th], ALU.mult, ALU.add))

                    def ready(th):
                        chain.wait(made[th])
                        if th == TH - 1:
                            dve.sem_inc(s_x2, 1)

                    return [lambda th=th: one(th) for th in range(TH)] + stats_steps(dve, chain, rows, stats, mv[u], ready)

                def root(b, u, i):
                    dve.wait_ge(s_std, b + 1)
                    dve.wait_ge(s_q, b + 1)
                    return scale_steps(dve, chain, mv[u][:, :, 1], std[u], work[u], rstd[u], EPS, mv[u][:, :, 0], shift[u])

                def step(k):
                    run_on(k(3), copy)
                    weave(root(*k()) if k() else [], add(*k(1)) if k(1) else [])
                    if k() or k(1):
                        chain.restart()
                    if k(1):
                        dve.sem_inc(s_mv, 1)
                    if k():
                        dve.sem_inc(s_rs, 1)

                pipelined(dve, B, 4, step)

            @block.scalar
            def _(act):
                act.sem_inc(s_cb, 2)

                def load(b, u, i):
                    act.wait_ge(s_py, b + 1)
                    act.dma_start(wo[u], WO[b]).then_inc(s_w[u], 16)

                def hidden(b, u, i):
                    act.wait_ge(s_pc, b + 3)
                    act.wait_ge(s_py, b + 1)
                    act.activation(cb[u], pc[u][:, 0:T], ACT.Copy).then_inc(s_cb, 1)

                def norm(b, u, i):
                    act.wait_ge(s_rs, b + 1)
                    act.wait_ge(s_ql, b + 1)
                    for th, row in enumerate(x_rows(b)):
                        n = act.activation(q[u][:, th, :], row, ACT.Identity, scale=rstd[u][:, th:th + 1], bias=shift[u][:, th:th + 1])
                    n.then_inc(s_q, 1)

                def root(b, u, i):
                    act.wait_ge(s_mv, b + 1)
                    act.activation(std[u], mv[u][:, :, 1], ACT.Sqrt, bias=eps).then_inc(s_std, 1)

                def high(b, u, i):
                    act.wait_ge(s_q, b + 3)
                    act.wait_ge(s_st[u], 32 * i + 32)
                    act.activation(qh[u].bitcast(F32R), q[u], ACT.Copy).then_inc(s_qh, 1)

                def step(k):
                    run_on(k(2), load, hidden)
                    run_on(k(1), root)
                    run_on(k(), norm, high)

                pipelined(act, B, 2, step)

    X3 = out["out"][0:B * T].rearrange("(u p) c -> u p c", p=P)
    stats6 = sb(whole, "stats6", [P, UNITS, 6])
    with ExitStack() as st:
        qs = [sb(st, f"qs{i}", [P, NH, C]) for i in range(4)]
        ks = [sb(st, f"ks{i}", [P, NH, C]) for i in range(4)]
        vt = [sb(st, f"vt{i}", [P, CB, P]) for i in range(4)]
        pt = [sb(st, f"pt{i}", [P, NH, C]) for i in range(2)]
        lns = sb(st, "lns", [P, C])
        inv = sb(st, "inv", [P, C])
        att = sb(st, "att", [P, C])
        corr = sb(st, "corr", [P, C])
        minus_gate = sb(st, "minus_gate", [P, 1])
        mx = sb(st, "mx", [P, CB, NH])
        mh = sb(st, "mh", [NH, C])
        ml = sb(st, "ml", [NH, C])
        ones = sb(st, "ones6", [P, HD1])
        BANKS = 3
        pA = [pb(st, f"pA{i}", [P, C]) for i in range(BANKS)]
        pB = [pb(st, f"pB{i}", [P, C]) for i in range(2)]
        pV = [pb(st, f"pV{i}", [P, C]) for i in range(2)]
        pS = pb(st, "pS", [P, C])
        s_ld = [sem(f"s_ld{i}", st) for i in range(4)]
        s_v = [sem(f"s_v{i}", st) for i in range(4)]
        (s_rep, s_a, s_red, s_mt, s_mh, s_md, s_b, s_exp, s_av, s_x3, s_c, s_dve, s_act, s_dn, s_pool, s_go, s_st, s_rep0) = [
            sem(n + "_6", st) for n in ("s_rep", "s_a", "s_red", "s_mt", "s_mh", "s_md", "s_b", "s_exp",
                                        "s_av", "s_x3", "s_c", "s_dve", "s_act", "s_dn", "s_pool", "s_go", "s_st", "s_rep0")]
        block = st.enter_context(nc.Block())
        TRIP = 4
        NS = 3 * HD1
        TILES = NH * CB
        RING = TILES + 1
        units = lambda d: d.rearrange("b (g h d) c -> (b g) d h c", g=TH, h=NH)
        KHu, KLu, QHu, QLu = units(KH), units(KL), units(QH), units(QL)

        def unit_loop(eng, body):
            trips = UNITS // TRIP
            for u in range(TRIP):
                body(u, 0, u)
            with eng.Fori(1, trips - 1) as i:
                for u in range(TRIP):
                    body(i * TRIP + u, i, u)
            for u in range(TRIP):
                body(UNITS - TRIP + u, trips - 1, u)

        def bank(u, t):
            return pA[(u * RING + t) % BANKS]

        def last_use(j, u, t):
            return RING * j + t + 1 + (BANKS - (2 if u * RING + t < 2 else BANKS))

        def exists(j):
            return not isinstance(j, int) or 0 <= j < UNITS

        SPREAD = ((2, 3), (2, 2), (0, 1), (3, 3))
        EARLY = sum(sum(n) for n in SPREAD[2:])

        def ahead(j, u, s, part):
            n = 1 if s < 2 else 2
            t0 = sum(sum(m) for m in SPREAD[2 if s >= 2 else 0:s]) + sum(SPREAD[s][:part]) + (0 if s >= 2 else EARLY)
            return [(j + n, (u + n) % TRIP, t0 + w) for w in range(SPREAD[s][part])] if exists(j + n) else []

        @block.sync
        def _(sp):
            def load(j, u):
                for dst, src in ((ks[u][0:HD1], KHu[j]), (ks[u][HD1:2 * HD1], KLu[j]),
                                 (qs[u][0:HD1], QHu[j]), (qs[u][HD1:2 * HD1], QHu[j]), (qs[u][2 * HD1:NS], QLu[j])):
                    sp.dma_start(dst, src).then_inc(s_ld[u], 16)

            def load_values(j, u):
                sp.dma_start(vt[u], a["v_t"][j]).then_inc(s_v[u], 16)

            def store(j):
                sp.wait_ge(s_x3, j + 1)
                sp.dma_start(X3[j], ap(XN, j * ROW, [[1, C]])).then_inc(s_st, 16)

            def shift(j, u):
                sp.wait_ge(s_mh, j + 1)
                for row, part in enumerate((mh, ml)):
                    sp.dma_start(qs[u][NS + row:NS + row + 1],
                                 bass.AP(part.tensor, part.offset, [list(part.ap[0]), [C, 1], [1, C]])).then_inc(s_md, 16)

            def body(j, i, u):
                before, n = exists(j - 1), (u + TRIP - 1) % TRIP
                if before and exists(j + 3):
                    sp.wait_ge(s_b, TILES * j)
                if exists(j + 3):
                    load(j + 3, n)
                if exists(j + 1):
                    shift(j + 1, (u + 1) % TRIP)
                if before:
                    store(j - 1)
                if exists(j + 3):
                    load_values(j + 3, n)

            for u in range(3):
                load(u, u)
                load_values(u, u)
            shift(0, 0)
            unit_loop(sp, body)
            store(UNITS - 1)
            sp.wait_ge(s_st, 16 * UNITS)

        @block.gpsimd
        def _(pool):
            chain = Chain(s_pool, pool)
            chain.link(pool.memset(ones, 1.0))
            for u in range(4):
                chain.link(pool.memset(ks[u][NS:P], 1.0))
            chain.restart()
            pool.sem_inc(s_c, 1)

            def body(j, i, u):
                if isinstance(j, int) and j == 0:
                    return
                pool.wait_ge(s_ld[u], i * 80 + 80)
                pool.sem_inc(s_go, 1)
                chain.link(pool.tensor_copy(ks[u][2 * HD1:NS].bitcast(F32R), ks[u][0:HD1]))
                chain.restart()
                pool.sem_inc(s_rep, 1)

            unit_loop(pool, body)

        @block.tensor
        def _(pe):
            pe.sem_inc(s_red, BANKS)
            pe.sem_inc(s_exp, 2)
            pe.sem_inc(s_dn, 2)

            def first(tiles):
                for j, u, t in tiles:
                    if t == 0:
                        if exists(j - 1):
                            pe.wait_ge(s_rep, j)
                        else:
                            pe.wait_ge(s_rep0, 1)
                    pe.wait_ge(s_red, last_use(j, u, t))
                    h, m0 = t // CB, t % CB * P
                    pe.matmul(bank(u, t), qs[u][0:NS, h, m0:m0 + P].bitcast(F32R), ks[u][0:NS, h, :].bitcast(F32R),
                              start=True, stop=True).then_inc(s_a, 1)

            def maxima(j, u):
                rows = bank(u, TILES)
                pe.wait_ge(s_red, RING * j + TILES + BANKS)
                for k in range(CB):
                    t = pe.transpose(rows[0:NH, k * P:(k + 1) * P], mx[:, k, :], ident)
                t.then_inc(s_mt, 1)

            def second(j, u, s, part, tiles):
                if s == 0 and part == 0:
                    pe.wait_ge(s_md, 32 * j + 32)
                for h in (2 * part, 2 * part + 1):
                    pe.wait_ge(s_exp, TILES * j + NH * s + h + 1)
                    pe.matmul(pB[h % 2], ks[u][0:NS + 2, h, s * P:(s + 1) * P].bitcast(F32R), qs[u][0:NS + 2, h, :].bitcast(F32R),
                              start=True, stop=True).then_inc(s_b, 1)
                    first(tiles[h % 2:h % 2 + 1])

            def values(j, i, u, s):
                if s == 0:
                    pe.wait_ge(s_v[u], i * 16 + 16)
                    pe.wait_ge(s_dn, j + 1)
                pe.wait_ge(s_exp, TILES * j + NH * s + NH + 2)
                for h in range(NH):
                    pe.matmul(pV[u % 2][h * HD1:(h + 1) * HD1, :], vt[u][:, s, h * HD1:(h + 1) * HD1], pt[s % 2][:, h, :],
                              start=(s == 0), stop=(s == CB - 1))

            def sums(j, u, s):
                if s == 0:
                    pe.wait_ge(s_dn, j + 2)
                for h in range(NH):
                    m = pe.matmul(pS[h * HD1:(h + 1) * HD1, :], ones, pt[s % 2][:, h, :], start=(s == 0), stop=(s == CB - 1))
                m.then_inc(s_av, 1)

            def body(j, i, u):
                for s in range(CB):
                    last = (j, i, u, s - 1) if s else (j - 1, i if u else i - 1, (u + TRIP - 1) % TRIP, CB - 1)
                    for part in range(2):
                        tiles = ahead(j, u, s, part)
                        late = 0 if (s, part) == (2, 1) else 2
                        second(j, u, s, part, tiles[:late])
                        if exists(last[0]):
                            if part == 0:
                                values(*last)
                            else:
                                sums(last[0], *last[2:])
                        if (s, part) == (2, 0) and exists(j + 1):
                            maxima(j + 1, (u + 1) % TRIP)
                        first(tiles[late:])

            first([(0, 0, t) for t in range(TILES)])
            maxima(0, 0)
            first([(1, 1, t) for t in range(EARLY)])
            pe.wait_ge(s_c, 1)
            unit_loop(pe, body)
            values(UNITS - 1, UNITS // TRIP - 1, TRIP - 1, CB - 1)
            sums(UNITS - 1, TRIP - 1, CB - 1)

        @block.scalar
        def _(act):
            act.sem_inc(s_av, 2)
            act.preload_act_table_set("natural_log_exp_and_others")
            act.wait_ge(s_ld[0], 80)
            act.activation(ks[0][2 * HD1:NS].bitcast(F32R), ks[0][0:HD1], ACT.Copy).then_inc(s_rep0, 1)

            def inverse(j, u):
                act.wait_ge(s_av, 4 * j + 6)
                act.activation(lns, pS, ACT.Ln).then_inc(s_act, 1)
                act.wait_ge(s_act, 2 * j + 1)
                act.wait_ge(s_dn, j + 2)
                act.activation(inv, lns, ACT.Exp, scale=-1.0).then_inc(s_act, 1)

            def body(j, i, u):
                for s in range(CB):
                    act.wait_ge(s_av, 4 * j + s + 1)
                    for h in range(NH):
                        act.wait_ge(s_b, TILES * j + NH * s + h + 1)
                        act.activation(pt[s % 2][:, h, :], pB[h % 2], ACT.Exp, scale=SCALE1).then_inc(s_exp, 1)
                    if s == 0 and exists(j - 1):
                        inverse(j - 1, (u + TRIP - 1) % TRIP)

            unit_loop(act, body)
            inverse(UNITS - 1, TRIP - 1)

        @block.vector
        def _(dve):
            chain = Chain(s_dve, dve)

            def reduce(tiles):
                for j, u, t in tiles:
                    dve.wait_ge(s_a, TILES * j + t + 1)
                    dve.tensor_reduce(mx[:, t % CB, t // CB:t // CB + 1], bank(u, t), op=ALU.max, axis=AX.X).then_inc(s_red, 1)

            def shift(j, u):
                dve.wait_ge(s_mt, j + 1)
                if exists(j - 1):
                    dve.wait_ge(s_md, 32 * j)
                rows = bank(u, TILES)[0:NH, :]
                chain.link(dve.tensor_scalar(mh.bitcast(F32R), rows, -1.0, None, ALU.mult))
                chain.link(dve.scalar_tensor_tensor(ml.bitcast(F32R), rows, -1.0, mh, ALU.mult, ALU.subtract))
                chain.restart()
                dve.sem_inc(s_red, 1)
                dve.sem_inc(s_mh, 1)

            def release(j, u):
                dve.wait_ge(s_act, 2 * j + 2)
                chain.inc(dve.tensor_tensor(corr, pS, inv, ALU.mult))
                chain.link(dve.tensor_tensor(att, pV[u % 2], inv, ALU.mult))
                dve.sem_inc(s_dn, 1)

            def norm():
                chain.inc(dve.scalar_tensor_tensor(att, corr, 2.0, att, ALU.subtract, ALU.mult))

            def add(j, i, u):
                chain.wait()
                row = ap(XN, j * ROW, [[1, C]])
                chain.link(dve.scalar_tensor_tensor(row, att, minus_gate, row, ALU.mult, ALU.add))
                dve.sem_inc(s_x3, 1)
                chain.inc(dve.bn_stats(ap(stats6, j * 6, [[1, 6]]), row))
                chain.restart()

            def body(j, i, u):
                before = (j - 1, i if u else i - 1, (u + TRIP - 1) % TRIP)
                for s in range(CB):
                    if s == CB // 2 and exists(j + 1):
                        shift(j + 1, (u + 1) % TRIP)
                    reduce(ahead(j, u, s, 0))
                    if s == 1 and exists(j - 1):
                        release(before[0], before[2])
                    if s == 1 and exists(j - 1):
                        t = ahead(j, u, s, 1)
                        reduce(t[:1])
                        norm()
                        reduce(t[1:])
                        add(*before)
                    else:
                        reduce(ahead(j, u, s, 1))

            chain.link(dve.tensor_scalar(minus_gate, gates[:, 1:2], -1.0, None, ALU.mult))
            reduce([(0, 0, t) for t in range(TILES)])
            shift(0, 0)
            reduce([(1, 1, t) for t in range(EARLY)])
            unit_loop(dve, body)
            release(UNITS - 1, TRIP - 1)
            norm()
            add(UNITS - 1, UNITS // TRIP - 1, TRIP - 1)

    with ExitStack() as era3:
        WF = sb(era3, "WF", [P, E1, CB, C])
        WP = sb(era3, "WP", [P, E1, CB, C])
        TE = sb(era3, "TE", [P, TILES9])
        TEi = sb(era3, "TEi", [1, TILES9], I32)
        s_wf = sem("s_wf", era3)
        s_wp = sem("s_wp9", era3)
        with ExitStack() as era4:
            LG = sb(era4, "LG", [P, UNITS, E1])
            with ExitStack() as st:
                xT = [sb(st, f"xT{i}", [P, CB, P]) for i in range(2)]
                wr = sb(st, "wr", [P, CB, E1])
                xs = [sb(st, f"xn{i}", [P, C]) for i in range(2)]
                mv = sb(st, "mv7", [P, UNITS, 2])
                std = sb(st, "std7", [P, UNITS])
                work = sb(st, "work7", [P, UNITS])
                rstd = sb(st, "rstd7", [P, UNITS])
                zero = sb(st, "zero7", [P, C])
                pT = [pb(st, f"pT{i}", [P, CB, P]) for i in range(2)]
                pL = [pb(st, f"pL{i}", [E1, C]) for i in range(2)]
                pM = [pb(st, f"pM{i}", [P, C]) for i in range(2)]
                lt = [sb(st, f"lt{i}", [E1, P]) for i in range(2)]
                s_lt, s_m, s_go = [sem(n + "_7", st) for n in ("s_lt", "s_m", "s_go")]
                s_wr, s_mv, s_std, s_xn, s_t, s_ev, s_l, s_lg, s_dve, s_z, s_junk, s_cp = [sem(n + "_7", st) for n in (
                    "s_wr", "s_mv", "s_std", "s_xn", "s_t", "s_ev", "s_l", "s_lg", "s_dve", "s_z", "s_junk", "s_cp")]
                block = st.enter_context(nc.Block())

                @block.sync
                def _(sp):
                    sp.dma_start(wr, a["w_router"].rearrange("(k p) e -> p k e", p=P)).then_inc(s_wr, 16)
                    sp.wait_ge(s_z, 1)
                    sp.dma_start(out["out"][B * T:], zero).then_inc(s_junk, 16)
                    for e in range(E1):
                        sp.dma_start(WF[:, e], a["w_fc"][e].rearrange("(k p) d -> p k d", p=P)).then_inc(s_wf, 16)
                    for e in range(E1):
                        sp.dma_start(WP[:, e], a["w_proj"][e].rearrange("(k p) c -> p k c", p=P)).then_inc(s_wp, 16)
                    sp.wait_ge(s_junk, 16)

                @block.gpsimd
                def _(pool):
                    pool.memset(zero, 0.0).then_inc(s_z, 1)

                @block.vector
                def _(dve):
                    chain = Chain(s_dve, dve)
                    for j in range(UNITS):
                        chain.inc(dve.bn_aggr(mv[:, j, :], stats6[:, j, :]))
                    chain.restart()
                    dve.sem_inc(s_mv, 1)
                    dve.wait_ge(s_std, 1)
                    weave(scale_steps(dve, chain, mv[:, :, 1], std, work, rstd))
                    chain.restart()

                    def scale(j, u):
                        dve.wait_ge(s_t, j + 1)
                        dve.wait_ge(s_cp, j + 1)
                        dve.tensor_scalar(xs[u], ap(XN, j * ROW, [[1, C]]), ap(mv, 2 * j, [[1, 1]]), ap(rstd, j, [[1, 1]]),
                                          ALU.subtract, ALU.mult).then_inc(s_xn, 1)

                    def columns(j, u):
                        dve.wait_ge(s_t, j + 3)
                        dve.wait_ge(s_l, j + 1)
                        dve.tensor_copy(xT[u], pT[u]).then_inc(s_ev, 1)

                    scale(0, 0)
                    scale(1, 1)
                    with dve.Fori(0, UNITS // 2 - 1) as i:
                        for u in range(2):
                            columns(2 * i + u, u)
                            scale(2 * i + u + 2, u)
                    columns(UNITS - 2, 0)
                    columns(UNITS - 1, 1)

                @block.scalar
                def _(act):
                    act.wait_ge(s_mv, 1)
                    act.activation(std, mv[:, :, 1], ACT.Sqrt, bias=eps).then_inc(s_std, 1)

                    def keep(j, u):
                        act.wait_ge(s_xn, j + 1)
                        act.activation(ap(XN, j * ROW, [[1, C]]), xs[u], ACT.Copy).then_inc(s_cp, 1)

                    def copy(j, u, i):
                        act.wait_ge(s_l, j + 3)
                        act.wait_ge(s_m, j + 1)
                        act.activation(lt[u], pL[u][:, 0:P], ACT.Copy).then_inc(s_lt, 1)

                    def logits(j, u, i):
                        act.wait_ge(s_m, j + 3)
                        act.activation(ap(LG, j * E1, [[1, E1]]), pM[u][:, 0:E1], ACT.Copy).then_inc(s_lg, 1)

                    def step(k):
                        run_on(k(2), lambda j, u, i: keep(j, u))
                        run_on(k(1), copy)
                        run_on(k(), logits)

                    pipelined(act, UNITS, 2, step)

                @block.tensor
                def _(pe):
                    for s in (s_t, s_cp, s_l, s_ev, s_lg, s_lt, s_m):
                        pe.sem_inc(s, 2)
                    pe.wait_ge(s_wr, 16)

                    def turn(j, u):
                        pe.wait_ge(s_xn, j + 1)
                        pe.wait_ge(s_ev, j + 1)
                        for k in range(CB):
                            t = pe.transpose(pT[u][:, k, :], xs[u][:, k * P:(k + 1) * P], ident)
                        t.then_inc(s_t, 1)

                    def route(j, u, i):
                        pe.wait_ge(s_ev, j + 3)
                        pe.wait_ge(s_lt, j + 1)
                        for k in range(CB):
                            m = pe.matmul(pL[u][:, 0:P], wr[:, k, :], xT[u][:, k, :], start=(k == 0), stop=(k == CB - 1))
                        m.then_inc(s_l, 1)

                    def flip(j, u, i):
                        pe.wait_ge(s_lt, j + 3)
                        pe.wait_ge(s_lg, j + 1)
                        pe.sem_inc(s_go, 1)
                        pe.transpose(pM[u][:, 0:E1], lt[u], ident[0:E1, 0:E1]).then_inc(s_m, 1)

                    def step(k):
                        run_on(k(2), lambda j, u, i: turn(j, u))
                        run_on(k(1), route)
                        run_on(k(), flip)

                    pipelined(pe, UNITS, 2, step)

            with ExitStack() as st:
                A = [sb(st, f"A8{i}", [P, UNITS, E1]) for i in range(5)]
                over = sb(st, "over8", [P, UNITS // 2, E1, E1])
                V = {n: sb(st, n + "_8", [P, UNITS]) for n in ("v1", "v2", "s1", "s2", "e2")}
                later = sb(st, "later8", [P, E1, E1])
                before = sb(st, "before8", [P, P])
                ones = sb(st, "ones8", [P, P])
                number = sb(st, "number8", [P, TILES9 + UNITS])
                numi = sb(st, "numi8", [P, TILES9 + UNITS], I32)
                N8 = {n: sb(st, n + "_8", [P, E1]) for n in ("n", "nt", "end", "x")}
                Ni = sb(st, "Ni8", [P, E1], I32)
                slot = [sb(st, f"slot8{i}", [P, UNITS], U32) for i in range(2)]
                pP = pb(st, "pP", [P, UNITS, E1])
                pN = pb(st, "pN", [P, UNITS, E1])
                s_c, s_mask, s_pre, s_d, s_e, s_dve, s_slot, s_sc, s_v = [sem(n + "_8", st) for n in (
                    "s_c", "s_mask", "s_pre", "s_d", "s_e", "s_dve", "s_slot", "s_sc", "s_v")]
                block = st.enter_context(nc.Block())

                @block.gpsimd
                def _(pool):
                    chain = Chain(s_c, pool)
                    chain.link(pool.memset(later, 1.0))
                    chain.link(pool.memset(before, 1.0))
                    chain.link(pool.memset(ones, 1.0))
                    chain.link(pool.affine_select(out=later, in_=later, compare_op=ALU.is_gt, fill=0.0, base=0,
                                                  pattern=[[1, E1], [-1, E1]], channel_multiplier=0))
                    chain.link(pool.affine_select(out=before, in_=before, compare_op=ALU.is_gt, fill=0.0, base=0,
                                                  pattern=[[1, P]], channel_multiplier=-1))
                    chain.link(pool.iota(numi[:, 0:TILES9], [[1, TILES9]], base=0, channel_multiplier=0))
                    chain.link(pool.iota(numi[:, TILES9:], [[P, UNITS]], base=0, channel_multiplier=1))
                    pool.wait_ge(s_slot, 1)
                    for j in range(UNITS):
                        for w in range(2):
                            pool.indirect_dma_start(
                                out=XS, out_offset=bass.IndirectOffsetOnAxis(ap=slot[w][:, j:j + 1], axis=0),
                                in_=XN[:, j, :], in_offset=None).then_inc(s_sc, 16)
                    pool.wait_ge(s_sc, 16 * 2 * UNITS)

                @block.scalar
                def _(act):
                    act.wait_ge(s_d, 1)
                    act.activation(V["e2"], V["s1"], ACT.Exp).then_inc(s_e, 1)

                @block.tensor
                def _(pe):
                    pe.wait_ge(s_mask, 1)
                    pe.matmul(pP.rearrange("p u e -> p (u e)"), before, A[2].rearrange("p u e -> p (u e)"), start=True, stop=True)
                    pe.matmul(pN.rearrange("p u e -> p (u e)"), ones, A[2].rearrange("p u e -> p (u e)"), start=True, stop=True
                              ).then_inc(s_pre, 1)

                @block.vector
                def _(dve):
                    chain = Chain(s_dve, dve)
                    link, inc = chain.link, chain.inc
                    best, second, both, t0, t1 = A
                    n = UNITS // 2
                    for half in range(2):
                        mine = ap(LG, half * n * E1, [[E1, n], [1, E1], [0, E1]])
                        other = ap(LG, half * n * E1, [[E1, n], [0, E1], [1, E1]])
                        rank, equal = (t[:, half * n:(half + 1) * n] for t in (t0, t1))
                        link(dve.tensor_tensor(over, other, mine, ALU.is_gt))
                        link(dve.tensor_reduce(rank, over, op=ALU.add, axis=AX.X))
                        link(dve.tensor_tensor(over, other, mine, ALU.is_equal))
                        if half == 0:
                            dve.wait_ge(s_c, 7)
                        link(dve.tensor_tensor(over, over, ap(later, 0, [[0, n], [E1, E1], [1, E1]]), ALU.mult))
                        link(dve.tensor_reduce(equal, over, op=ALU.add, axis=AX.X))
                        link(dve.tensor_tensor(rank, rank, equal, ALU.add))
                    inc(dve.tensor_scalar(best, t0, 0.0, None, ALU.is_equal))
                    inc(dve.tensor_scalar(second, t0, 1.0, None, ALU.is_equal))
                    link(dve.tensor_scalar(both, t0, 1.0, None, ALU.is_le))
                    dve.sem_inc(s_mask, 1)

                    def pick(out_, which, of):
                        link(dve.tensor_tensor(t1, which, of, ALU.mult))
                        link(dve.tensor_reduce(out_, t1, op=ALU.add, axis=AX.X))

                    pick(V["v1"], best, LG)
                    pick(V["v2"], second, LG)
                    link(dve.tensor_tensor(V["s1"], V["v2"], V["v1"], ALU.subtract))
                    dve.sem_inc(s_d, 1)
                    inc(dve.tensor_copy(number, numi))
                    dve.wait_ge(s_e, 1)
                    link(dve.tensor_scalar(V["v1"], V["e2"], 1.0, None, ALU.add))
                    link(dve.reciprocal(V["v1"], V["v1"]))
                    link(dve.tensor_scalar(V["v1"], V["v1"], gates[:, 3:4], None, ALU.mult))
                    inc(dve.tensor_copy(XN[:, :, C + 1], V["v1"]))
                    inc(dve.tensor_tensor(XN[:, :, C + 2], V["v1"], V["e2"], ALU.mult))
                    inc(dve.tensor_copy(XN[:, :, C], number[:, TILES9:]))
                    pick(XN[:, :, C + 3], best, ap(number, 0, [[0, UNITS], [1, E1]]))
                    dve.wait_ge(s_pre, 1)
                    link(dve.tensor_copy(t0, pN))
                    cur, nxt, step = t0, t1, 1
                    while step < UNITS:
                        inc(dve.tensor_copy(nxt[:, 0:step], cur[:, 0:step]))
                        link(dve.tensor_tensor(nxt[:, step:], cur[:, step:], cur[:, 0:UNITS - step], ALU.add))
                        cur, nxt, step = nxt, cur, 2 * step
                    link(dve.tensor_copy(N8["n"], cur[:, UNITS - 1, :]))
                    link(dve.tensor_scalar(Ni, N8["n"], float(P - 1), None, ALU.add))
                    link(dve.tensor_scalar(Ni, Ni, 7, None, ALU.arith_shift_right))
                    link(dve.tensor_copy(N8["nt"], Ni))
                    a0, a1, step = N8["nt"], N8["end"], 1
                    link(dve.tensor_copy(N8["x"], N8["nt"]))
                    a0 = N8["x"]
                    while step < E1:
                        inc(dve.tensor_copy(a1[:, 0:step], a0[:, 0:step]))
                        link(dve.tensor_tensor(a1[:, step:], a0[:, step:], a0[:, 0:E1 - step], ALU.add))
                        a0, a1, step = a1, a0, 2 * step
                    cmp9 = over.rearrange("p u e f -> p (u e f)")[:, 0:TILES9 * E1].rearrange("p (t e) -> p t e", e=E1)
                    link(dve.tensor_tensor(cmp9, ap(number, 0, [[1, TILES9], [0, E1]]), ap(a0, 0, [[0, TILES9], [1, E1]]), ALU.is_ge))
                    link(dve.tensor_reduce(TE, cmp9, op=ALU.add, axis=AX.X))
                    link(dve.tensor_scalar(TE, TE, float(E1 - 1), None, ALU.min))
                    inc(dve.tensor_scalar(TEi, TE[0:1, :], float(CB * C), None, ALU.mult))
                    link(dve.tensor_tensor(a1, a0, N8["nt"], ALU.subtract))
                    link(dve.tensor_scalar(a1, a1, float(P), None, ALU.mult))
                    link(dve.tensor_tensor(nxt, cur, pN, ALU.subtract))
                    link(dve.tensor_tensor(nxt, nxt, pP, ALU.add))
                    link(dve.tensor_tensor(cur, nxt, ap(a1, 0, [[0, UNITS], [1, E1]]), ALU.add))
                    for w, which in enumerate((best, second)):
                        link(dve.tensor_tensor(nxt, which, cur, ALU.mult))
                        link(dve.tensor_reduce(V["s2"], nxt, op=ALU.add, axis=AX.X))
                        link(dve.tensor_copy(slot[w], V["s2"]))
                    dve.sem_inc(s_slot, 1)

        with ExitStack() as st:
            xs, xT, hr, hT, ys = ([ap(XN, (2 * n + i) * C, [[1, C]]) for i in range(2)] for n in range(5))
            xT, hT = ([t.rearrange("p (k n) -> p k n", n=P) for t in ring] for ring in (xT, hT))
            meta = sb(st, "meta", [P, TILES9, ROW - C])
            wt = [sb(st, f"wt{i}", [P, TILES9]) for i in range(3)]
            idx = [sb(st, f"idx{i}", [P, 1], U32) for i in range(2)]
            pT = [pb(st, f"p9T{i}", [P, CB, P]) for i in range(2)]
            pH = [pb(st, f"pH{i}", [P, C]) for i in range(2)]
            pG = [pb(st, f"pG{i}", [P, CB, P]) for i in range(2)]
            pY = [pb(st, f"pY{i}", [P, C]) for i in range(2)]
            s_x = [sem(f"s_x9{i}", st) for i in range(2)]
            s_t, s_xT, s_h, s_hr, s_g, s_hT, s_y, s_meta, s_ys, s_add, s_dve, s_go = [sem(n + "_9", st) for n in (
                "s_t", "s_xT", "s_h", "s_hr", "s_g", "s_hT", "s_y", "s_meta", "s_ys", "s_add", "s_dve", "s_go")]
            tiles = XS.rearrange("(t p) w -> t p w", p=P)
            block = st.enter_context(nc.Block())

            @block.sync
            def _(sp):
                for u in range(2):
                    sp.dma_start(xs[u], tiles[u][:, 0:C]).then_inc(s_x[u], 16)
                sp.dma_start(meta, XS.rearrange("(t p) w -> p t w", p=P)[:, :, C:]).then_inc(s_meta, 16)
                with sp.Fori(0, TILES9 // 2 - 1) as i:
                    for u in range(2):
                        j = 2 * i + u
                        sp.wait_ge(s_t, j + 1)
                        sp.dma_start(xs[u], tiles[j + 2][:, 0:C]).then_inc(s_x[u], 16)

            @block.tensor
            def _(pe):
                def columns(j, i, u):
                    pe.wait_ge(s_x[u], i * 16 + 16)
                    pe.wait_ge(s_xT, j + 1)
                    for k in range(CB):
                        t = pe.transpose(pT[u][:, k, :], xs[u][:, k * P:(k + 1) * P], ident)
                    t.then_inc(s_t, 1)

                def up(j, u):
                    e = pe.value_load(TEi[0:1, j:j + 1] if isinstance(j, int) else ap(TEi, j, [[1, 1]]), min_val=0, max_val=(E1 - 1) * CB * C)
                    pe.wait_ge(s_xT, j + 3)
                    pe.wait_ge(s_hr, j + 1)
                    for k in range(CB):
                        m = pe.matmul(pH[u], xT[u][:, k, :], ap(WF, e + k * C, [[1, C]]), start=(k == 0), stop=(k == CB - 1))
                    m.then_inc(s_h, 1)

                def turn(j, u):
                    pe.wait_ge(s_hr, j + 3)
                    pe.wait_ge(s_hT, j + 1)
                    for k in range(CB):
                        t = pe.transpose(pG[u][:, k, :], hr[u][:, k * P:(k + 1) * P], ident)
                    t.then_inc(s_g, 1)

                def down(j, u):
                    e = pe.value_load(TEi[0:1, j:j + 1] if isinstance(j, int) else ap(TEi, j, [[1, 1]]), min_val=0, max_val=(E1 - 1) * CB * C)
                    pe.wait_ge(s_hT, j + 3)
                    pe.wait_ge(s_ys, j + 1)
                    for k in range(CB):
                        m = pe.matmul(pY[u], hT[u][:, k, :], ap(WP, e + k * C, [[1, C]]), start=(k == 0), stop=(k == CB - 1))
                    m.then_inc(s_y, 1)

                for s in (s_xT, s_hr, s_hT, s_ys, s_g, s_y):
                    pe.sem_inc(s, 2)
                pe.sem_inc(s_h, 1)
                pe.wait_ge(s_wf, 16 * E1)
                columns(0, 0, 0)
                up(0, 0)
                columns(1, 0, 1)
                turn(0, 0)
                pe.wait_ge(s_wp, 16 * E1)
                with pe.Fori(0, TILES9 // 2 - 1) as i:
                    for u in range(2):
                        j = 2 * i + u
                        up(j + 1, 1 - u)
                        columns(j + 2, i + 1, u)
                        down(j, u)
                        turn(j + 1, 1 - u)
                up(TILES9 - 1, 1)
                down(TILES9 - 2, 0)
                turn(TILES9 - 1, 1)
                down(TILES9 - 1, 1)

            @block.scalar
            def _(act):
                with act.Fori(0, TILES9 // 2) as i:
                    for u in range(2):
                        j = 2 * i + u
                        act.wait_ge(s_h, j + 2)
                        act.wait_ge(s_g, j + 1)
                        act.activation(hr[u], pH[u], ACT.Relu).then_inc(s_hr, 1)
                        act.wait_ge(s_g, j + 3)
                        act.wait_ge(s_y, j + 1)
                        act.activation(hT[u], pG[u], ACT.Square).then_inc(s_hT, 1)

            @block.vector
            def _(dve):
                chain = Chain(s_dve, dve)

                def columns(j, u):
                    dve.wait_ge(s_t, j + 1)
                    dve.wait_ge(s_h, j)
                    dve.tensor_copy(xT[u], pT[u]).then_inc(s_xT, 1)

                def body(j, u):
                    if not isinstance(j, int) or j + 2 < TILES9:
                        columns(j + 2, u)
                    if not isinstance(j, int) or j > 1:
                        dve.wait_ge(s_add, 16 * (j - 1))
                    chain.inc(dve.tensor_copy(idx[u], ap(meta, j * (ROW - C), [[1, 1]])))
                    dve.wait_ge(s_y, j + 3)
                    chain.link(dve.tensor_scalar(ys[u], pY[u], ap(wt[0], j, [[1, 1]]), None, ALU.mult))
                    chain.restart()
                    dve.sem_inc(s_ys, 1)

                for u in range(2):
                    dve.wait_ge(s_t, u + 1)
                    dve.tensor_copy(xT[u], pT[u]).then_inc(s_xT, 1)
                dve.wait_ge(s_meta, 16)
                first, second, best = (meta[:, :, n] for n in (1, 2, 3))
                chain.link(dve.tensor_tensor(wt[0], best, TE, ALU.is_equal))
                chain.inc(dve.tensor_scalar(wt[1], wt[0], -1.0, 1.0, ALU.mult, ALU.add))
                chain.link(dve.tensor_tensor(wt[0], wt[0], first, ALU.mult))
                chain.link(dve.tensor_tensor(wt[2], wt[1], second, ALU.mult))
                chain.link(dve.tensor_tensor(wt[0], wt[0], wt[2], ALU.add))
                chain.restart()
                for u in range(2):
                    body(u, u)
                with dve.Fori(1, TILES9 // 2 - 1) as i:
                    for u in range(2):
                        body(2 * i + u, u)
                for u in range(2):
                    body(TILES9 - 2 + u, u)

            @block.gpsimd
            def _(pool):
                def add(j, u):
                    pool.wait_ge(s_ys, j + 3)
                    if not isinstance(j, int) or j > 0:
                        pool.wait_ge(s_add, 16 * j)
                    pool.sem_inc(s_go, 1)
                    pool.indirect_dma_start(out=out["out"], out_offset=bass.IndirectOffsetOnAxis(ap=idx[u], axis=0),
                                            in_=ys[u], in_offset=None, compute_op=ALU.add).then_inc(s_add, 16)

                for u in range(2):
                    add(u, u)
                with pool.Fori(1, TILES9 // 2) as i:
                    for u in range(2):
                        add(2 * i + u, u)
                pool.wait_ge(s_add, 16 * TILES9)


def kernel(x, ctx_2048, g_xattn, g_ffn, L0_xattn_ssm_kernel, L0_xattn_D, L0_ffn_sim_matrix, L0_ffn_gates,
           L0_ffn_w_q, L0_ffn_w_k, L0_ffn_w_v, L0_ffn_o_weights, L1_ffn_w_router, L1_ffn_w_fc, L1_ffn_w_proj):
    import numpy as _np
    import concourse.bacc as _bacc
    from concourse.bass_utils import run_bass_kernel_spmd as _run

    ctx = _np.asarray(ctx_2048)
    conv = ctx.reshape(HALF, B8, H0, HD0, CB, P)[..., ::-1].transpose(2, 5, 0, 4, 1, 3)
    conv = _np.concatenate([conv, conv[..., :CYC - HD0]], axis=-1)
    laid = {
        "x": x,
        "ctx": ctx,
        "ctx_conv": conv.reshape(H0, P, HALF * CB * B8 * CYC),
        "v_t": ctx.reshape(UNITS, P, CB, P).transpose(0, 3, 2, 1),
        "g": _np.concatenate([_np.asarray(g_xattn), _np.asarray(g_ffn)]),
        "kern_pad": _np.pad(_np.asarray(L0_xattn_ssm_kernel), ((0, 0), (P - 1, 0))),
        "skip": L0_xattn_D,
        "sim": L0_ffn_sim_matrix,
        "eg": L0_ffn_gates,
        "w_v": L0_ffn_w_v,
        "w_o": L0_ffn_o_weights,
        "w_router": L1_ffn_w_router,
        "w_fc": L1_ffn_w_fc,
        "w_proj": L1_ffn_w_proj,
    }
    laid = {name: _np.ascontiguousarray(array) for name, array in laid.items()}
    nc = _bacc.Bacc("TRN2", target_bir_lowering=False, num_devices=1)
    ins = {name: nc.dram_tensor("in_" + name, array.shape, F32, kind="ExternalInput").ap()
           for name, array in laid.items()}
    out = nc.dram_tensor("out_rows", [B * T + P, C], F32, kind="ExternalOutput").ap()
    build(nc, ins, {"out": out})
    r = _run(nc, [{"in_" + name: array for name, array in laid.items()}], core_ids=[0])
    return r.results[0]["out_rows"][:B * T].reshape(B, T, C)
```
